# Optimizing a Trainium2 kernel written in Bass

```python
import numpy as np
import jax
import jax.numpy as jnp

def _softmax(x, axis=-1):
    return jax.nn.softmax(x, axis=axis)

def _gelu(x):
    return jax.nn.gelu(x, approximate=True)

def _silu(x):
    return jax.nn.silu(x)

def _sigmoid(x):
    return jax.nn.sigmoid(x)

def _layernorm(x, axis=-1, eps=1e-05):
    m = jnp.mean(x, axis=axis, keepdims=True)
    v = jnp.var(x, axis=axis, keepdims=True)
    return (x - m) / jnp.sqrt(v + eps)

def _scatter_add(tgt, idx, src, axis=0):
    return tgt.at[idx].add(src)

def _segment_sum(src, seg, n):
    return jax.ops.segment_sum(src, seg, n)
kernel_name = 'mk_flamingo_gated_d1_seqx_r4_c2dca7'

def setup_inputs(seed: int=0):
    np.random.seed(seed)
    _w = jnp.asarray

    def _rec_inputs():
        import jax
        import jax.numpy as jnp
        _rk = jax.random.key(seed)
        x = 7.22e-05 + 1 * jax.random.normal(jax.random.fold_in(_rk, 1), (32, 256, 256), jnp.float32)
        _lenS = 256 - jax.random.randint(jax.random.fold_in(_rk, 7), (32,), 0, max(1, 256 // 4) + 1, jnp.int32)
        _lenS2 = 77 - jax.random.randint(jax.random.fold_in(_rk, 8), (32,), 0, max(1, 77 // 4) + 1, jnp.int32)
        _ctx_768P = jax.random.normal(jax.random.fold_in(_rk, 11), (32, 16, 192), jnp.float32)
        _ctx_768c = jax.random.dirichlet(jax.random.fold_in(_rk, 511), 0.3 * jnp.ones((16,), jnp.float32), (32, 77))
        _ctx_768t = jnp.einsum('bsk,bkd->bsd', _ctx_768c, _ctx_768P)
        _ctx_768t = _ctx_768t * jax.lax.rsqrt(jnp.mean(jnp.square(_ctx_768t)) + 1e-12) * 0.953939
        ctx_768 = 2.09791e-05 + 1.00001 * (_ctx_768t + 0.3 * jax.random.normal(jax.random.fold_in(_rk, 611), (32, 77, 192), jnp.float32))
        _g = jax.random.normal(jax.random.fold_in(_rk, 9001), (2, 1), jnp.float32)
        _g = jnp.sign(_g) * jnp.maximum(jnp.abs(_g), 1.0) + (_g == 0) * 1.0
        g_xattn = _g[0]
        g_ffn = _g[1]
        return (x, ctx_768, g_xattn, g_ffn)
    x, ctx_768, g_xattn, g_ffn = _rec_inputs()

    def _L0_xattn_setup():
        import jax, jax.numpy as jnp
        import numpy as np
        HEADS = 8
        DIM_HEAD = 64
        SCALE = DIM_HEAD ** (-0.5)
        key = jax.random.key(seed)
        ks = jax.random.split(key, 7)
        b, n, m = (4, 512, 256)
        qd, cd, inner = (256, 192, HEADS * DIM_HEAD)
        s = lambda fan_in: 1.0 / np.sqrt(fan_in)
        return {'x': jax.random.normal(ks[0], (b, n, qd), jnp.float32), 'context': jax.random.normal(ks[1], (b, m, cd), jnp.float32), 'Wq': jax.random.normal(ks[2], (qd, inner), jnp.float32) * s(qd), 'Wk': jax.random.normal(ks[3], (cd, inner), jnp.float32) * s(cd), 'Wv': jax.random.normal(ks[4], (cd, inner), jnp.float32) * s(cd), 'Wout': jax.random.normal(ks[5], (inner, qd), jnp.float32) * s(inner), 'bout': jax.random.normal(ks[6], (qd,), jnp.float32) * 0.01}
    _L0_xattn_all = _L0_xattn_setup()
    _L0_xattn_in = {k: v for k, v in _L0_xattn_all.items() if k in ('Wq', 'Wk', 'Wv', 'Wout', 'bout')}
    del _L0_xattn_all

    def _L0_ffn_setup():
        import jax, jax.numpy as jnp
        import numpy as np
        B, S, D = (2, 256, 256)
        H = 128
        E = 16
        K = 2
        HS = 2 * H
        ROUTE_SCALE = 1.0

        def _gated_mlp_act(y):
            u, g = jnp.split(y, 2, axis=-1)
            return u * jax.nn.silu(g)
        key = jax.random.key(seed)
        ks = jax.random.split(key, 6)
        s = 0.02
        return {'x': jax.random.normal(ks[0], (B, S, D), dtype=jnp.float32), 'Wg': jax.random.normal(ks[1], (E, D), dtype=jnp.float32) * s, 'W1': jax.random.normal(ks[2], (E, D, 2 * H), dtype=jnp.float32) * s, 'W2': jax.random.normal(ks[3], (E, H, D), dtype=jnp.float32) * s, 'Ws1': jax.random.normal(ks[4], (D, 2 * HS), dtype=jnp.float32) * s, 'Ws2': jax.random.normal(ks[5], (HS, D), dtype=jnp.float32) * s}
    _L0_ffn_all = _L0_ffn_setup()
    _L0_ffn_in = {k: v for k, v in _L0_ffn_all.items() if k in ('Wg', 'W1', 'W2', 'Ws1', 'Ws2')}
    del _L0_ffn_all
    return {'x': x, 'ctx_768': ctx_768, 'g_xattn': g_xattn, 'g_ffn': g_ffn, 'L0_xattn_Wq': _L0_xattn_in['Wq'], 'L0_xattn_Wk': _L0_xattn_in['Wk'], 'L0_xattn_Wv': _L0_xattn_in['Wv'], 'L0_xattn_Wout': _L0_xattn_in['Wout'], 'L0_xattn_bout': _L0_xattn_in['bout'], 'L0_ffn_Wg': _L0_ffn_in['Wg'], 'L0_ffn_W1': _L0_ffn_in['W1'], 'L0_ffn_W2': _L0_ffn_in['W2'], 'L0_ffn_Ws1': _L0_ffn_in['Ws1'], 'L0_ffn_Ws2': _L0_ffn_in['Ws2']}

def reference(x, ctx_768, g_xattn, g_ffn, L0_xattn_Wq, L0_xattn_Wk, L0_xattn_Wv, L0_xattn_Wout, L0_xattn_bout, L0_ffn_Wg, L0_ffn_W1, L0_ffn_W2, L0_ffn_Ws1, L0_ffn_Ws2):
    import jax
    import jax.numpy as jnp

    def _L0_xattn_ref(x, context, Wq, Wk, Wv, Wout, bout):
        import jax, jax.numpy as jnp
        import numpy as np
        HEADS = 8
        DIM_HEAD = 64
        SCALE = DIM_HEAD ** (-0.5)
        b, n, _ = x.shape
        m = context.shape[1]
        q = (x @ Wq).reshape(b, n, HEADS, DIM_HEAD)
        k = (context @ Wk).reshape(b, m, HEADS, DIM_HEAD)
        v = (context @ Wv).reshape(b, m, HEADS, DIM_HEAD)
        sim = jnp.einsum('bihd,bjhd->bhij', q, k) * SCALE
        attn = jax.nn.softmax(sim, axis=-1)
        out = jnp.einsum('bhij,bjhd->bihd', attn, v).reshape(b, n, HEADS * DIM_HEAD)
        return out @ Wout + bout

    def _L0_ffn_ref(x, Wg, W1, W2, Ws1, Ws2):
        import jax, jax.numpy as jnp
        import numpy as np
        B, S, D = (2, 256, 256)
        H = 128
        E = 16
        K = 2
        HS = 2 * H
        ROUTE_SCALE = 1.0

        def _gated_mlp_act(y):
            u, g = jnp.split(y, 2, axis=-1)
            return u * jax.nn.silu(g)
        x_shape = x.shape
        xf = x.reshape(-1, D)
        scores = jax.nn.softmax(xf @ Wg.T, axis=-1)
        wk, idx = jax.lax.top_k(scores, K)
        wk = wk * ROUTE_SCALE
        cw = jnp.sum(jax.nn.one_hot(idx, E, dtype=xf.dtype) * wk[..., None], axis=1)
        h = _gated_mlp_act(jnp.einsum('td,edh->teh', xf, W1))
        z = jnp.einsum('te,teh,ehd->td', cw, h, W2)
        ys = _gated_mlp_act(xf @ Ws1) @ Ws2
        return (z + ys).reshape(x_shape)
    x = x + jnp.tanh(g_xattn[0]) * _L0_xattn_ref(_layernorm(x, axis=-1), ctx_768, L0_xattn_Wq, L0_xattn_Wk, L0_xattn_Wv, L0_xattn_Wout, L0_xattn_bout)
    x = x + jnp.tanh(g_ffn[0]) * _L0_ffn_ref(_layernorm(x, axis=-1), L0_ffn_Wg, L0_ffn_W1, L0_ffn_W2, L0_ffn_Ws1, L0_ffn_Ws2)
    return x

_drawn_inputs = setup_inputs


def setup_inputs(seed=0):
    import zlib

    import numpy as np

    out = dict(_drawn_inputs(seed))
    spreads = {}
    factors = {'L0_xattn_bout': 7.78,
     'L0_ffn_Wg': 8.0,
     'L0_ffn_W1': 8.0,
     'L0_ffn_W2': 8.0,
     'L0_ffn_Ws1': 3.845,
     'L0_ffn_Ws2': 3.829}
    for name, (base, spread) in spreads.items():
        noise = np.random.default_rng([zlib.crc32(name.encode()), seed]).standard_normal(out[name].shape)
        drawn = base * np.exp(spread * noise) if base else spread * noise
        out[name] = jnp.asarray(drawn.astype(out[name].dtype))
    for name, factor in factors.items():
        out[name] = (out[name] * factor).astype(out[name].dtype)
    return out
```

```python
from contextlib import ExitStack

import concourse.bass as bass
from concourse import mybir

ALU = mybir.AluOpType
ACT = mybir.ActivationFunctionType
AX = mybir.AxisListType
F32 = mybir.dt.float32
F32R = mybir.dt.float32r
BF16 = mybir.dt.bfloat16
I32 = mybir.dt.int32

P = 128
B, N, D = 32, 256, 256
CK, CD = 77, 192
H, DH = 8, 64
INNER = H * DH
E, HID = 16, 128
HS = 2 * HID
T = B * N
TILES = T // P
DC = D // P
GB = 4
GROUPS = B // GB
GK = GB * CK
HK = H * CK
HALF = HK // 2
SLOT_TILES = 2 * TILES + E
LN_EPS = 1e-5
SCALE = DH ** -0.5
KP = 96


def wait(eng, sem, value):
    if not isinstance(value, int) or value > 0:
        eng.wait_ge(sem, value)


def f32(ap):
    return ap.bitcast(F32)


def products(nc, out, pairs, start=True, stop=True):
    last = None
    for n, (lh, ll, rh, rl) in enumerate(pairs):
        nc.tensor.matmul(out, lh, rh, start=start and n == 0, stop=False)
        nc.tensor.matmul(out, lh, rl, start=False, stop=False)
        last = nc.tensor.matmul(out, ll, rh, start=False, stop=stop and n == len(pairs) - 1)
    return last


class Common:
    pass


def allocator(nc, ctx):
    def sb(name, shape, dt=F32):
        return ctx.enter_context(nc.sbuf_tensor(name, shape, dt))

    def ps(name, shape):
        return ctx.enter_context(nc.psum_tensor(name, shape, F32))

    def sem(name):
        return ctx.enter_context(nc.semaphore(name))

    return sb, ps, sem


def rstd_steps(nc, v, stats, mean, rstd, var, chain, root_ready, root_done):
    step = [0]

    def link(ins):
        step[0] += 1
        ins.then_inc(chain, 1)
        v.wait_ge(chain, step[0])

    me, mo = stats[:, :, 1], stats[:, :, 4]
    link(nc.vector.tensor_tensor(mean, me, mo, ALU.add))
    link(nc.vector.tensor_scalar(mean, mean, 0.5, None, ALU.mult))
    link(nc.vector.tensor_tensor(rstd, mean, me, ALU.subtract))
    link(nc.vector.tensor_tensor(rstd, rstd, rstd, ALU.mult))
    link(nc.vector.scalar_tensor_tensor(rstd, stats[:, :, 2], 1.0 / D, rstd, ALU.mult, ALU.add))
    link(nc.vector.scalar_tensor_tensor(rstd, stats[:, :, 5], 1.0 / D, rstd, ALU.mult, ALU.add))
    link(nc.vector.tensor_scalar(rstd, rstd, LN_EPS, None, ALU.add))
    nc.vector.tensor_copy(var, rstd).then_inc(root_ready, 1)
    v.wait_ge(root_done, 1)
    link(nc.vector.reciprocal(rstd, rstd))
    link(nc.vector.tensor_tensor(var, var, rstd, ALU.mult))
    link(nc.vector.tensor_tensor(var, var, rstd, ALU.mult))
    link(nc.vector.tensor_scalar(var, var, -0.5, 1.5, ALU.mult, ALU.add))
    link(nc.vector.tensor_tensor(rstd, rstd, var, ALU.mult))


def prepare(nc, c):
    XB = 4
    with ExitStack() as ctx:
        sb, ps, sem = allocator(nc, ctx)
        wqT = sb("wqT", [DH, H, D])
        wkT = sb("wkT", [DH, H, CD])
        wqc = sb("wqc", [DH, H, D])
        qmean = sb("qmean", [DH, H])
        wv_raw = sb("wv_raw", [P, 2, INNER])
        wo_raw = sb("wo_raw", [P, 4, D])
        xs = [sb(f"xs{i}", [P, 4, D]) for i in range(XB)]
        stats = sb("stats1", [P, TILES, 6])
        mean1 = sb("mean1", [P, TILES])
        var1 = sb("var1", [P, TILES])
        gates = sb("gates", [P, 2])
        iota_row = sb("iota_row_f", [P, P])
        pk = [ps(f"pk{i}", [P, 512]) for i in range(4)]

        weights_in, wv_in, wo_in, gates_in = sem("weights_in"), sem("wv_in"), sem("wo_in"), sem("gates_in")
        x_in = [sem(f"pre_x_in{i}") for i in range(XB)]
        stats_done, chain1 = sem("stats_done"), sem("chain1")
        root_ready, root_done = sem("root_ready1"), sem("root_done1")
        qmean_done, qmean_scaled, centred = sem("qmean_done"), sem("qmean_scaled"), sem("centred")
        fold_done, fold_hi, fold_lo = sem("fold_done"), sem("fold_hi"), sem("fold_lo")
        tanh_done, bias_done, wo_scaled = sem("tanh_done"), sem("bias_done"), sem("wo_scaled")
        zeroed, w_hi, w_lo, ident_done = sem("zeroed"), sem("w_hi"), sem("w_lo"), sem("ident_done")

        with nc.Block() as block:

            @block.sync
            def _(sp):
                sp.dma_start(wqT[:, :, :], c.WqT.rearrange("(h i) d -> i h d", h=H)).then_inc(weights_in, 16)
                sp.dma_start(wkT[:, :, :], c.WkT.rearrange("(h i) d -> i h d", h=H)).then_inc(weights_in, 16)
                sp.dma_start(gates[:, 0:1], c.g_xattn.broadcast_to((P, 1))).then_inc(gates_in, 16)
                sp.dma_start(gates[:, 1:2], c.g_ffn.broadcast_to((P, 1))).then_inc(gates_in, 16)
                sp.dma_start(c.bias[:, :], c.bout.broadcast_to((P, D))).then_inc(gates_in, 16)
                for n in range(TILES // 4):
                    if n >= XB:
                        sp.wait_ge(stats_done, 4 * (n - XB + 1))
                    sp.dma_start(xs[n % XB][:, :, :],
                                 c.x[n * 512:(n + 1) * 512, :].rearrange("(i p) d -> p i d", p=P)
                                 ).then_inc(x_in[n % XB], 16)
                    if n == 3:
                        sp.dma_start(wv_raw[:, 0, :], c.Wv[0:P, :]).then_inc(wv_in, 16)
                        sp.dma_start(wv_raw[0:CD - P, 1, :], c.Wv[P:CD, :]).then_inc(wv_in, 16)
                        sp.dma_start(wo_raw[:, :, :], c.Wout.rearrange("(c p) n -> p c n", p=P)).then_inc(wo_in, 16)

            @block.gpsimd
            def _(pool):
                nc.gpsimd.memset(c.ident[:, :], 0.0).then_inc(ident_done, 1)
                pool.wait_ge(ident_done, 1)
                nc.gpsimd.affine_select(out=c.ident[:, :], in_=c.ident[:, :], compare_op=ALU.not_equal, fill=1.0,
                                        base=0, pattern=[[-1, P]], channel_multiplier=1).then_inc(ident_done, 1)
                for w in (c.wv_hi, c.wv_lo):
                    nc.gpsimd.memset(f32(w[:, 1, :]), 0.0).then_inc(zeroed, 1)
                for w in (c.wqk_hi, c.wqk_lo):
                    nc.gpsimd.memset(f32(w[:, 1, :, :]), 0.0).then_inc(zeroed, 1)
                pool.wait_ge(w_hi, 2)
                nc.gpsimd.tensor_tensor(c.wv_lo[:, 0, :], wv_raw[:, 0, :], f32(c.wv_hi[:, 0, :]),
                                        ALU.subtract).then_inc(w_lo, 1)
                nc.gpsimd.tensor_tensor(c.wv_lo[0:CD - P, 1, :], wv_raw[0:CD - P, 1, :],
                                        f32(c.wv_hi[0:CD - P, 1, :]), ALU.subtract).then_inc(w_lo, 1)
                pool.wait_ge(w_hi, 3)
                nc.gpsimd.tensor_tensor(c.wo_lo[:, :, :], wo_raw[:, :, :], f32(c.wo_hi[:, :, :]),
                                        ALU.subtract).then_inc(w_lo, 1)

            @block.tensor
            def _(pe):
                pe.wait_ge(centred, H)
                for h in range(H):
                    for cc, rows in ((0, P), (1, CD - P)):
                        n = 2 * h + cc
                        if n >= 4:
                            pe.wait_ge(fold_lo, n - 3)
                        nc.tensor.matmul(pk[n % 4][0:rows, 0:D], wkT[:, h, cc * P:cc * P + rows], wqc[:, h, :],
                                         start=True, stop=True).then_inc(fold_done, 1)

            @block.scalar
            def _(act):
                act.wait_ge(gates_in, 48)
                nc.scalar.activation(c.tanh_g[:, :], gates[:, :], ACT.Tanh).then_inc(tanh_done, 1)
                act.wait_ge(wv_in, 32)
                act.wait_ge(zeroed, 4)
                nc.scalar.activation(c.wv_hi[:, 0, :], wv_raw[:, 0, :], ACT.Copy).then_inc(w_hi, 1)
                nc.scalar.activation(c.wv_hi[0:CD - P, 1, :], wv_raw[0:CD - P, 1, :], ACT.Copy).then_inc(w_hi, 1)
                for n in range(2 * H):
                    h, cc = n // 2, n % 2
                    rows = CD - P if cc else P
                    act.wait_ge(fold_done, n + 1)
                    nc.scalar.activation(c.wqk_hi[0:rows, cc, h, :], pk[n % 4][0:rows, 0:D],
                                         ACT.Copy).then_inc(fold_hi, 1)
                act.wait_ge(wo_scaled, 1)
                nc.scalar.activation(c.wo_hi[:, :, :], wo_raw[:, :, :], ACT.Copy).then_inc(w_hi, 1)
                act.wait_ge(root_ready, 1)
                nc.scalar.activation(c.rstd1[:, :], c.rstd1[:, :], ACT.Sqrt).then_inc(root_done, 1)

            @block.vector
            def _(v):
                v.wait_ge(weights_in, 32)
                nc.vector.tensor_reduce(qmean[:, :], wqT[:, :, :], AX.X, ALU.add).then_inc(qmean_done, 1)
                v.wait_ge(qmean_done, 1)
                nc.vector.tensor_scalar(qmean[:, :], qmean[:, :], 1.0 / D, None, ALU.mult).then_inc(qmean_scaled, 1)
                v.wait_ge(qmean_scaled, 1)
                for h in range(H):
                    nc.vector.tensor_scalar(wqc[:, h, :], wqT[:, h, :], qmean[:, h:h + 1], SCALE,
                                            ALU.subtract, ALU.mult).then_inc(centred, 1)

                def tile_stats(t):
                    n = t // 4
                    v.wait_ge(x_in[n % XB], 16 * (n // XB + 1))
                    nc.vector.bn_stats(stats[:, t, :], xs[n % XB][:, t % 4, :]).then_inc(stats_done, 1)

                for n in range(2 * H):
                    h, cc = n // 2, n % 2
                    rows = CD - P if cc else P
                    tile_stats(n)
                    v.wait_ge(fold_hi, n + 1)
                    nc.vector.tensor_tensor(c.wqk_lo[0:rows, cc, h, :], pk[n % 4][0:rows, 0:D],
                                            f32(c.wqk_hi[0:rows, cc, h, :]), ALU.subtract).then_inc(fold_lo, 1)
                v.wait_ge(tanh_done, 1)
                v.wait_ge(gates_in, 48)
                nc.vector.tensor_scalar(c.bias[:, :], c.bias[:, :], c.tanh_g[:, 0:1], None,
                                        ALU.mult).then_inc(bias_done, 1)
                v.wait_ge(wo_in, 16)
                nc.vector.tensor_scalar(wo_raw[:, :, :], wo_raw[:, :, :], c.tanh_g[:, 0:1], None,
                                        ALU.mult).then_inc(wo_scaled, 1)
                for t in range(2 * H, TILES):
                    tile_stats(t)
                v.wait_ge(stats_done, TILES)
                rstd_steps(nc, v, stats, mean1[:, :], c.rstd1[:, :], var1[:, :], chain1, root_ready, root_done)


def attend(nc, c):
    with ExitStack() as ctx:
        sb, ps, sem = allocator(nc, ctx)
        ctx_raw = sb("ctx_raw", [P, 2, GK])
        ctxM = [sb(f"ctxM_{s}", [P, 2, GK], F32R) for s in ("hi", "lo")]
        ctxb_raw = [sb(f"ctxb_raw{i}", [P, 2, CK]) for i in range(2)]
        ctxb = [[sb(f"ctxb{i}_{s}", [P, 2, CK], F32R) for s in ("hi", "lo")] for i in range(2)]
        xT_raw = [sb(f"xT_raw{i}", [P, DC, N]) for i in range(2)]
        xT = [[sb(f"xT{i}_{s}", [P, DC, N], F32R) for s in ("hi", "lo")] for i in range(2)]
        x_tok = [sb(f"x_tok{i}", [P, 2, D]) for i in range(2)]
        x1_tok = [sb(f"x1_tok{i}", [P, 2, D]) for i in range(2)]
        M = [sb(f"M_{s}", [P, 2 * DC * GB * HK], F32R) for s in ("hi", "lo")]
        prob = [sb(f"prob{i}", [P, HK]) for i in range(2)]
        row_max = [sb(f"row_max{i}", [P, H]) for i in range(2)]
        row_sum = [sb(f"row_sum{i}", [P, H]) for i in range(2)]
        PT = [sb(f"PT_{s}", [KP, H, N], F32R) for s in ("hi", "lo")]
        V = [sb(f"V_{s}", [KP, 4, 4, DH], F32R) for s in ("hi", "lo")]
        OT = [sb(f"OT_{s}", [P, 4, N], F32R) for s in ("hi", "lo")]
        ps_proj = [ps(f"ps_proj{i}", [P, 512]) for i in range(2)]
        ps_s = ps("ps_s", [P, 2, 512])
        ps_pt = [ps(f"ps_pt{i}", [P, 512]) for i in range(2)]
        ps_o = [ps(f"ps_o{i}", [P, 512]) for i in range(2)]

        ctx_in = sem("ctx_in")
        ctxb_in = [sem(f"ctxb_in{i}") for i in range(2)]
        xT_in = [sem(f"xT_in{i}") for i in range(2)]
        x_in = [sem(f"x_in{i}") for i in range(2)]
        x1_out = [sem(f"x1_out{i}") for i in range(2)]
        pads_zero, ctx_hi, ctx_split = sem("pads_zero"), sem("ctx_hi"), sem("ctx_split")
        x_hi, x_split, cb_split = sem("x_hi"), sem("x_split"), sem("cb_split")
        normed, biased = sem("normed"), sem("biased")
        score_done, M_done, V_done, PT_done, OT_done, out_done = (
            sem("score_done"), sem("M_done"), sem("V_done"), sem("PT_done"), sem("OT_done"), sem("out_done"))
        M_hi, V_hi, PT_hi, OT_hi, exp_done = sem("M_hi"), sem("V_hi"), sem("PT_hi"), sem("OT_hi"), sem("exp_done")
        M_lo, V_lo, PT_lo, OT_lo = sem("M_lo"), sem("V_lo"), sem("PT_lo"), sem("OT_lo")
        max_done, sub_done, sum_done, inv_done = sem("max_done"), sem("sub_done"), sem("sum_done"), sem("inv_done")
        x1_done, x1_stats = sem("x1_done"), sem("x1_stats")

        MPAR = DC * GB * HK

        def M_at(s, parity, cc, q, lo, size):
            return M[s][:, bass.ds(parity * MPAR + (cc * GB + q) * HK + lo, size)]

        def groups(eng, body):
            body(0, True, False)
            with eng.Fori(1, GROUPS - 1) as g:
                body(g, False, False)
            body(GROUPS - 1, False, True)

        def tokens(b):
            return c.x[bass.ds(b * N, N), :].rearrange("(i p) d -> p i d", p=P)

        with nc.Block() as block:

            @block.sync
            def _(sp):
                def load_x_side(b, par):
                    sp.dma_start(xT_raw[par][:, :, :],
                                 c.xT[:, bass.ds(b * N, N)].rearrange("(c p) n -> p c n", p=P)).then_inc(xT_in[par], 16)
                    sp.dma_start(ctxb_raw[par][:, 0, :], c.ctxT[0:P, bass.ds(b * CK, CK)]).then_inc(ctxb_in[par], 16)
                    sp.dma_start(ctxb_raw[par][0:CD - P, 1, :],
                                 c.ctxT[P:CD, bass.ds(b * CK, CK)]).then_inc(ctxb_in[par], 16)

                def load_group(g):
                    sp.dma_start(ctx_raw[:, 0, :], c.ctxT[0:P, bass.ds(g * GK, GK)]).then_inc(ctx_in, 16)
                    sp.dma_start(ctx_raw[0:CD - P, 1, :], c.ctxT[P:CD, bass.ds(g * GK, GK)]).then_inc(ctx_in, 16)

                def store(b, par):
                    sp.wait_ge(x1_done, 2 * b + 2)
                    sp.dma_start(c.x1[bass.ds(b * N, N), :].rearrange("(i p) d -> p i d", p=P),
                                 x1_tok[par][:, :, :]).then_inc(x1_out[par], 16)

                load_group(0)
                load_x_side(0, 0)
                sp.dma_start(x_tok[0][:, :, :], tokens(0)).then_inc(x_in[0], 16)

                def body(g, first, last):
                    for q in range(GB):
                        b, par, nxt = GB * g + q, q % 2, (q + 1) % 2
                        if q == 0 and not last:
                            sp.wait_ge(ctx_split, g + 1)
                            load_group(g + 1)
                        if not (last and q == GB - 1):
                            wait(sp, x_split, b)
                            wait(sp, cb_split, b)
                            load_x_side(b + 1, nxt)
                            wait(sp, x1_done, 2 * b)
                            sp.dma_start(x_tok[nxt][:, :, :], tokens(b + 1)).then_inc(x_in[nxt], 16)
                        if not (first and q == 0):
                            store(b - 1, nxt)

                groups(sp, body)
                store(B - 1, (B - 1) % 2)
                for par in range(2):
                    sp.wait_ge(x1_out[par], 16 * (B // 2))

            @block.gpsimd
            def _(pool):
                for w in (*ctxM, *ctxb[0], *ctxb[1]):
                    nc.gpsimd.memset(f32(w[:, 1, :]), 0.0).then_inc(pads_zero, 1)
                for w in (*PT, *V):
                    nc.gpsimd.memset(f32(w[:]), 0.0).then_inc(pads_zero, 1)

                pool.wait_ge(pads_zero, 10)

                def split_group(g):
                    pool.wait_ge(ctx_hi, 2 * g + 2)
                    nc.gpsimd.tensor_tensor(ctxM[1][:, 0, :], ctx_raw[:, 0, :], f32(ctxM[0][:, 0, :]), ALU.subtract)
                    nc.gpsimd.tensor_tensor(ctxM[1][0:CD - P, 1, :], ctx_raw[0:CD - P, 1, :],
                                            f32(ctxM[0][0:CD - P, 1, :]), ALU.subtract).then_inc(ctx_split, 1)

                def split_batch(b, par):
                    pool.wait_ge(x_hi, 3 * b + 3)
                    nc.gpsimd.tensor_tensor(xT[par][1][:, :, :], xT_raw[par][:, :, :], f32(xT[par][0][:, :, :]),
                                            ALU.subtract).then_inc(x_split, 1)
                    nc.gpsimd.tensor_tensor(ctxb[par][1][:, 0, :], ctxb_raw[par][:, 0, :],
                                            f32(ctxb[par][0][:, 0, :]), ALU.subtract)
                    nc.gpsimd.tensor_tensor(ctxb[par][1][0:CD - P, 1, :], ctxb_raw[par][0:CD - P, 1, :],
                                            f32(ctxb[par][0][0:CD - P, 1, :]), ALU.subtract).then_inc(cb_split, 1)

                def norm(b, i):
                    pool.wait_ge(inv_done, 2 * b + i + 1)
                    pr = prob[i][:, :].rearrange("p (h k) -> p h k", h=H)
                    nc.gpsimd.tensor_tensor(pr, pr, row_sum[i][:, :].unsqueeze(2).broadcast_to((P, H, CK)),
                                            ALU.mult).then_inc(normed, 1)

                split_group(0)
                split_batch(0, 0)

                def body(g, first, last):
                    for q in range(GB):
                        b, par, nxt = GB * g + q, q % 2, (q + 1) % 2
                        if not (last and q == GB - 1):
                            split_batch(b + 1, nxt)
                        norm(b, 0)
                        if q == 0 and not last:
                            split_group(g + 1)
                        pool.wait_ge(x_in[par], 16 * (2 * g + q // 2 + 1))
                        xr = x_tok[par][:, :, :]
                        nc.gpsimd.tensor_tensor(xr, xr, c.bias[:, :].unsqueeze(1).broadcast_to((P, 2, D)),
                                                ALU.add).then_inc(biased, 1)
                        norm(b, 1)

                groups(pool, body)

            @block.tensor
            def _(pe):
                def make_M(n, g, cc, h):
                    wait(pe, M_lo, n - 1)
                    bank = ps_proj[cc]
                    products(nc, bank[:, 0:GK], [
                        (c.wqk_hi[:, k, h, cc * P:(cc + 1) * P], c.wqk_lo[:, k, h, cc * P:(cc + 1) * P],
                         ctxM[0][:, k, :], ctxM[1][:, k, :]) for k in range(2)]).then_inc(M_done, 1)

                def scores(b, g, q, i):
                    wait(pe, sub_done, 2 * b + i)
                    xs = xT[q % 2]
                    for half in range(2):
                        last = products(nc, ps_s[:, half, 0:HALF], [
                            (xs[0][:, k, i * P:(i + 1) * P], xs[1][:, k, i * P:(i + 1) * P],
                             M_at(0, g % 2, k, q, half * HALF, HALF), M_at(1, g % 2, k, q, half * HALF, HALF))
                            for k in range(DC)])
                    last.then_inc(score_done, 1)

                def attend_values(b):
                    pe.wait_ge(PT_lo, 4 * b + 4)
                    pe.wait_ge(V_lo, b + 1)
                    wait(pe, x1_done, 2 * b)
                    for k in range(2):
                        for pr in range(2):
                            pair = 2 * k + pr
                            last = products(nc, ps_o[k][:, pr * N:(pr + 1) * N], [
                                (V[0][:, pair, 2 * j:2 * j + 2, :].rearrange("p a e -> p (a e)"),
                                 V[1][:, pair, 2 * j:2 * j + 2, :].rearrange("p a e -> p (a e)"),
                                 PT[0][:, 2 * pair + j, :], PT[1][:, 2 * pair + j, :]) for j in range(2)])
                        last.then_inc(OT_done, 1)

                def project_out(b):
                    pe.wait_ge(OT_lo, 2 * b + 2)
                    for i in range(2):
                        products(nc, ps_o[i][:, 0:D], [
                            (OT[0][:, k, i * P:(i + 1) * P], OT[1][:, k, i * P:(i + 1) * P],
                             c.wo_hi[:, k, :], c.wo_lo[:, k, :]) for k in range(4)]).then_inc(out_done, 1)

                def make_V(b, par, m_units):
                    pe.wait_ge(cb_split, b + 1)
                    pe.wait_ge(M_lo, m_units)
                    products(nc, ps_proj[0][0:CK, :], [
                        (ctxb[par][0][:, k, :], ctxb[par][1][:, k, :], c.wv_hi[:, k, :], c.wv_lo[:, k, :])
                        for k in range(2)]).then_inc(V_done, 1)

                def transpose_probs(b, i):
                    pe.wait_ge(normed, 2 * b + i + 1)
                    for j in range(2):
                        wait(pe, PT_lo, 4 * b + 2 * i + j - 1)
                        for h in range(4):
                            lo = (4 * j + h) * CK
                            last = nc.tensor.transpose(ps_pt[j][0:CK, h * P:(h + 1) * P], prob[i][:, lo:lo + CK],
                                                       c.ident[:, :])
                        last.then_inc(PT_done, 1)

                pe.wait_ge(pads_zero, 10)
                pe.wait_ge(ctx_split, 1)
                for n in range(2 * H):
                    make_M(n, 0, n % 2, n // 2)

                def body(g, first, last):
                    for q in range(GB):
                        b = GB * g + q
                        pe.wait_ge(x_split, b + 1)
                        if q == 0:
                            pe.wait_ge(M_lo, 2 * H * (g + 1))
                        scores(b, g, q, 0)
                        if not (first and q == 0):
                            attend_values(b - 1)
                        scores(b, g, q, 1)
                        make_V(b, q % 2, 2 * H * GROUPS if last else 2 * H + 4 * b)
                        if not (first and q == 0):
                            project_out(b - 1)
                        if not last:
                            if q == 0:
                                pe.wait_ge(ctx_split, g + 2)
                            for k in range(4):
                                if k == 0:
                                    pe.wait_ge(V_lo, b + 1)
                                make_M(2 * H + 4 * b + k, g + 1, k % 2, 2 * q + k // 2)
                        transpose_probs(b, 0)
                        transpose_probs(b, 1)

                groups(pe, body)
                attend_values(B - 1)
                project_out(B - 1)

            def M_out(s, parity, cc, h):
                region = M[s][:, bass.ds(parity * MPAR + cc * GB * HK, GB * HK)]
                return region.rearrange("p (b x) -> p b x", b=GB)[:, :, h * CK:(h + 1) * CK]

            def M_bank(cc):
                return ps_proj[cc][:, 0:GK].rearrange("p (b k) -> p b k", b=GB)

            def V_out(s):
                return V[s][0:CK, :, 0:4:3, :]

            V_bank = ps_proj[0][0:CK, :].rearrange("p (a b e) -> p a b e", a=4, b=2)

            def PT_out(s, i, j):
                return PT[s][0:CK, 4 * j:4 * j + 4, i * P:(i + 1) * P]

            def PT_bank(j):
                return ps_pt[j][0:CK, :].rearrange("p (h n) -> p h n", h=4)

            def OT_out(s, k):
                return OT[s][:, 2 * k:2 * k + 2, :]

            def OT_bank(k):
                return ps_o[k][:, :].rearrange("p (c n) -> p c n", c=2)

            @block.scalar
            def _(act):
                def high(out, bank, done):
                    nc.scalar.activation(out, bank, ACT.Copy).then_inc(done, 1)

                def exponentials(b, i):
                    act.wait_ge(sub_done, 2 * b + i + 1)
                    nc.scalar.activation(prob[i][:, :], prob[i][:, :], ACT.Exp,
                                         scale=c.rstd1[:, bass.ds(2 * b + i, 1)]).then_inc(exp_done, 1)

                def high_OT(b):
                    for k in range(2):
                        act.wait_ge(OT_done, 2 * b + k + 1)
                        high(OT_out(0, k), OT_bank(k), OT_hi)

                def high_M(n, parity, cc, h):
                    act.wait_ge(M_done, n + 1)
                    high(M_out(0, parity, cc, h), M_bank(cc), M_hi)

                def high_group(g):
                    act.wait_ge(ctx_in, 32 * (g + 1))
                    wait(act, M_done, 2 * H * g)
                    high(ctxM[0][:, 0, :], ctx_raw[:, 0, :], ctx_hi)
                    high(ctxM[0][0:CD - P, 1, :], ctx_raw[0:CD - P, 1, :], ctx_hi)

                def high_batch(b, b_half, par):
                    act.wait_ge(xT_in[par], 16 * (b_half + 1))
                    wait(act, score_done, 2 * b - 2)
                    high(xT[par][0][:, :, :], xT_raw[par][:, :, :], x_hi)
                    act.wait_ge(ctxb_in[par], 32 * (b_half + 1))
                    wait(act, V_done, b - 1)
                    high(ctxb[par][0][:, 0, :], ctxb_raw[par][:, 0, :], x_hi)
                    high(ctxb[par][0][0:CD - P, 1, :], ctxb_raw[par][0:CD - P, 1, :], x_hi)

                act.wait_ge(pads_zero, 10)
                high_group(0)
                high_batch(0, 0, 0)
                for n in range(2 * H):
                    high_M(n, 0, n % 2, n // 2)

                def body(g, first, last):
                    for q in range(GB):
                        b = GB * g + q
                        if not (last and q == GB - 1):
                            high_batch(b + 1, 2 * g + (q + 1) // 2, (q + 1) % 2)
                        if q == 0 and not last:
                            high_group(g + 1)
                        exponentials(b, 0)
                        if not (first and q == 0):
                            high_OT(b - 1)
                        act.wait_ge(V_done, b + 1)
                        high(V_out(0), V_bank, V_hi)
                        exponentials(b, 1)
                        if not last:
                            for k in range(4):
                                high_M(2 * H + 4 * b + k, (g + 1) % 2, k % 2, 2 * q + k // 2)
                        for i in range(2):
                            for j in range(2):
                                act.wait_ge(PT_done, 4 * b + 2 * i + j + 1)
                                high(PT_out(0, i, j), PT_bank(j), PT_hi)

                groups(act, body)
                high_OT(B - 1)

            @block.vector
            def _(v):
                def low(lo, hi, bank, done):
                    nc.vector.tensor_tensor(lo, bank, f32(hi), ALU.subtract).then_inc(done, 1)

                S = ps_s[:, :, 0:HALF].rearrange("p a (h k) -> p a h k", h=4)

                def subtract_max(b, i):
                    v.wait_ge(score_done, 2 * b + i + 1)
                    mx = row_max[i][:, :].rearrange("p (a h) -> p a h", a=2)
                    nc.vector.tensor_reduce(mx, S, AX.X, ALU.max).then_inc(max_done, 1)
                    v.wait_ge(max_done, 2 * b + i + 1)
                    wait(v, PT_done, 4 * b + 2 * i - 2)
                    nc.vector.tensor_tensor(prob[i][:, :].rearrange("p (a h k) -> p a h k", a=2, h=4), S,
                                            mx.unsqueeze(3).broadcast_to((P, 2, 4, CK)),
                                            ALU.subtract).then_inc(sub_done, 1)

                def sums(b, i):
                    v.wait_ge(exp_done, 2 * b + i + 1)
                    wait(v, normed, 2 * b + i - 1)
                    nc.vector.tensor_reduce(row_sum[i][:, :], prob[i][:, :].rearrange("p (h k) -> p h k", h=H),
                                            AX.X, ALU.add).then_inc(sum_done, 1)
                    v.wait_ge(sum_done, 2 * b + i + 1)
                    nc.vector.reciprocal(row_sum[i][:, :], row_sum[i][:, :]).then_inc(inv_done, 1)

                def low_OT(b, k):
                    v.wait_ge(OT_hi, 2 * b + k + 1)
                    low(OT_out(1, k), OT_out(0, k), OT_bank(k), OT_lo)

                def residual(b, b_half, par):
                    v.wait_ge(biased, b + 1)
                    wait(v, x1_out[par], 16 * b_half)
                    for i in range(2):
                        v.wait_ge(out_done, 2 * b + i + 1)
                        nc.vector.tensor_tensor(x1_tok[par][:, i, :], ps_o[i][:, 0:D], x_tok[par][:, i, :],
                                                ALU.add).then_inc(x1_done, 1)
                        v.wait_ge(x1_done, 2 * b + i + 1)
                        nc.vector.bn_stats(c.stats2[:, bass.ds((2 * b + i) * 6, 6)],
                                           x1_tok[par][:, i, :]).then_inc(x1_stats, 1)

                def low_M(n, parity, cc, h):
                    v.wait_ge(M_hi, n + 1)
                    low(M_out(1, parity, cc, h), M_out(0, parity, cc, h), M_bank(cc), M_lo)

                v.wait_ge(pads_zero, 10)
                for n in range(2 * H):
                    low_M(n, 0, n % 2, n // 2)

                def body(g, first, last):
                    for q in range(GB):
                        b = GB * g + q
                        subtract_max(b, 0)
                        if not (first and q == 0):
                            low_OT(b - 1, 0)
                        sums(b, 0)
                        if not (first and q == 0):
                            low_OT(b - 1, 1)
                        subtract_max(b, 1)
                        v.wait_ge(V_hi, b + 1)
                        low(V_out(1), V_out(0), V_bank, V_lo)
                        sums(b, 1)
                        if not (first and q == 0):
                            residual(b - 1, 2 * g + (q - 1) // 2, (q + 1) % 2)
                        if not last:
                            for k in range(4):
                                low_M(2 * H + 4 * b + k, (g + 1) % 2, k % 2, 2 * q + k // 2)
                        for i in range(2):
                            for j in range(2):
                                v.wait_ge(PT_hi, 4 * b + 2 * i + j + 1)
                                low(PT_out(1, i, j), PT_out(0, i, j), PT_bank(j), PT_lo)

                groups(v, body)
                low_OT(B - 1, 0)
                low_OT(B - 1, 1)
                residual(B - 1, B // 2 - 1, (B - 1) % 2)
                v.wait_ge(x1_stats, 2 * B)



def gate(nc, c):
    STEPS = TILES // 4
    with ExitStack() as ctx:
        sb, ps, sem = allocator(nc, ctx)
        mean2, rstd2, shift2 = sb("mean2", [P, TILES]), sb("rstd2", [P, TILES]), sb("shift2", [P, TILES])
        var2 = sb("var2", [P, TILES])
        wg_raw = sb("wg_raw", [P, DC, E])
        wg = [sb(f"wg_{s}", [P, DC, P], F32R) for s in ("hi", "lo")]
        x1_in = [sb(f"x1_in{i}", [P, 4, D]) for i in range(2)]
        y = [sb(f"y{i}", [P, 4, D]) for i in range(2)]
        yT = [[sb(f"yT{i}_{s}", [P, DC, 512], F32R) for s in ("hi", "lo")] for i in range(2)]
        lgT = [sb(f"lgT{i}", [P, 512]) for i in range(2)]
        ps_y = [ps(f"ps_y{i}", [P, 512]) for i in range(4)]
        ps_lt = [ps(f"ps_lt{i}", [P, 512]) for i in range(2)]
        ps_l = [ps(f"ps_l{i}", [P, 4, P]) for i in range(2)]

        x1_loaded = [sem(f"x1_loaded{i}") for i in range(2)]
        y_stored = [sem(f"y_stored{i}") for i in range(2)]
        raw_in, wg_in = c.weights_raw_in, sem("wg_in")
        chain2, root_ready, root_done, ln_ready = sem("chain2"), sem("root_ready2"), sem("root_done2"), sem("ln_ready")
        wg_zero, wg_hi_done, wg_ready = sem("wg_zero"), sem("wg_hi_done"), sem("wg_ready")
        y_done, yT_done, yT_hi, yT_lo = sem("y_done"), sem("yT_done"), sem("yT_hi"), sem("yT_lo")
        lt_done, lt_copied, l_done, l_copied = sem("lt_done"), sem("lt_copied"), sem("l_done"), sem("l_copied")
        logits = c.logits[:, :].rearrange("p (t e) -> p t e", e=E)
        stats = c.stats2[:, :].rearrange("p (t s) -> p t s", s=6)

        def pipeline(eng, step):
            for G in range(4):
                step(G, G % 2, G // 2)
            with eng.Fori(2, STEPS // 2) as j:
                for r in range(2):
                    step(2 * j + r, r, j)
            for G in (STEPS, STEPS + 1):
                step(G, G % 2, STEPS // 2)

        def fills(G, lag):
            return not isinstance(G, int) or 0 <= G - lag < STEPS

        with nc.Block() as block:

            @block.sync
            def _(sp):
                sp.dma_start(wg_raw[:, :, :], c.WgT.rearrange("(k p) e -> p k e", p=P)).then_inc(wg_in, 16)

                def step(G, r, j):
                    if fills(G, 0):
                        wait(sp, y_done, 4 * (G - 1))
                        sp.dma_start(x1_in[r][:, :, :],
                                     c.x1[bass.ds(G * 512, 512), :].rearrange("(i p) d -> p i d", p=P)
                                     ).then_inc(x1_loaded[r], 16)
                    if fills(G, 1):
                        sp.wait_ge(y_done, 4 * G)
                        sp.dma_start(c.y[bass.ds((G - 1) * 512, 512), :].rearrange("(i p) d -> p i d", p=P),
                                     y[1 - r][:, :, :]).then_inc(y_stored[1 - r], 16)

                pipeline(sp, step)
                for r in range(2):
                    sp.wait_ge(y_stored[r], 16 * (STEPS // 2))

            @block.gpsimd
            def _(pool):
                for w in wg:
                    nc.gpsimd.memset(f32(w[:, :, :]), 0.0).then_inc(wg_zero, 1)
                for e in range(0, E, 4):
                    pool.dma_start(c.w1_raw[:, e:e + 4, :, :],
                                   c.W1[e:e + 4].rearrange("e (k p) h -> p e k h", p=P)).then_inc(raw_in, 16)
                    pool.dma_start(c.w2_raw[:, e:e + 4, :],
                                   c.W2[e:e + 4].rearrange("e p d -> p e d")).then_inc(raw_in, 16)
                pool.wait_ge(raw_in, 16 * 8)

            @block.tensor
            def _(pe):
                pe.wait_ge(wg_ready, 1)

                def step(G, r, j):
                    if fills(G, 0):
                        wait(pe, yT_lo, 2 * (G - 1))
                        pe.wait_ge(y_done, 4 * G + 4)
                        for k in range(DC):
                            for i in range(4):
                                last = nc.tensor.transpose(ps_y[2 * r + k][:, i * P:(i + 1) * P],
                                                           y[r][:, i, k * P:(k + 1) * P], c.ident[:, :])
                            last.then_inc(yT_done, 1)
                    if fills(G, 2):
                        pe.wait_ge(lt_copied, G - 1)
                        wait(pe, l_copied, G - 2)
                        for i in range(4):
                            last = nc.tensor.transpose(ps_l[r][:, i, :], lgT[r][:, i * P:(i + 1) * P],
                                                       c.ident[:, :])
                        last.then_inc(l_done, 1)
                    if fills(G, 1):
                        pe.wait_ge(yT_lo, 2 * G)
                        wait(pe, lt_copied, G - 2)
                        products(nc, ps_lt[1 - r][:, :], [
                            (wg[0][:, k, :], wg[1][:, k, :], yT[1 - r][0][:, k, :], yT[1 - r][1][:, k, :])
                            for k in range(DC)]).then_inc(lt_done, 1)

                pipeline(pe, step)

            @block.scalar
            def _(act):
                act.wait_ge(root_ready, 1)
                nc.scalar.activation(rstd2[:, :], rstd2[:, :], ACT.Sqrt).then_inc(root_done, 1)
                act.wait_ge(wg_zero, 2)
                act.wait_ge(wg_in, 16)
                nc.scalar.activation(wg[0][:, :, 0:E], wg_raw[:, :, :], ACT.Copy).then_inc(wg_hi_done, 1)

                def step(G, r, j):
                    if fills(G, 0):
                        wait(act, lt_done, G - 1)
                        for k in range(DC):
                            act.wait_ge(yT_done, 2 * G + k + 1)
                            nc.scalar.activation(yT[r][0][:, k, :], ps_y[2 * r + k][:, :], ACT.Copy).then_inc(yT_hi, 1)
                    if fills(G, 1):
                        act.wait_ge(lt_done, G)
                        wait(act, l_done, G - 2)
                        nc.scalar.activation(lgT[1 - r][:, :], ps_lt[1 - r][:, :], ACT.Copy).then_inc(lt_copied, 1)

                pipeline(act, step)

            @block.vector
            def _(v):
                rstd_steps(nc, v, stats, mean2[:, :], rstd2[:, :], var2[:, :], chain2, root_ready, root_done)
                nc.vector.scalar_tensor_tensor(shift2[:, :], mean2[:, :], -1.0, rstd2[:, :], ALU.mult,
                                               ALU.mult).then_inc(ln_ready, 1)
                v.wait_ge(wg_hi_done, 1)
                nc.vector.tensor_tensor(wg[1][:, :, 0:E], wg_raw[:, :, :], f32(wg[0][:, :, 0:E]),
                                        ALU.subtract).then_inc(wg_ready, 1)
                v.wait_ge(ln_ready, 1)

                def step(G, r, j):
                    if fills(G, 0):
                        v.wait_ge(x1_loaded[r], 16 * (j + 1))
                        wait(v, y_stored[r], 16 * j)
                        wait(v, yT_done, 2 * (G - 1))
                        for i in range(4):
                            nc.vector.tensor_scalar(y[r][:, i, :], x1_in[r][:, i, :],
                                                    rstd2[:, bass.ds(4 * G + i, 1)], shift2[:, bass.ds(4 * G + i, 1)],
                                                    ALU.mult, ALU.add).then_inc(y_done, 1)
                    if fills(G, 2):
                        v.wait_ge(l_done, G - 1)
                        nc.vector.tensor_copy(
                            c.logits[:, bass.ds((G - 2) * 4 * E, 4 * E)].rearrange("p (i e) -> p i e", e=E),
                            ps_l[r][:, :, 0:E]).then_inc(l_copied, 1)
                    if fills(G, 0):
                        for k in range(DC):
                            v.wait_ge(yT_hi, 2 * G + k + 1)
                            nc.vector.tensor_tensor(yT[r][1][:, k, :], ps_y[2 * r + k][:, :],
                                                    f32(yT[r][0][:, k, :]), ALU.subtract).then_inc(yT_lo, 1)

                pipeline(v, step)


def route(nc, c):
    W = TILES * E
    with ExitStack() as ctx:
        sb, ps, sem = allocator(nc, ctx)
        rank_row = sb("rank_row", [P, E])
        tile_no, part_no = sb("tile_no", [P, TILES]), sb("part_no", [P, 1])
        iota_lo, iota_hi = sb("iota_lo", [P, P], BF16), sb("iota_hi", [P, SLOT_TILES], BF16)
        before, ones = sb("before", [P, P], BF16), sb("ones", [P, P], BF16)
        top = [sb(f"top{k}", [P, TILES]) for k in range(2)]
        first = sb("first", [P, TILES])
        mask = [sb(f"mask{k}", [P, W]) for k in range(2)]
        work, rest = sb("work", [P, W]), sb("rest", [P, W])
        both = sb("both", [P, W], BF16)
        total = sb("total", [P, TILES])
        zeros = sb("zeros_t", [P, TILES])
        counts, upto, place = sb("counts", [P, W]), sb("upto", [P, W]), sb("place", [P, W])
        padded_i, padded = sb("padded_i", [P, E], I32), sb("padded", [P, E])
        ends, offsets = sb("ends", [P, E]), sb("offsets", [P, E])
        slot = [sb(f"slot{k}", [P, TILES]) for k in range(2)]
        part_i = sb("part_i", [P, TILES], I32)
        slot_hi = [sb(f"slot_hi{k}", [P, TILES]) for k in range(2)]
        slot_lo = [sb(f"slot_lo{k}", [P, TILES]) for k in range(2)]
        tile_iota, tile_ends = sb("tile_iota", [1, SLOT_TILES]), sb("tile_ends", [1, E])
        passed, tile_sum = sb("passed", [1, SLOT_TILES * E]), sb("tile_sum", [1, SLOT_TILES])
        OH = 8
        hot_lo = [sb(f"hot_lo{i}", [P, P], BF16) for i in range(OH)]
        hot_hi = [sb(f"hot_hi{i}", [P, 2 * SLOT_TILES], BF16) for i in range(OH)]
        inverse = sb("inverse", [P, 2 * SLOT_TILES])
        ps_before = [ps(f"ps_before{i}", [P, 512]) for i in range(2)]
        ps_count = [ps(f"ps_count{i}", [P, 512]) for i in range(2)]
        ps_inv = ps("ps_inv", [P, 512])

        consts, chain, gap_ready, exp_done = sem("consts"), sem("chain"), sem("gap_ready"), sem("exp_done_r")
        both_ready, counted = sem("both_ready"), sem("counted")
        hot_lo_ready, hot_hi_ready, hot_used = sem("hot_lo_ready"), sem("hot_hi_ready"), sem("hot_used")
        slots_ready, split_hi, split_lo = sem("slots_ready"), sem("w_split_hi"), sem("w_split_lo")

        def te(t):
            return t[:, :].rearrange("p (t e) -> p t e", e=E)

        def per_tile(t):
            return t[:, :].unsqueeze(2).broadcast_to((P, TILES, E))

        def per_expert(t):
            return t[:, :].unsqueeze(1).broadcast_to((P, TILES, E))

        halves = [slice(0, 512), slice(512, 1024)]

        with nc.Block() as block:

            @block.gpsimd
            def _(pool):
                steps = [0]

                def link(ins):
                    steps[0] += 1
                    ins.then_inc(consts, 1)
                    pool.wait_ge(consts, steps[0])

                g = nc.gpsimd
                exact = dict(allow_small_or_imprecise_dtypes=True)
                link(g.iota(rank_row[:, :], [[-1, E]], base=E, channel_multiplier=0, **exact))
                link(g.iota(tile_no[:, :], [[1, TILES]], base=0, channel_multiplier=0, **exact))
                link(g.iota(part_no[:, :], [[0, 1]], base=0, channel_multiplier=1, **exact))
                link(g.iota(iota_lo[:, :], [[1, P]], base=0, channel_multiplier=0, **exact))
                link(g.iota(iota_hi[:, :], [[1, SLOT_TILES]], base=0, channel_multiplier=0, **exact))
                link(g.iota(tile_iota[:, :], [[1, SLOT_TILES]], base=0, channel_multiplier=0, **exact))
                link(g.memset(ones[:, :], 1.0))
                link(g.memset(zeros[:, :], 0.0))
                link(g.affine_select(out=before[:, :], in_=ones[:, :], compare_op=ALU.is_gt, fill=0.0, base=0,
                                     pattern=[[1, P]], channel_multiplier=-1))
                for n in range(4):
                    e = slice(4 * n, 4 * n + 4)
                    pool.wait_ge(split_hi, 2 * n + 2)
                    g.tensor_tensor(c.w1_lo[:, e, :, :], c.w1_raw[:, e, :, :], f32(c.w1_hi[:, e, :, :]),
                                    ALU.subtract).then_inc(split_lo, 1)
                    g.tensor_tensor(c.w2_lo[:, e, :], c.w2_raw[:, e, :], f32(c.w2_hi[:, e, :]),
                                    ALU.subtract).then_inc(split_lo, 1)

            @block.scalar
            def _(act):
                def high(n):
                    e = slice(4 * n, 4 * n + 4)
                    nc.scalar.activation(c.w1_hi[:, e, :, :], c.w1_raw[:, e, :, :], ACT.Copy).then_inc(split_hi, 1)
                    nc.scalar.activation(c.w2_hi[:, e, :], c.w2_raw[:, e, :], ACT.Copy).then_inc(split_hi, 1)

                high(0)
                act.wait_ge(gap_ready, 1)
                nc.scalar.activation(te(work), te(work), ACT.Exp).then_inc(exp_done, 1)
                act.wait_ge(gap_ready, 2)
                nc.scalar.activation(c.weight[1][:, :], c.weight[1][:, :], ACT.Exp).then_inc(exp_done, 1)
                for n in range(1, 4):
                    high(n)

            @block.tensor
            def _(pe):
                pe.wait_ge(consts, 9)
                pe.wait_ge(both_ready, 1)
                for i in range(2):
                    nc.tensor.matmul(ps_before[i][:, :], before[:, :], both[:, halves[i]],
                                     start=True, stop=True).then_inc(counted, 1)
                    nc.tensor.matmul(ps_count[i][:, :], ones[:, :], both[:, halves[i]],
                                     start=True, stop=True).then_inc(counted, 1)

                def add_tile(j, u, first, last):
                    pe.wait_ge(hot_lo_ready, OH * j + u + 1)
                    pe.wait_ge(hot_hi_ready, 2 * (OH * j + u + 1))
                    nc.tensor.matmul(ps_inv[:, 0:2 * SLOT_TILES], hot_lo[u][:, :], hot_hi[u][:, :],
                                     start=first, stop=last, skip_group_check=True).then_inc(hot_used, 1)

                rounds = 2 * TILES // OH
                for u in range(OH):
                    add_tile(0, u, u == 0, False)
                with pe.Fori(1, rounds - 1) as j:
                    for u in range(OH):
                        add_tile(j, u, False, False)
                for u in range(OH):
                    add_tile(rounds - 1, u, False, u == OH - 1)

            @block.vector
            def _(v):
                steps = [0]

                def link(ins):
                    steps[0] += 1
                    ins.then_inc(chain, 1)
                    v.wait_ge(chain, steps[0])

                V = nc.vector
                v.wait_ge(consts, 9)
                logits, source = te(c.logits), te(c.logits)
                for k in range(2):
                    link(V.tensor_reduce(top[k][:, :], source, AX.X, ALU.max))
                    link(V.tensor_tensor(te(mask[k]), source, per_tile(top[k]), ALU.is_equal))
                    link(V.tensor_tensor(te(mask[k]), te(mask[k]), per_expert(rank_row), ALU.mult))
                    link(V.tensor_reduce(first[:, :], te(mask[k]), AX.X, ALU.max))
                    link(V.tensor_tensor(te(mask[k]), te(mask[k]), per_tile(first), ALU.is_equal))
                    if k == 0:
                        link(V.scalar_tensor_tensor(rest[:, :], mask[0][:, :], -3e38, c.logits[:, :],
                                                    ALU.mult, ALU.add))
                        source = te(rest)
                link(V.tensor_tensor(both[:, :], mask[0][:, :], mask[1][:, :], ALU.add))
                V.tensor_tensor(te(work), logits, per_tile(top[0]), ALU.subtract).then_inc(gap_ready, 1)
                V.tensor_tensor(c.weight[1][:, :], top[1][:, :], top[0][:, :], ALU.subtract).then_inc(gap_ready, 1)
                V.memset(total[:, :], 0.0).then_inc(both_ready, 1)

                v.wait_ge(counted, 4)
                for i in range(2):
                    link(V.tensor_copy(counts[:, halves[i]], ps_count[i][:, :]))
                for e in range(E):
                    ins = V.tensor_tensor_scan(te(upto)[:, :, e], te(counts)[:, :, e], zeros[:, :], 0.0,
                                               ALU.add, ALU.add)
                link(ins)
                link(V.tensor_scalar(padded_i[:, :], te(upto)[:, TILES - 1, :], float(P - 1), None, ALU.add))
                link(V.tensor_scalar(padded_i[:, :], padded_i[:, :], 7, 7, ALU.logical_shift_right,
                                     ALU.logical_shift_left))
                link(V.tensor_copy(padded[:, :], padded_i[:, :]))
                link(V.tensor_tensor_scan(ends[:, :], padded[:, :], zeros[:, 0:E], 0.0, ALU.add, ALU.add))
                link(V.tensor_tensor(offsets[:, :], ends[:, :], padded[:, :], ALU.subtract))
                link(V.tensor_tensor(te(place), te(upto), te(counts), ALU.subtract))
                link(V.tensor_tensor(te(place), te(place), per_expert(offsets), ALU.add))
                for i in range(2):
                    link(V.tensor_tensor(place[:, halves[i]], ps_before[i][:, :], place[:, halves[i]], ALU.add))
                for k in range(2):
                    link(V.tensor_tensor(mask[k][:, :], mask[k][:, :], place[:, :], ALU.mult))
                    link(V.tensor_reduce(slot[k][:, :], te(mask[k]), AX.X, ALU.add))
                    link(V.tensor_copy(c.slot_i[k][:, :], slot[k][:, :]))
                    link(V.tensor_scalar(part_i[:, :], c.slot_i[k][:, :], 7, None, ALU.logical_shift_right))
                    link(V.tensor_copy(slot_hi[k][:, :], part_i[:, :]))
                    link(V.scalar_tensor_tensor(slot_lo[k][:, :], slot_hi[k][:, :], -float(P), slot[k][:, :],
                                                ALU.mult, ALU.add))

                def one_hots(j, u):
                    t, k = bass.ds(j * (OH // 2) + u // 2, 1), u % 2
                    wait(v, hot_used, OH * (j - 1) + u + 1)
                    V.tensor_scalar(hot_lo[u][:, :], iota_lo[:, :], slot_lo[k][:, t], None,
                                    ALU.is_equal).then_inc(hot_lo_ready, 1)
                    V.tensor_scalar(hot_hi[u][:, 0:SLOT_TILES], iota_hi[:, :], slot_hi[k][:, t], tile_no[:, t],
                                    ALU.is_equal, ALU.mult).then_inc(hot_hi_ready, 1)
                    V.tensor_scalar(hot_hi[u][:, SLOT_TILES:], iota_hi[:, :], slot_hi[k][:, t], part_no[:, 0:1],
                                    ALU.is_equal, ALU.mult).then_inc(hot_hi_ready, 1)

                for u in range(OH):
                    one_hots(0, u)
                with v.Fori(1, 2 * TILES // OH) as j:
                    for u in range(OH):
                        one_hots(j, u)

                v.wait_ge(exp_done, 2)
                link(V.tensor_reduce(total[:, :], te(work), AX.X, ALU.add))
                link(V.reciprocal(total[:, :], total[:, :]))
                link(V.tensor_scalar(c.weight[0][:, :], total[:, :], c.tanh_g[:, 1:2], None, ALU.mult))
                link(V.tensor_tensor(c.weight[1][:, :], c.weight[1][:, :], c.weight[0][:, :], ALU.mult))

                link(V.tensor_scalar(tile_ends[:, :], ends[0:1, :], 1.0 / P, None, ALU.mult))
                link(V.tensor_tensor(passed[:, :].rearrange("p (t e) -> p t e", e=E),
                                     tile_iota[:, :].unsqueeze(2).broadcast_to((1, SLOT_TILES, E)),
                                     tile_ends[:, :].unsqueeze(1).broadcast_to((1, SLOT_TILES, E)), ALU.is_ge))
                link(V.tensor_reduce(tile_sum[:, :], passed[:, :].rearrange("p (t e) -> p t e", e=E), AX.X, ALU.add))
                link(V.tensor_scalar(c.tile_expert[:, :], tile_sum[:, :], float(E - 1), None, ALU.min))

                v.wait_ge(hot_used, 2 * TILES)
                link(V.tensor_copy(inverse[:, :], ps_inv[:, 0:2 * SLOT_TILES]))
                link(V.scalar_tensor_tensor(c.slot_token[:, :], inverse[:, 0:SLOT_TILES], float(P),
                                            inverse[:, SLOT_TILES:], ALU.mult, ALU.add))
                v.wait_ge(split_lo, 8)


def experts(nc, c):
    U = 8
    ROUNDS = SLOT_TILES // U
    with ExitStack() as ctx:
        sb, ps, sem = allocator(nc, ctx)
        index = [sb(f"index{i}", [P, U // 2], I32) for i in range(2)]
        rows = [sb(f"rows{i}", [P, D]) for i in range(U)]
        yT = [[sb(f"eyT{i}_{s}", [P, DC, P], F32R) for s in ("hi", "lo")] for i in range(2)]
        silu = [sb(f"silu{i}", [P, HID]) for i in range(2)]
        a = [sb(f"a{i}", [P, HID]) for i in range(2)]
        aT = [[sb(f"aT{i}_{s}", [P, P], F32R) for s in ("hi", "lo")] for i in range(2)]
        z = [sb(f"z{i}", [P, D]) for i in range(4)]
        ps_y = [ps(f"ps_ey{i}", [P, DC, P]) for i in range(2)]
        ps_h = [ps(f"ps_h{i}", [P, 2 * HID]) for i in range(2)]
        ps_a = [ps(f"ps_a{i}", [P, P]) for i in range(2)]
        ps_z = [ps(f"ps_z{i}", [P, D]) for i in range(2)]
        index_ready, go = sem("index_ready"), sem("gather_go")
        gathered = [sem(f"gathered{i}") for i in range(U)]
        z_stored = [sem(f"z_stored{i}") for i in range(4)]
        yT_done, yT_hi, yT_lo = sem("eyT_done"), sem("eyT_hi"), sem("eyT_lo")
        h_done, silu_done, a_done = sem("h_done"), sem("silu_done"), sem("a_done")
        aT_done, aT_hi, aT_lo, z_done, z_copied = (
            sem("aT_done"), sem("aT_hi"), sem("aT_lo"), sem("z_done"), sem("z_copied"))

        def tiles(eng, step):
            for u in range(U):
                step(u, u, 0)
            with eng.Fori(1, ROUNDS) as j:
                for u in range(U):
                    step(U * j + u, u, j)

        with nc.Block() as block:

            @block.gpsimd
            def _(pool):
                def step(t, u, j):
                    if u % 4 == 0:
                        pool.wait_ge(index_ready, 2 * j + u // 4 + 1)
                    wait(pool, yT_done, t - U + 1)
                    pool.sem_inc(go, 1)
                    pool.indirect_dma_start(rows[u][:, :], None, c.y,
                                            bass.IndirectOffsetOnAxis(index[u // 4][:, u % 4:u % 4 + 1], 0)
                                            ).then_inc(gathered[u], 16)

                tiles(pool, step)

            @block.sync
            def _(sp):
                def step(t, u, j):
                    sp.wait_ge(z_copied, t + 1)
                    sp.dma_start(c.z[bass.ds(t * P, P), :], z[u % 4][:, :]).then_inc(z_stored[u % 4], 16)

                tiles(sp, step)
                for i in range(4):
                    sp.wait_ge(z_stored[i], 16 * (SLOT_TILES // 4))

            @block.tensor
            def _(pe):
                def transpose_rows(t, u, j):
                    pe.wait_ge(gathered[u], 16 * (j + 1))
                    wait(pe, yT_lo, t - 1)
                    for k in range(DC):
                        last = nc.tensor.transpose(ps_y[u % 2][:, k, :], rows[u][:, k * P:(k + 1) * P], c.ident[:, :])
                    last.then_inc(yT_done, 1)

                def hidden(t, u, w1_at):
                    pe.wait_ge(yT_lo, t + 1)
                    wait(pe, a_done, t - 1)
                    y_ = yT[u % 2]
                    products(nc, ps_h[u % 2][:, :], [
                        (y_[0][:, k, :], y_[1][:, k, :],
                         c.w1_hi_flat[:, bass.ds(w1_at + k * D, D)], c.w1_lo_flat[:, bass.ds(w1_at + k * D, D)])
                        for k in range(DC)]).then_inc(h_done, 1)

                def transpose_a(t, u):
                    pe.wait_ge(a_done, t + 1)
                    wait(pe, aT_lo, t - 1)
                    nc.tensor.transpose(ps_a[u % 2][:, :], a[u % 2][:, :], c.ident[:, :]).then_inc(aT_done, 1)

                def down(t, u, w2_at):
                    pe.wait_ge(aT_lo, t + 1)
                    wait(pe, z_copied, t - 1)
                    a_ = aT[u % 2]
                    products(nc, ps_z[u % 2][:, :], [
                        (a_[0][:, :], a_[1][:, :], c.w2_hi_flat[:, bass.ds(w2_at, D)],
                         c.w2_lo_flat[:, bass.ds(w2_at, D)])]).then_inc(z_done, 1)

                def expert_of(t):
                    return pe.value_load(c.tile_expert[0:1, bass.ds(t, 1)], min_val=0, max_val=E - 1)

                def step(t, u, j):
                    e = expert_of(t)
                    if isinstance(t, int) and t == 0:
                        transpose_rows(0, 0, 0)
                    hidden(t, u, e * (DC * D))
                    if u < U - 1:
                        transpose_rows(t + 1, u + 1, j)
                    elif isinstance(t, int):
                        transpose_rows(t + 1, 0, j + 1)
                    else:
                        transpose_rows(t + 1, 0, j + 1)
                    transpose_a(t, u)
                    down(t, u, e * D)

                for u in range(U):
                    step(u, u, 0)
                with pe.Fori(1, ROUNDS - 1) as j:
                    for u in range(U):
                        step(U * j + u, u, j)
                for u in range(U):
                    t = U * (ROUNDS - 1) + u
                    e = expert_of(t)
                    hidden(t, u, e * (DC * D))
                    if u < U - 1:
                        transpose_rows(t + 1, u + 1, ROUNDS - 1)
                    transpose_a(t, u)
                    down(t, u, e * D)

            @block.scalar
            def _(act):
                def step(t, u, j):
                    p = u % 2
                    act.wait_ge(yT_done, t + 1)
                    wait(act, h_done, t - 1)
                    nc.scalar.activation(yT[p][0][:, :, :], ps_y[p][:, :, :], ACT.Copy).then_inc(yT_hi, 1)
                    act.wait_ge(h_done, t + 1)
                    wait(act, a_done, t - 1)
                    nc.scalar.activation(silu[p][:, :], ps_h[p][:, HID:], ACT.Silu).then_inc(silu_done, 1)
                    act.wait_ge(aT_done, t + 1)
                    wait(act, z_done, t - 1)
                    nc.scalar.activation(aT[p][0][:, :], ps_a[p][:, :], ACT.Copy).then_inc(aT_hi, 1)

                tiles(act, step)

            @block.vector
            def _(v):
                def indices(first_tile, half):
                    nc.vector.tensor_copy(index[half][:, :],
                                          c.slot_token[:, bass.ds(first_tile, 4)]).then_inc(index_ready, 1)

                indices(0, 0)
                indices(4, 1)

                def step(t, u, j, last_round):
                    p = u % 2
                    v.wait_ge(yT_hi, t + 1)
                    nc.vector.tensor_tensor(yT[p][1][:, :, :], ps_y[p][:, :, :], f32(yT[p][0][:, :, :]),
                                            ALU.subtract).then_inc(yT_lo, 1)
                    v.wait_ge(silu_done, t + 1)
                    wait(v, aT_done, t - 1)
                    nc.vector.tensor_tensor(a[p][:, :], ps_h[p][:, 0:HID], silu[p][:, :],
                                            ALU.mult).then_inc(a_done, 1)
                    v.wait_ge(aT_hi, t + 1)
                    nc.vector.tensor_tensor(aT[p][1][:, :], ps_a[p][:, :], f32(aT[p][0][:, :]),
                                            ALU.subtract).then_inc(aT_lo, 1)
                    v.wait_ge(z_done, t + 1)
                    if isinstance(t, int):
                        wait(v, z_stored[u % 4], 16 * (t // 4))
                    else:
                        v.wait_ge(z_stored[u % 4], 16 * (2 * j + u // 4))
                    nc.vector.tensor_copy(z[u % 4][:, :], ps_z[p][:, :]).then_inc(z_copied, 1)
                    if u % 4 == 3 and not last_round:
                        v.wait_ge(gathered[u], 16 * (j + 1))
                        indices(U * (j + 1) + u - 3, u // 4)

                for u in range(U):
                    step(u, u, 0, False)
                with v.Fori(1, ROUNDS - 1) as j:
                    for u in range(U):
                        step(U * j + u, u, j, False)
                for u in range(U):
                    step(U * (ROUNDS - 1) + u, u, ROUNDS - 1, True)


def combine(nc, c):
    STEPS = TILES // 4
    with ExitStack() as ctx:
        sb, ps, sem = allocator(nc, ctx)
        ws1_raw, ws2_raw = sb("ws1_raw", [P, DC, 2 * HS]), sb("ws2_raw", [P, 2, D])
        ws1 = [sb(f"ws1_{s}", [P, DC, 2 * HS], F32R) for s in ("hi", "lo")]
        ws2 = [sb(f"ws2_{s}", [P, 2, D], F32R) for s in ("hi", "lo")]
        index = [sb(f"zindex{i}", [P, 2, 4], I32) for i in range(2)]
        zg = [sb(f"zg{i}", [P, 8, D]) for i in range(2)]
        y = [sb(f"cy{i}", [P, 4, D]) for i in range(2)]
        x1 = [sb(f"cx{i}", [P, 4, D]) for i in range(2)]
        o = [sb(f"o{i}", [P, 4, D]) for i in range(2)]
        yT = [sb(f"cyT_{s}", [P, DC, 512], F32R) for s in ("hi", "lo")]
        silu = [sb(f"csilu{i}", [P, 512]) for i in range(2)]
        a = [sb(f"ca{i}", [P, 512]) for i in range(2)]
        aT = [[sb(f"caT{i}_{s}", [P, 2, 512], F32R) for s in ("hi", "lo")] for i in range(2)]
        ps_y = [ps(f"ps_cy{i}", [P, 512]) for i in range(2)]
        ps_g = [ps(f"ps_g{i}", [P, 512]) for i in range(2)]
        ps_u = [ps(f"ps_u{i}", [P, 512]) for i in range(2)]
        ps_o = [ps(f"ps_co{i}", [P, 512]) for i in range(2)]

        ws_in, ws_scaled, ws_hi, ws_ready = sem("ws_in"), sem("ws_scaled"), sem("ws_hi"), sem("ws_ready")
        y_in = [sem(f"cy_in{i}") for i in range(2)]
        x1_in = [sem(f"cx_in{i}") for i in range(2)]
        gathered = [sem(f"zgathered{i}") for i in range(2)]
        out_stored = [sem(f"out_stored{i}") for i in range(2)]
        index_ready, go = sem("zindex_ready"), sem("zgather_go")
        yT_done, yT_hi, yT_lo = sem("cyT_done"), sem("cyT_hi"), sem("cyT_lo")
        g_done, u_done, silu_done, a_done = sem("g_done"), sem("u_done"), sem("csilu_done"), sem("ca_done")
        aT_hi, aT_lo, o_done, added, fin1, fin2 = (
            sem("caT_hi"), sem("caT_lo"), sem("co_done"), sem("added"), sem("fin1"), sem("fin2"))

        def pipeline(eng, step):
            for G in range(4):
                step(G, G % 2, G // 2)
            with eng.Fori(2, STEPS // 2 - 1) as j:
                for r in range(2):
                    step(2 * j + r, r, j)
            for G in range(STEPS - 2, STEPS + 1):
                step(G, G % 2, G // 2)

        def exists(G):
            return not isinstance(G, int) or 0 <= G < STEPS

        with nc.Block() as block:

            @block.sync
            def _(sp):
                sp.dma_start(ws1_raw[:, :, :], c.Ws1.rearrange("(k p) h -> p k h", p=P)).then_inc(ws_in, 16)
                sp.dma_start(ws2_raw[:, :, :], c.Ws2.rearrange("(k p) h -> p k h", p=P)).then_inc(ws_in, 16)

                def rows(dram, G):
                    return dram[bass.ds(G * 512, 512), :].rearrange("(i p) d -> p i d", p=P)

                def step(G, r, j):
                    if exists(G):
                        wait(sp, yT_done, 2 * (G - 1))
                        sp.dma_start(y[r][:, :, :], rows(c.y, G)).then_inc(y_in[r], 16)
                        wait(sp, added, 4 * (G - 1))
                        sp.dma_start(x1[r][:, :, :], rows(c.x1, G)).then_inc(x1_in[r], 16)
                    if isinstance(G, int) and G == 0:
                        return
                    sp.wait_ge(fin2, 4 * G - 4) if not isinstance(G, int) or G > 1 else None
                    if not isinstance(G, int) or G > 1:
                        sp.dma_start(rows(c.out, G - 2), o[r][:, :, :]).then_inc(out_stored[r], 16)

                pipeline(sp, step)
                sp.wait_ge(fin2, 4 * STEPS)
                sp.dma_start(rows(c.out, STEPS - 1), o[(STEPS - 1) % 2][:, :, :]).then_inc(
                    out_stored[(STEPS - 1) % 2], 16)
                for r in range(2):
                    sp.wait_ge(out_stored[r], 16 * (STEPS // 2))

            @block.gpsimd
            def _(pool):
                def step(G, r, j):
                    if not exists(G):
                        return
                    pool.wait_ge(index_ready, 2 * G + 2)
                    wait(pool, fin2, 4 * (G - 1))
                    pool.sem_inc(go, 1)
                    for i in range(4):
                        for k in range(2):
                            pool.indirect_dma_start(
                                zg[r][:, 2 * i + k, :], None, c.z,
                                bass.IndirectOffsetOnAxis(index[r][:, k, i:i + 1], 0)).then_inc(gathered[r], 16)

                pipeline(pool, step)

            @block.tensor
            def _(pe):
                pe.wait_ge(ws_ready, 2)

                def transpose_y(G, r, j):
                    pe.wait_ge(y_in[r], 16 * (j + 1))
                    wait(pe, yT_lo, 2 * G)
                    for k in range(DC):
                        for i in range(4):
                            last = nc.tensor.transpose(ps_y[k][:, i * P:(i + 1) * P], y[r][:, i, k * P:(k + 1) * P],
                                                       c.ident[:, :])
                        last.then_inc(yT_done, 1)

                def hidden(G):
                    pe.wait_ge(yT_lo, 2 * G + 2)
                    wait(pe, a_done, 2 * G)
                    for n in range(2):
                        for bank, first, done in ((ps_g[n], HS + n * P, g_done), (ps_u[n], n * P, u_done)):
                            products(nc, bank[:, :], [
                                (ws1[0][:, k, first:first + P], ws1[1][:, k, first:first + P],
                                 yT[0][:, k, :], yT[1][:, k, :]) for k in range(DC)]).then_inc(done, 1)

                def down(G, r):
                    pe.wait_ge(aT_lo, 2 * G + 2)
                    for i in range(4):
                        wait(pe, added, 4 * G + i - 1)
                        products(nc, ps_o[i % 2][:, 0:D], [
                            (aT[r][0][:, n, i * P:(i + 1) * P], aT[r][1][:, n, i * P:(i + 1) * P],
                             ws2[0][:, n, :], ws2[1][:, n, :]) for n in range(2)]).then_inc(o_done, 1)

                transpose_y(0, 0, 0)

                def step(G, r, j):
                    if exists(G):
                        hidden(G)
                    if not isinstance(G, int) or G > 0:
                        down(G - 1, 1 - r)
                    if not isinstance(G, int) or G < STEPS - 1:
                        transpose_y(G + 1, 1 - r, j + r)

                pipeline(pe, step)

            @block.scalar
            def _(act):
                act.wait_ge(ws_in, 32)
                nc.scalar.activation(ws1[0][:, :, :], ws1_raw[:, :, :], ACT.Copy).then_inc(ws_hi, 1)
                act.wait_ge(ws_scaled, 1)
                nc.scalar.activation(ws2[0][:, :, :], ws2_raw[:, :, :], ACT.Copy).then_inc(ws_hi, 1)

                def high_yT(G):
                    wait(act, u_done, 2 * G)
                    for k in range(DC):
                        act.wait_ge(yT_done, 2 * G + k + 1)
                        nc.scalar.activation(yT[0][:, k, :], ps_y[k][:, :], ACT.Copy).then_inc(yT_hi, 1)

                high_yT(0)

                def step(G, r, j):
                    if exists(G):
                        for n in range(2):
                            act.wait_ge(g_done, 2 * G + n + 1)
                            wait(act, a_done, 2 * G + n - 1)
                            nc.scalar.activation(silu[n][:, :], ps_g[n][:, :], ACT.Silu).then_inc(silu_done, 1)
                            if n == 1:
                                high_aT(G, r, 0)
                        high_aT(G, r, 1)
                    if not isinstance(G, int) or G < STEPS - 1:
                        high_yT(G + 1)

                def high_aT(G, r, n):
                    act.wait_ge(a_done, 2 * G + n + 1)
                    wait(act, o_done, 4 * (G - 1))
                    nc.scalar.activation(aT[r][0][:, n, :], a[n][:, :], ACT.Copy).then_inc(aT_hi, 1)

                pipeline(act, step)

            @block.vector
            def _(v):
                V = nc.vector
                v.wait_ge(ws_in, 32)
                V.tensor_scalar(ws2_raw[:, :, :], ws2_raw[:, :, :], c.tanh_g[:, 1:2], None,
                                ALU.mult).then_inc(ws_scaled, 1)
                v.wait_ge(ws_hi, 2)
                V.tensor_tensor(ws1[1][:, :, :], ws1_raw[:, :, :], f32(ws1[0][:, :, :]),
                                ALU.subtract).then_inc(ws_ready, 1)
                V.tensor_tensor(ws2[1][:, :, :], ws2_raw[:, :, :], f32(ws2[0][:, :, :]),
                                ALU.subtract).then_inc(ws_ready, 1)

                def indices(G, r):
                    for k in range(2):
                        V.tensor_copy(index[r][:, k, :],
                                      c.slot_i[k][:, bass.ds(4 * G, 4)]).then_inc(index_ready, 1)

                def low_yT(G):
                    for k in range(DC):
                        v.wait_ge(yT_hi, 2 * G + k + 1)
                        V.tensor_tensor(yT[1][:, k, :], ps_y[k][:, :], f32(yT[0][:, k, :]),
                                        ALU.subtract).then_inc(yT_lo, 1)

                def low_aT(G, r, n):
                    v.wait_ge(aT_hi, 2 * G + n + 1)
                    V.tensor_tensor(aT[r][1][:, n, :], a[n][:, :], f32(aT[r][0][:, n, :]),
                                    ALU.subtract).then_inc(aT_lo, 1)

                def outputs(G, r, j):
                    v.wait_ge(x1_in[r], 16 * (j + 1))
                    wait(v, out_stored[r], 16 * j)
                    for i in range(4):
                        v.wait_ge(o_done, 4 * G + i + 1)
                        V.tensor_tensor(o[r][:, i, :], ps_o[i % 2][:, 0:D], x1[r][:, i, :],
                                        ALU.add).then_inc(added, 1)
                    v.wait_ge(gathered[r], 128 * (j + 1))
                    for k, done, before in ((0, fin1, added), (1, fin2, fin1)):
                        for i in range(4):
                            v.wait_ge(before, 4 * G + i + 1)
                            V.scalar_tensor_tensor(o[r][:, i, :], zg[r][:, 2 * i + k, :],
                                                   c.weight[k][:, bass.ds(4 * G + i, 1)], o[r][:, i, :],
                                                   ALU.mult, ALU.add).then_inc(done, 1)

                indices(0, 0)
                indices(1, 1)
                low_yT(0)

                def step(G, r, j):
                    if exists(G):
                        for n in range(2):
                            v.wait_ge(silu_done, 2 * G + n + 1)
                            v.wait_ge(u_done, 2 * G + n + 1)
                            wait(v, aT_lo, 2 * G + n - 1)
                            V.tensor_tensor(a[n][:, :], ps_u[n][:, :], silu[n][:, :], ALU.mult).then_inc(a_done, 1)
                            if n == 1:
                                low_aT(G, r, 0)
                        low_aT(G, r, 1)
                    if not isinstance(G, int) or G > 0:
                        outputs(G - 1, 1 - r, j if r else j - 1)
                    if not isinstance(G, int) or G < STEPS - 1:
                        low_yT(G + 1)
                    if not isinstance(G, int) or G > 0:
                        if not isinstance(G, int) or G + 1 < STEPS:
                            indices(G + 1, 1 - r)

                pipeline(v, step)


def flamingo(nc, x, xT, ctxT, g_xattn, g_ffn, WqT, WkT, Wv, Wout, bout, WgT, W1, W2, Ws1, Ws2, out, upto=9):
    c = Common()
    c.x, c.xT, c.ctxT, c.g_xattn, c.g_ffn = x, xT, ctxT, g_xattn, g_ffn
    c.WqT, c.WkT, c.Wv, c.Wout, c.bout = WqT, WkT, Wv, Wout, bout
    c.WgT, c.W1, c.W2, c.Ws1, c.Ws2, c.out = WgT, W1, W2, Ws1, Ws2, out
    c.x1 = nc.dram_tensor("x1_scratch", (T, D), F32, kind="Internal").ap()
    with ExitStack() as ctx:
        sb, _, _ = allocator(nc, ctx)
        c.ident = sb("ident", [P, P])
        c.tanh_g = sb("tanh_g", [P, 2])
        c.stats2 = sb("stats2", [P, TILES * 6])
        with ExitStack() as attention:
            sb, _, _ = allocator(nc, attention)
            c.rstd1 = sb("rstd1", [P, TILES])
            c.bias = sb("bias", [P, D])
            c.wqk_hi, c.wqk_lo = (sb(f"wqk_{s}", [P, 2, H, D], F32R) for s in ("hi", "lo"))
            c.wv_hi, c.wv_lo = (sb(f"wv_{s}", [P, 2, INNER], F32R) for s in ("hi", "lo"))
            c.wo_hi, c.wo_lo = (sb(f"wo_{s}", [P, 4, D], F32R) for s in ("hi", "lo"))
            prepare(nc, c)
            if upto >= 1:
                attend(nc, c)
        if upto < 2:
            return
        sb, _, _ = allocator(nc, ctx)
        c.y = nc.dram_tensor("y_scratch", (T, D), F32, kind="Internal").ap()
        c.z = nc.dram_tensor("z_scratch", (SLOT_TILES * P, D), F32, kind="Internal").ap()
        c.logits = sb("logits", [P, TILES * E])
        c.weight = [sb(f"weight{k}", [P, TILES]) for k in range(2)]
        c.slot_i = [sb(f"slot_i{k}", [P, TILES], I32) for k in range(2)]
        c.slot_token = sb("slot_token", [P, SLOT_TILES], I32)
        c.tile_expert = sb("tile_expert", [1, SLOT_TILES], I32)
        with ExitStack() as split_weights:
            sb, _, sem = allocator(nc, split_weights)
            c.weights_raw_in = sem("weights_raw_in")
            flat = [sb(f"w1_{s}", [P, E * DC * D], F32R) for s in ("hi", "lo")]
            c.w1_hi_flat, c.w1_lo_flat = flat
            c.w1_hi, c.w1_lo = (w[:, :].rearrange("p (e k h) -> p e k h", e=E, k=DC) for w in flat)
            flat = [sb(f"w2_{s}", [P, E * D], F32R) for s in ("hi", "lo")]
            c.w2_hi_flat, c.w2_lo_flat = flat
            c.w2_hi, c.w2_lo = (w[:, :].rearrange("p (e d) -> p e d", e=E) for w in flat)
            with ExitStack() as raw_weights:
                sb, _, _ = allocator(nc, raw_weights)
                c.w1_raw, c.w2_raw = sb("w1_raw", [P, E, DC, 2 * HID]), sb("w2_raw", [P, E, D])
                gate(nc, c)
                if upto >= 3:
                    route(nc, c)
            if upto >= 4:
                experts(nc, c)
        if upto >= 5:
            combine(nc, c)


_INS = ["x", "xT", "ctxT", "g_xattn", "g_ffn", "WqT", "WkT", "Wv", "Wout", "bout", "WgT", "W1", "W2", "Ws1", "Ws2"]


def kernel(**inputs):
    import numpy as np
    import concourse.bacc as bacc
    from concourse.bass_utils import run_bass_kernel_spmd

    def lay(name):
        return np.asarray(inputs[name])

    x = lay("x").reshape(T, D)
    laid = {
        "x": x,
        "xT": x.T,
        "ctxT": lay("ctx_768").reshape(B * CK, CD).T,
        "g_xattn": lay("g_xattn").reshape(1, 1),
        "g_ffn": lay("g_ffn").reshape(1, 1),
        "WqT": lay("L0_xattn_Wq").T,
        "WkT": lay("L0_xattn_Wk").T,
        "Wv": lay("L0_xattn_Wv"),
        "Wout": lay("L0_xattn_Wout"),
        "bout": lay("L0_xattn_bout").reshape(1, D),
        "WgT": lay("L0_ffn_Wg").T,
        "W1": lay("L0_ffn_W1"),
        "W2": lay("L0_ffn_W2"),
        "Ws1": lay("L0_ffn_Ws1"),
        "Ws2": lay("L0_ffn_Ws2"),
    }
    nc = bacc.Bacc("TRN2", target_bir_lowering=False, num_devices=1)
    arrays, args = {}, []
    for name in _INS:
        arrays[f"in_{name}"] = a = np.ascontiguousarray(laid[name])
        args.append(nc.dram_tensor(f"in_{name}", a.shape, mybir.dt.from_np(a.dtype), kind="ExternalInput").ap())
    out = nc.dram_tensor("out", (T, D), F32, kind="ExternalOutput").ap()
    flamingo(nc, *args, out)
    got = run_bass_kernel_spmd(nc, [arrays], core_ids=[0])
    return got.results[0]["out"].reshape(B, N, D)
```

```python
from contextlib import ExitStack

import concourse.bass as bass
from concourse import mybir

ALU = mybir.AluOpType
ACT = mybir.ActivationFunctionType
AX = mybir.AxisListType
F32 = mybir.dt.float32
F32R = mybir.dt.float32r
BF16 = mybir.dt.bfloat16
I32 = mybir.dt.int32

P = 128
B, N, D = 32, 256, 256
CK, CD = 77, 192
H, DH = 8, 64
INNER = H * DH
E, HID = 16, 128
HS = 2 * HID
T = B * N
TILES = T // P
DC = D // P
GB = 4
GROUPS = B // GB
GK = GB * CK
HK = H * CK
HALF = HK // 2
PAIRS = TILES + E
SLOT_TILES = 2 * PAIRS
LN_EPS = 1e-5
SCALE = DH ** -0.5
KP = 96


def wait(eng, sem, value):
    if not isinstance(value, int) or value > 0:
        eng.wait_ge(sem, value)


def f32(ap):
    return ap.bitcast(F32)


def products(nc, out, pairs, start=True, stop=True):
    last = None
    for n, (lh, ll, rh, rl) in enumerate(pairs):
        nc.tensor.matmul(out, lh, rh, start=start and n == 0, stop=False)
        nc.tensor.matmul(out, lh, rl, start=False, stop=False)
        last = nc.tensor.matmul(out, ll, rh, start=False, stop=stop and n == len(pairs) - 1)
    return last


class Common:
    pass


def allocator(nc, ctx):
    def sb(name, shape, dt=F32):
        return ctx.enter_context(nc.sbuf_tensor(name, shape, dt))

    def ps(name, shape):
        return ctx.enter_context(nc.psum_tensor(name, shape, F32))

    def sem(name):
        return ctx.enter_context(nc.semaphore(name))

    return sb, ps, sem


def rstd_steps(nc, v, stats, mean, rstd, var, chain, root_ready, root_done):
    step = [0]

    def link(ins):
        step[0] += 1
        ins.then_inc(chain, 1)
        v.wait_ge(chain, step[0])

    me, mo = stats[:, :, 1], stats[:, :, 4]
    link(nc.vector.tensor_tensor(mean, me, mo, ALU.add))
    link(nc.vector.tensor_scalar(mean, mean, 0.5, None, ALU.mult))
    link(nc.vector.tensor_tensor(rstd, mean, me, ALU.subtract))
    link(nc.vector.tensor_tensor(rstd, rstd, rstd, ALU.mult))
    link(nc.vector.scalar_tensor_tensor(rstd, stats[:, :, 2], 1.0 / D, rstd, ALU.mult, ALU.add))
    link(nc.vector.scalar_tensor_tensor(rstd, stats[:, :, 5], 1.0 / D, rstd, ALU.mult, ALU.add))
    link(nc.vector.tensor_scalar(rstd, rstd, LN_EPS, None, ALU.add))
    nc.vector.tensor_copy(var, rstd).then_inc(root_ready, 1)
    v.wait_ge(root_done, 1)
    link(nc.vector.reciprocal(rstd, rstd))
    link(nc.vector.tensor_tensor(var, var, rstd, ALU.mult))
    link(nc.vector.tensor_tensor(var, var, rstd, ALU.mult))
    link(nc.vector.tensor_scalar(var, var, -0.5, 1.5, ALU.mult, ALU.add))
    link(nc.vector.tensor_tensor(rstd, rstd, var, ALU.mult))


def prepare(nc, c):
    XB = 4
    with ExitStack() as ctx:
        sb, ps, sem = allocator(nc, ctx)
        wqT = sb("wqT", [DH, H, D])
        wkT = sb("wkT", [DH, H, CD])
        wqc = sb("wqc", [DH, H, D])
        qmean = sb("qmean", [DH, H])
        wv_raw = sb("wv_raw", [P, 2, INNER])
        wo_raw = sb("wo_raw", [P, 4, D])
        xs = [sb(f"xs{i}", [P, 4, D]) for i in range(XB)]
        stats = sb("stats1", [P, TILES, 6])
        mean1 = sb("mean1", [P, TILES])
        var1 = sb("var1", [P, TILES])
        gates = sb("gates", [P, 2])
        iota_row = sb("iota_row_f", [P, P])
        pk = [ps(f"pk{i}", [P, 512]) for i in range(4)]

        weights_in, wv_in, wo_in, gates_in = sem("weights_in"), sem("wv_in"), sem("wo_in"), sem("gates_in")
        x_in = [sem(f"pre_x_in{i}") for i in range(XB)]
        stats_done, chain1 = sem("stats_done"), sem("chain1")
        root_ready, root_done = sem("root_ready1"), sem("root_done1")
        qmean_done, qmean_scaled, centred = sem("qmean_done"), sem("qmean_scaled"), sem("centred")
        fold_done, fold_hi, fold_lo = sem("fold_done"), sem("fold_hi"), sem("fold_lo")
        tanh_done, bias_done, wo_scaled = sem("tanh_done"), sem("bias_done"), sem("wo_scaled")
        zeroed, w_hi, w_lo, ident_done = sem("zeroed"), sem("w_hi"), sem("w_lo"), sem("ident_done")

        with nc.Block() as block:

            @block.sync
            def _(sp):
                sp.dma_start(wqT[:, :, :], c.WqT.rearrange("(h i) d -> i h d", h=H)).then_inc(weights_in, 16)
                sp.dma_start(wkT[:, :, :], c.WkT.rearrange("(h i) d -> i h d", h=H)).then_inc(weights_in, 16)
                sp.dma_start(gates[:, 0:1], c.g_xattn.broadcast_to((P, 1))).then_inc(gates_in, 16)
                sp.dma_start(gates[:, 1:2], c.g_ffn.broadcast_to((P, 1))).then_inc(gates_in, 16)
                sp.dma_start(c.bias[:, :], c.bout.broadcast_to((P, D))).then_inc(gates_in, 16)
                for n in range(TILES // 4):
                    if n >= XB:
                        sp.wait_ge(stats_done, 4 * (n - XB + 1))
                    sp.dma_start(xs[n % XB][:, :, :],
                                 c.x[n * 512:(n + 1) * 512, :].rearrange("(i p) d -> p i d", p=P)
                                 ).then_inc(x_in[n % XB], 16)
                    if n == 3:
                        sp.dma_start(wv_raw[:, 0, :], c.Wv[0:P, :]).then_inc(wv_in, 16)
                        sp.dma_start(wv_raw[0:CD - P, 1, :], c.Wv[P:CD, :]).then_inc(wv_in, 16)
                        sp.dma_start(wo_raw[:, :, :], c.Wout.rearrange("(c p) n -> p c n", p=P)).then_inc(wo_in, 16)

            @block.gpsimd
            def _(pool):
                nc.gpsimd.memset(c.ident[:, :], 0.0).then_inc(ident_done, 1)
                pool.wait_ge(ident_done, 1)
                nc.gpsimd.affine_select(out=c.ident[:, :], in_=c.ident[:, :], compare_op=ALU.not_equal, fill=1.0,
                                        base=0, pattern=[[-1, P]], channel_multiplier=1).then_inc(ident_done, 1)
                for w in (c.wv_hi, c.wv_lo):
                    nc.gpsimd.memset(f32(w[:, 1, :]), 0.0).then_inc(zeroed, 1)
                for w in (c.wqk_hi, c.wqk_lo):
                    nc.gpsimd.memset(f32(w[:, 1, :, :]), 0.0).then_inc(zeroed, 1)
                pool.wait_ge(w_hi, 2)
                nc.gpsimd.tensor_tensor(c.wv_lo[:, 0, :], wv_raw[:, 0, :], f32(c.wv_hi[:, 0, :]),
                                        ALU.subtract).then_inc(w_lo, 1)
                nc.gpsimd.tensor_tensor(c.wv_lo[0:CD - P, 1, :], wv_raw[0:CD - P, 1, :],
                                        f32(c.wv_hi[0:CD - P, 1, :]), ALU.subtract).then_inc(w_lo, 1)
                pool.wait_ge(w_hi, 3)
                nc.gpsimd.tensor_tensor(c.wo_lo[:, :, :], wo_raw[:, :, :], f32(c.wo_hi[:, :, :]),
                                        ALU.subtract).then_inc(w_lo, 1)

            @block.tensor
            def _(pe):
                pe.wait_ge(centred, H)
                for h in range(H):
                    for cc, rows in ((0, P), (1, CD - P)):
                        n = 2 * h + cc
                        if n >= 4:
                            pe.wait_ge(fold_lo, n - 3)
                        nc.tensor.matmul(pk[n % 4][0:rows, 0:D], wkT[:, h, cc * P:cc * P + rows], wqc[:, h, :],
                                         start=True, stop=True).then_inc(fold_done, 1)

            @block.scalar
            def _(act):
                act.wait_ge(gates_in, 48)
                nc.scalar.activation(c.tanh_g[:, :], gates[:, :], ACT.Tanh).then_inc(tanh_done, 1)
                act.wait_ge(wv_in, 32)
                act.wait_ge(zeroed, 4)
                nc.scalar.activation(c.wv_hi[:, 0, :], wv_raw[:, 0, :], ACT.Copy).then_inc(w_hi, 1)
                nc.scalar.activation(c.wv_hi[0:CD - P, 1, :], wv_raw[0:CD - P, 1, :], ACT.Copy).then_inc(w_hi, 1)
                for n in range(2 * H):
                    h, cc = n // 2, n % 2
                    rows = CD - P if cc else P
                    act.wait_ge(fold_done, n + 1)
                    nc.scalar.activation(c.wqk_hi[0:rows, cc, h, :], pk[n % 4][0:rows, 0:D],
                                         ACT.Copy).then_inc(fold_hi, 1)
                act.wait_ge(wo_scaled, 1)
                nc.scalar.activation(c.wo_hi[:, :, :], wo_raw[:, :, :], ACT.Copy).then_inc(w_hi, 1)
                act.wait_ge(root_ready, 1)
                nc.scalar.activation(c.rstd1[:, :], c.rstd1[:, :], ACT.Sqrt).then_inc(root_done, 1)

            @block.vector
            def _(v):
                v.wait_ge(weights_in, 32)
                nc.vector.tensor_reduce(qmean[:, :], wqT[:, :, :], AX.X, ALU.add).then_inc(qmean_done, 1)
                v.wait_ge(qmean_done, 1)
                nc.vector.tensor_scalar(qmean[:, :], qmean[:, :], 1.0 / D, None, ALU.mult).then_inc(qmean_scaled, 1)
                v.wait_ge(qmean_scaled, 1)
                for h in range(H):
                    nc.vector.tensor_scalar(wqc[:, h, :], wqT[:, h, :], qmean[:, h:h + 1], SCALE,
                                            ALU.subtract, ALU.mult).then_inc(centred, 1)

                def tile_stats(t):
                    n = t // 4
                    v.wait_ge(x_in[n % XB], 16 * (n // XB + 1))
                    nc.vector.bn_stats(stats[:, t, :], xs[n % XB][:, t % 4, :]).then_inc(stats_done, 1)

                for n in range(2 * H):
                    h, cc = n // 2, n % 2
                    rows = CD - P if cc else P
                    tile_stats(n)
                    v.wait_ge(fold_hi, n + 1)
                    nc.vector.tensor_tensor(c.wqk_lo[0:rows, cc, h, :], pk[n % 4][0:rows, 0:D],
                                            f32(c.wqk_hi[0:rows, cc, h, :]), ALU.subtract).then_inc(fold_lo, 1)
                v.wait_ge(tanh_done, 1)
                v.wait_ge(gates_in, 48)
                nc.vector.tensor_scalar(c.bias[:, :], c.bias[:, :], c.tanh_g[:, 0:1], None,
                                        ALU.mult).then_inc(bias_done, 1)
                v.wait_ge(wo_in, 16)
                nc.vector.tensor_scalar(wo_raw[:, :, :], wo_raw[:, :, :], c.tanh_g[:, 0:1], None,
                                        ALU.mult).then_inc(wo_scaled, 1)
                for t in range(2 * H, TILES):
                    tile_stats(t)
                v.wait_ge(stats_done, TILES)
                rstd_steps(nc, v, stats, mean1[:, :], c.rstd1[:, :], var1[:, :], chain1, root_ready, root_done)


def attend(nc, c):
    with ExitStack() as ctx:
        sb, ps, sem = allocator(nc, ctx)
        ctx_raw = sb("ctx_raw", [P, 2, GK])
        ctxM = [sb(f"ctxM_{s}", [P, 2, GK], F32R) for s in ("hi", "lo")]
        ctxb_raw = [sb(f"ctxb_raw{i}", [P, 2, CK]) for i in range(2)]
        ctxb = [[sb(f"ctxb{i}_{s}", [P, 2, CK], F32R) for s in ("hi", "lo")] for i in range(2)]
        xT_raw = [sb(f"xT_raw{i}", [P, DC, N]) for i in range(2)]
        xT = [[sb(f"xT{i}_{s}", [P, DC, N], F32R) for s in ("hi", "lo")] for i in range(2)]
        x_tok = [sb(f"x_tok{i}", [P, 2, D]) for i in range(2)]
        x1_tok = [sb(f"x1_tok{i}", [P, 2, D]) for i in range(2)]
        M = [sb(f"M_{s}", [P, 2 * DC * GB * HK], F32R) for s in ("hi", "lo")]
        prob = [sb(f"prob{i}", [P, HK]) for i in range(2)]
        row_max = [sb(f"row_max{i}", [P, H]) for i in range(2)]
        row_sum = [sb(f"row_sum{i}", [P, H]) for i in range(2)]
        PT = [sb(f"PT_{s}", [KP, H, N], F32R) for s in ("hi", "lo")]
        V = [sb(f"V_{s}", [KP, 4, 4, DH], F32R) for s in ("hi", "lo")]
        OT = [sb(f"OT_{s}", [P, 4, N], F32R) for s in ("hi", "lo")]
        ps_proj = [ps(f"ps_proj{i}", [P, 512]) for i in range(2)]
        ps_s = ps("ps_s", [P, 2, 512])
        ps_pt = [ps(f"ps_pt{i}", [P, 512]) for i in range(2)]
        ps_o = [ps(f"ps_o{i}", [P, 512]) for i in range(2)]

        ctx_in = sem("ctx_in")
        ctxb_in = [sem(f"ctxb_in{i}") for i in range(2)]
        xT_in = [sem(f"xT_in{i}") for i in range(2)]
        x_in = [sem(f"x_in{i}") for i in range(2)]
        x1_out = [sem(f"x1_out{i}") for i in range(2)]
        pads_zero, ctx_hi, ctx_split = sem("pads_zero"), sem("ctx_hi"), sem("ctx_split")
        x_hi, x_split, cb_split = sem("x_hi"), sem("x_split"), sem("cb_split")
        normed, biased = sem("normed"), sem("biased")
        score_done, M_done, V_done, PT_done, OT_done, out_done = (
            sem("score_done"), sem("M_done"), sem("V_done"), sem("PT_done"), sem("OT_done"), sem("out_done"))
        M_hi, V_hi, PT_hi, OT_hi, exp_done = sem("M_hi"), sem("V_hi"), sem("PT_hi"), sem("OT_hi"), sem("exp_done")
        M_lo, V_lo, PT_lo, OT_lo = sem("M_lo"), sem("V_lo"), sem("PT_lo"), sem("OT_lo")
        max_done, sub_done, sum_done, inv_done = sem("max_done"), sem("sub_done"), sem("sum_done"), sem("inv_done")
        x1_done, x1_stats = sem("x1_done"), sem("x1_stats")

        MPAR = DC * GB * HK

        def M_at(s, parity, cc, q, lo, size):
            return M[s][:, bass.ds(parity * MPAR + (cc * GB + q) * HK + lo, size)]

        def groups(eng, body):
            body(0, True, False)
            with eng.Fori(1, GROUPS - 2) as g:
                body(g, False, False)
            body(GROUPS - 2, False, False)
            body(GROUPS - 1, False, True)

        def exists(g):
            return not isinstance(g, int) or g < GROUPS

        def tokens(b):
            return c.x[bass.ds(b * N, N), :].rearrange("(i p) d -> p i d", p=P)

        with nc.Block() as block:

            @block.sync
            def _(sp):
                def load_x_side(b, par):
                    sp.dma_start(xT_raw[par][:, :, :],
                                 c.xT[:, bass.ds(b * N, N)].rearrange("(c p) n -> p c n", p=P)).then_inc(xT_in[par], 16)
                    sp.dma_start(ctxb_raw[par][:, 0, :], c.ctxT[0:P, bass.ds(b * CK, CK)]).then_inc(ctxb_in[par], 16)
                    sp.dma_start(ctxb_raw[par][0:CD - P, 1, :],
                                 c.ctxT[P:CD, bass.ds(b * CK, CK)]).then_inc(ctxb_in[par], 16)

                def load_group(g):
                    sp.dma_start(ctx_raw[:, 0, :], c.ctxT[0:P, bass.ds(g * GK, GK)]).then_inc(ctx_in, 16)
                    sp.dma_start(ctx_raw[0:CD - P, 1, :], c.ctxT[P:CD, bass.ds(g * GK, GK)]).then_inc(ctx_in, 16)

                def store(b, par):
                    sp.wait_ge(x1_done, 2 * b + 2)
                    sp.dma_start(c.x1[bass.ds(b * N, N), :].rearrange("(i p) d -> p i d", p=P),
                                 x1_tok[par][:, :, :]).then_inc(x1_out[par], 16)

                load_group(0)
                load_x_side(0, 0)
                load_x_side(1, 1)
                sp.dma_start(x_tok[0][:, :, :], tokens(0)).then_inc(x_in[0], 16)
                sp.wait_ge(ctx_split, 1)
                load_group(1)

                def body(g, first, last):
                    for q in range(GB):
                        b, par, nxt = GB * g + q, q % 2, (q + 1) % 2
                        if q == 0 and exists(g + 2):
                            sp.wait_ge(ctx_split, g + 2)
                            load_group(g + 2)
                        if not (last and q >= GB - 2):
                            sp.wait_ge(x_split, b + 1)
                            sp.wait_ge(cb_split, b + 1)
                            load_x_side(b + 2, par)
                        if not (last and q == GB - 1):
                            wait(sp, x1_done, 2 * b)
                            sp.dma_start(x_tok[nxt][:, :, :], tokens(b + 1)).then_inc(x_in[nxt], 16)
                        if not (first and q == 0):
                            store(b - 1, nxt)

                groups(sp, body)
                store(B - 1, (B - 1) % 2)
                for par in range(2):
                    sp.wait_ge(x1_out[par], 16 * (B // 2))

            @block.gpsimd
            def _(pool):
                for w in (*ctxM, *ctxb[0], *ctxb[1]):
                    nc.gpsimd.memset(f32(w[:, 1, :]), 0.0).then_inc(pads_zero, 1)
                for w in (*PT, *V):
                    nc.gpsimd.memset(f32(w[:]), 0.0).then_inc(pads_zero, 1)

                pool.wait_ge(pads_zero, 10)

                def split_group(g):
                    pool.wait_ge(ctx_hi, 2 * g + 2)
                    nc.gpsimd.tensor_tensor(ctxM[1][:, 0, :], ctx_raw[:, 0, :], f32(ctxM[0][:, 0, :]), ALU.subtract)
                    nc.gpsimd.tensor_tensor(ctxM[1][0:CD - P, 1, :], ctx_raw[0:CD - P, 1, :],
                                            f32(ctxM[0][0:CD - P, 1, :]), ALU.subtract).then_inc(ctx_split, 1)

                def split_batch(b, par):
                    pool.wait_ge(x_hi, 3 * b + 3)
                    nc.gpsimd.tensor_tensor(xT[par][1][:, :, :], xT_raw[par][:, :, :], f32(xT[par][0][:, :, :]),
                                            ALU.subtract).then_inc(x_split, 1)
                    nc.gpsimd.tensor_tensor(ctxb[par][1][:, 0, :], ctxb_raw[par][:, 0, :],
                                            f32(ctxb[par][0][:, 0, :]), ALU.subtract)
                    nc.gpsimd.tensor_tensor(ctxb[par][1][0:CD - P, 1, :], ctxb_raw[par][0:CD - P, 1, :],
                                            f32(ctxb[par][0][0:CD - P, 1, :]), ALU.subtract).then_inc(cb_split, 1)

                def norm(b, i):
                    pool.wait_ge(inv_done, 2 * b + i + 1)
                    pr = prob[i][:, :].rearrange("p (h k) -> p h k", h=H)
                    nc.gpsimd.tensor_tensor(pr, pr, row_sum[i][:, :].unsqueeze(2).broadcast_to((P, H, CK)),
                                            ALU.mult).then_inc(normed, 1)

                split_group(0)
                split_batch(0, 0)
                split_group(1)

                def body(g, first, last):
                    for q in range(GB):
                        b, par, nxt = GB * g + q, q % 2, (q + 1) % 2
                        if not (last and q == GB - 1):
                            split_batch(b + 1, nxt)
                        norm(b, 0)
                        pool.wait_ge(x_in[par], 16 * (2 * g + q // 2 + 1))
                        xr = x_tok[par][:, :, :]
                        nc.gpsimd.tensor_tensor(xr, xr, c.bias[:, :].unsqueeze(1).broadcast_to((P, 2, D)),
                                                ALU.add).then_inc(biased, 1)
                        norm(b, 1)
                        if q == GB - 1 and exists(g + 2):
                            split_group(g + 2)

                groups(pool, body)

            @block.tensor
            def _(pe):
                def make_M(n, g, cc, h):
                    wait(pe, M_lo, n - 1)
                    bank = ps_proj[cc]
                    products(nc, bank[:, 0:GK], [
                        (c.wqk_hi[:, k, h, cc * P:(cc + 1) * P], c.wqk_lo[:, k, h, cc * P:(cc + 1) * P],
                         ctxM[0][:, k, :], ctxM[1][:, k, :]) for k in range(2)]).then_inc(M_done, 1)

                def scores(b, g, q, i):
                    wait(pe, sub_done, 2 * b + i)
                    xs = xT[q % 2]
                    for half in range(2):
                        last = products(nc, ps_s[:, half, 0:HALF], [
                            (xs[0][:, k, i * P:(i + 1) * P], xs[1][:, k, i * P:(i + 1) * P],
                             M_at(0, g % 2, k, q, half * HALF, HALF), M_at(1, g % 2, k, q, half * HALF, HALF))
                            for k in range(DC)])
                    last.then_inc(score_done, 1)

                def attend_values(b):
                    pe.wait_ge(PT_lo, 4 * b + 4)
                    pe.wait_ge(V_lo, b + 1)
                    wait(pe, x1_done, 2 * b)
                    for k in range(2):
                        for pr in range(2):
                            pair = 2 * k + pr
                            last = products(nc, ps_o[k][:, pr * N:(pr + 1) * N], [
                                (V[0][:, pair, 2 * j:2 * j + 2, :].rearrange("p a e -> p (a e)"),
                                 V[1][:, pair, 2 * j:2 * j + 2, :].rearrange("p a e -> p (a e)"),
                                 PT[0][:, 2 * pair + j, :], PT[1][:, 2 * pair + j, :]) for j in range(2)])
                        last.then_inc(OT_done, 1)

                def project_out(b):
                    pe.wait_ge(OT_lo, 2 * b + 2)
                    for i in range(2):
                        products(nc, ps_o[i][:, 0:D], [
                            (OT[0][:, k, i * P:(i + 1) * P], OT[1][:, k, i * P:(i + 1) * P],
                             c.wo_hi[:, k, :], c.wo_lo[:, k, :]) for k in range(4)]).then_inc(out_done, 1)

                def make_V(b, par, m_units):
                    pe.wait_ge(cb_split, b + 1)
                    pe.wait_ge(M_lo, m_units)
                    products(nc, ps_proj[0][0:CK, :], [
                        (ctxb[par][0][:, k, :], ctxb[par][1][:, k, :], c.wv_hi[:, k, :], c.wv_lo[:, k, :])
                        for k in range(2)]).then_inc(V_done, 1)

                def transpose_probs(b, i):
                    pe.wait_ge(normed, 2 * b + i + 1)
                    for j in range(2):
                        wait(pe, PT_lo, 4 * b + 2 * i + j - 1)
                        for h in range(4):
                            lo = (4 * j + h) * CK
                            last = nc.tensor.transpose(ps_pt[j][0:CK, h * P:(h + 1) * P], prob[i][:, lo:lo + CK],
                                                       c.ident[:, :])
                        last.then_inc(PT_done, 1)

                def make_M_units(b, g, q, head):
                    for k in (2 * head, 2 * head + 1):
                        make_M(2 * H + 4 * b + k, g + 1, k % 2, 2 * q + head)

                pe.wait_ge(pads_zero, 10)
                pe.wait_ge(ctx_split, 1)
                for n in range(2 * H):
                    make_M(n, 0, n % 2, n // 2)

                def body(g, first, last):
                    for q in range(GB):
                        b = GB * g + q
                        pe.wait_ge(x_split, b + 1)
                        if q == 0:
                            pe.wait_ge(M_lo, 2 * H * (g + 1))
                        scores(b, g, q, 0)
                        if not last:
                            if q == 0:
                                pe.wait_ge(ctx_split, g + 2)
                            wait(pe, V_lo, 0 if first and q == 0 else b)
                            make_M_units(b, g, q, 0)
                        if not (first and q == 0):
                            attend_values(b - 1)
                        scores(b, g, q, 1)
                        if not last:
                            make_M_units(b, g, q, 1)
                        transpose_probs(b, 0)
                        if not (first and q == 0):
                            project_out(b - 1)
                        make_V(b, q % 2, 2 * H * GROUPS if last else 2 * H + 4 * b + 3)
                        transpose_probs(b, 1)

                groups(pe, body)
                attend_values(B - 1)
                project_out(B - 1)

            def M_out(s, parity, cc, h):
                region = M[s][:, bass.ds(parity * MPAR + cc * GB * HK, GB * HK)]
                return region.rearrange("p (b x) -> p b x", b=GB)[:, :, h * CK:(h + 1) * CK]

            def M_bank(cc):
                return ps_proj[cc][:, 0:GK].rearrange("p (b k) -> p b k", b=GB)

            def V_out(s):
                return V[s][0:CK, :, 0:4:3, :]

            V_bank = ps_proj[0][0:CK, :].rearrange("p (a b e) -> p a b e", a=4, b=2)

            def PT_out(s, i, j):
                return PT[s][0:CK, 4 * j:4 * j + 4, i * P:(i + 1) * P]

            def PT_bank(j):
                return ps_pt[j][0:CK, :].rearrange("p (h n) -> p h n", h=4)

            def OT_out(s, k):
                return OT[s][:, 2 * k:2 * k + 2, :]

            def OT_bank(k):
                return ps_o[k][:, :].rearrange("p (c n) -> p c n", c=2)

            @block.scalar
            def _(act):
                def high(out, bank, done):
                    nc.scalar.activation(out, bank, ACT.Copy).then_inc(done, 1)

                def exponentials(b, i):
                    act.wait_ge(sub_done, 2 * b + i + 1)
                    nc.scalar.activation(prob[i][:, :], prob[i][:, :], ACT.Exp,
                                         scale=c.rstd1[:, bass.ds(2 * b + i, 1)]).then_inc(exp_done, 1)

                def high_OT(b):
                    for k in range(2):
                        act.wait_ge(OT_done, 2 * b + k + 1)
                        high(OT_out(0, k), OT_bank(k), OT_hi)

                def high_M(n, parity, cc, h):
                    act.wait_ge(M_done, n + 1)
                    high(M_out(0, parity, cc, h), M_bank(cc), M_hi)

                def high_M_units(b, g, q, head):
                    for k in (2 * head, 2 * head + 1):
                        high_M(2 * H + 4 * b + k, (g + 1) % 2, k % 2, 2 * q + head)

                def high_PT(b, i):
                    for j in range(2):
                        act.wait_ge(PT_done, 4 * b + 2 * i + j + 1)
                        high(PT_out(0, i, j), PT_bank(j), PT_hi)

                def high_group(g):
                    act.wait_ge(ctx_in, 32 * (g + 1))
                    wait(act, M_done, 2 * H * g)
                    high(ctxM[0][:, 0, :], ctx_raw[:, 0, :], ctx_hi)
                    high(ctxM[0][0:CD - P, 1, :], ctx_raw[0:CD - P, 1, :], ctx_hi)

                def high_batch(b, b_half, par):
                    act.wait_ge(xT_in[par], 16 * (b_half + 1))
                    wait(act, score_done, 2 * b - 2)
                    high(xT[par][0][:, :, :], xT_raw[par][:, :, :], x_hi)
                    act.wait_ge(ctxb_in[par], 32 * (b_half + 1))
                    wait(act, V_done, b - 1)
                    high(ctxb[par][0][:, 0, :], ctxb_raw[par][:, 0, :], x_hi)
                    high(ctxb[par][0][0:CD - P, 1, :], ctxb_raw[par][0:CD - P, 1, :], x_hi)

                act.wait_ge(pads_zero, 10)
                high_group(0)
                high_batch(0, 0, 0)
                for n in range(2 * H):
                    high_M(n, 0, n % 2, n // 2)
                high_group(1)

                def body(g, first, last):
                    for q in range(GB):
                        b = GB * g + q
                        if not (last and q == GB - 1):
                            high_batch(b + 1, 2 * g + (q + 1) // 2, (q + 1) % 2)
                        if not last:
                            high_M_units(b, g, q, 0)
                        exponentials(b, 0)
                        if not (first and q == 0):
                            high_OT(b - 1)
                        if not last:
                            high_M_units(b, g, q, 1)
                        exponentials(b, 1)
                        if q == GB - 1 and exists(g + 2):
                            high_group(g + 2)
                        high_PT(b, 0)
                        act.wait_ge(V_done, b + 1)
                        high(V_out(0), V_bank, V_hi)
                        high_PT(b, 1)

                groups(act, body)
                high_OT(B - 1)

            @block.vector
            def _(v):
                def low(lo, hi, bank, done):
                    nc.vector.tensor_tensor(lo, bank, f32(hi), ALU.subtract).then_inc(done, 1)

                S = ps_s[:, :, 0:HALF].rearrange("p a (h k) -> p a h k", h=4)

                def subtract_max(b, i):
                    v.wait_ge(score_done, 2 * b + i + 1)
                    mx = row_max[i][:, :].rearrange("p (a h) -> p a h", a=2)
                    nc.vector.tensor_reduce(mx, S, AX.X, ALU.max).then_inc(max_done, 1)
                    v.wait_ge(max_done, 2 * b + i + 1)
                    wait(v, PT_done, 4 * b + 2 * i - 2)
                    nc.vector.tensor_tensor(prob[i][:, :].rearrange("p (a h k) -> p a h k", a=2, h=4), S,
                                            mx.unsqueeze(3).broadcast_to((P, 2, 4, CK)),
                                            ALU.subtract).then_inc(sub_done, 1)

                def sums(b, i):
                    v.wait_ge(exp_done, 2 * b + i + 1)
                    wait(v, normed, 2 * b + i - 1)
                    nc.vector.tensor_reduce(row_sum[i][:, :], prob[i][:, :].rearrange("p (h k) -> p h k", h=H),
                                            AX.X, ALU.add).then_inc(sum_done, 1)
                    v.wait_ge(sum_done, 2 * b + i + 1)
                    nc.vector.reciprocal(row_sum[i][:, :], row_sum[i][:, :]).then_inc(inv_done, 1)

                def low_OT(b, k):
                    v.wait_ge(OT_hi, 2 * b + k + 1)
                    low(OT_out(1, k), OT_out(0, k), OT_bank(k), OT_lo)

                def residual(b, b_half, par):
                    v.wait_ge(biased, b + 1)
                    wait(v, x1_out[par], 16 * b_half)
                    for i in range(2):
                        v.wait_ge(out_done, 2 * b + i + 1)
                        nc.vector.tensor_tensor(x1_tok[par][:, i, :], ps_o[i][:, 0:D], x_tok[par][:, i, :],
                                                ALU.add).then_inc(x1_done, 1)
                        v.wait_ge(x1_done, 2 * b + i + 1)
                        nc.vector.bn_stats(c.stats2[:, bass.ds((2 * b + i) * 6, 6)],
                                           x1_tok[par][:, i, :]).then_inc(x1_stats, 1)

                def low_M(n, parity, cc, h):
                    v.wait_ge(M_hi, n + 1)
                    low(M_out(1, parity, cc, h), M_out(0, parity, cc, h), M_bank(cc), M_lo)

                def low_M_units(b, g, q, head):
                    for k in (2 * head, 2 * head + 1):
                        low_M(2 * H + 4 * b + k, (g + 1) % 2, k % 2, 2 * q + head)

                def low_PT(b, i):
                    for j in range(2):
                        v.wait_ge(PT_hi, 4 * b + 2 * i + j + 1)
                        low(PT_out(1, i, j), PT_out(0, i, j), PT_bank(j), PT_lo)

                v.wait_ge(pads_zero, 10)
                for n in range(2 * H):
                    low_M(n, 0, n % 2, n // 2)

                def body(g, first, last):
                    for q in range(GB):
                        b = GB * g + q
                        subtract_max(b, 0)
                        if not last:
                            low_M_units(b, g, q, 0)
                        sums(b, 0)
                        if not (first and q == 0):
                            low_OT(b - 1, 0)
                            low_OT(b - 1, 1)
                        subtract_max(b, 1)
                        if not last:
                            low_M_units(b, g, q, 1)
                        sums(b, 1)
                        low_PT(b, 0)
                        if not (first and q == 0):
                            residual(b - 1, 2 * g + (q - 1) // 2, (q + 1) % 2)
                        v.wait_ge(V_hi, b + 1)
                        low(V_out(1), V_out(0), V_bank, V_lo)
                        low_PT(b, 1)

                groups(v, body)
                low_OT(B - 1, 0)
                low_OT(B - 1, 1)
                residual(B - 1, B // 2 - 1, (B - 1) % 2)
                v.wait_ge(x1_stats, 2 * B)



def gate(nc, c):
    STEPS = TILES // 4
    with ExitStack() as ctx:
        sb, ps, sem = allocator(nc, ctx)
        mean2, rstd2, shift2 = sb("mean2", [P, TILES]), sb("rstd2", [P, TILES]), sb("shift2", [P, TILES])
        var2 = sb("var2", [P, TILES])
        wg_raw = sb("wg_raw", [P, DC, E])
        wg = [sb(f"wg_{s}", [P, DC, P], F32R) for s in ("hi", "lo")]
        x1_in = [sb(f"x1_in{i}", [P, 4, D]) for i in range(2)]
        y = [sb(f"y{i}", [P, 4, D]) for i in range(2)]
        yT = [[sb(f"yT{i}_{s}", [P, DC, 512], F32R) for s in ("hi", "lo")] for i in range(2)]
        lgT = [sb(f"lgT{i}", [P, 512]) for i in range(2)]
        ps_y = [ps(f"ps_y{i}", [P, 512]) for i in range(4)]
        ps_lt = [ps(f"ps_lt{i}", [P, 512]) for i in range(2)]
        ps_l = [ps(f"ps_l{i}", [P, 4, P]) for i in range(2)]

        x1_loaded = [sem(f"x1_loaded{i}") for i in range(2)]
        y_stored = [sem(f"y_stored{i}") for i in range(2)]
        raw_in, wg_in = c.weights_raw_in, sem("wg_in")
        chain2, root_ready, root_done, ln_ready = sem("chain2"), sem("root_ready2"), sem("root_done2"), sem("ln_ready")
        wg_zero, wg_hi_done, wg_ready = sem("wg_zero"), sem("wg_hi_done"), sem("wg_ready")
        y_done, yT_done, yT_hi, yT_lo = sem("y_done"), sem("yT_done"), sem("yT_hi"), sem("yT_lo")
        lt_done, lt_copied, l_done, l_copied = sem("lt_done"), sem("lt_copied"), sem("l_done"), sem("l_copied")
        logits = c.logits[:, :].rearrange("p (t e) -> p t e", e=E)
        stats = c.stats2[:, :].rearrange("p (t s) -> p t s", s=6)

        def pipeline(eng, step):
            for G in range(4):
                step(G, G % 2, G // 2)
            with eng.Fori(2, STEPS // 2) as j:
                for r in range(2):
                    step(2 * j + r, r, j)
            for G in (STEPS, STEPS + 1):
                step(G, G % 2, STEPS // 2)

        def fills(G, lag):
            return not isinstance(G, int) or 0 <= G - lag < STEPS

        with nc.Block() as block:

            @block.sync
            def _(sp):
                sp.dma_start(wg_raw[:, :, :], c.WgT.rearrange("(k p) e -> p k e", p=P)).then_inc(wg_in, 16)

                def step(G, r, j):
                    if fills(G, 0):
                        wait(sp, y_done, 4 * (G - 1))
                        sp.dma_start(x1_in[r][:, :, :],
                                     c.x1[bass.ds(G * 512, 512), :].rearrange("(i p) d -> p i d", p=P)
                                     ).then_inc(x1_loaded[r], 16)
                    if fills(G, 1):
                        sp.wait_ge(y_done, 4 * G)
                        sp.dma_start(c.y[bass.ds((G - 1) * 512, 512), :].rearrange("(i p) d -> p i d", p=P),
                                     y[1 - r][:, :, :]).then_inc(y_stored[1 - r], 16)

                pipeline(sp, step)
                for r in range(2):
                    sp.wait_ge(y_stored[r], 16 * (STEPS // 2))

            @block.gpsimd
            def _(pool):
                for w in wg:
                    nc.gpsimd.memset(f32(w[:, :, :]), 0.0).then_inc(wg_zero, 1)
                for e in range(0, E, 4):
                    pool.dma_start(c.w1_raw[:, e:e + 4, :, :],
                                   c.W1[e:e + 4].rearrange("e (k p) h -> p e k h", p=P)).then_inc(raw_in, 16)
                    pool.dma_start(c.w2_raw[:, e:e + 4, :],
                                   c.W2[e:e + 4].rearrange("e p d -> p e d")).then_inc(raw_in, 16)
                pool.wait_ge(raw_in, 16 * 8)

            @block.tensor
            def _(pe):
                pe.wait_ge(wg_ready, 1)

                def step(G, r, j):
                    if fills(G, 0):
                        wait(pe, yT_lo, 2 * (G - 1))
                        pe.wait_ge(y_done, 4 * G + 4)
                        for k in range(DC):
                            for i in range(4):
                                last = nc.tensor.transpose(ps_y[2 * r + k][:, i * P:(i + 1) * P],
                                                           y[r][:, i, k * P:(k + 1) * P], c.ident[:, :])
                            last.then_inc(yT_done, 1)
                    if fills(G, 2):
                        pe.wait_ge(lt_copied, G - 1)
                        wait(pe, l_copied, G - 2)
                        for i in range(4):
                            last = nc.tensor.transpose(ps_l[r][:, i, :], lgT[r][:, i * P:(i + 1) * P],
                                                       c.ident[:, :])
                        last.then_inc(l_done, 1)
                    if fills(G, 1):
                        pe.wait_ge(yT_lo, 2 * G)
                        wait(pe, lt_copied, G - 2)
                        products(nc, ps_lt[1 - r][:, :], [
                            (wg[0][:, k, :], wg[1][:, k, :], yT[1 - r][0][:, k, :], yT[1 - r][1][:, k, :])
                            for k in range(DC)]).then_inc(lt_done, 1)

                pipeline(pe, step)

            @block.scalar
            def _(act):
                act.wait_ge(root_ready, 1)
                nc.scalar.activation(rstd2[:, :], rstd2[:, :], ACT.Sqrt).then_inc(root_done, 1)
                act.wait_ge(wg_zero, 2)
                act.wait_ge(wg_in, 16)
                nc.scalar.activation(wg[0][:, :, 0:E], wg_raw[:, :, :], ACT.Copy).then_inc(wg_hi_done, 1)

                def step(G, r, j):
                    if fills(G, 0):
                        wait(act, lt_done, G - 1)
                        for k in range(DC):
                            act.wait_ge(yT_done, 2 * G + k + 1)
                            nc.scalar.activation(yT[r][0][:, k, :], ps_y[2 * r + k][:, :], ACT.Copy).then_inc(yT_hi, 1)
                    if fills(G, 1):
                        act.wait_ge(lt_done, G)
                        wait(act, l_done, G - 2)
                        nc.scalar.activation(lgT[1 - r][:, :], ps_lt[1 - r][:, :], ACT.Copy).then_inc(lt_copied, 1)

                pipeline(act, step)

            @block.vector
            def _(v):
                rstd_steps(nc, v, stats, mean2[:, :], rstd2[:, :], var2[:, :], chain2, root_ready, root_done)
                nc.vector.scalar_tensor_tensor(shift2[:, :], mean2[:, :], -1.0, rstd2[:, :], ALU.mult,
                                               ALU.mult).then_inc(ln_ready, 1)
                v.wait_ge(wg_hi_done, 1)
                nc.vector.tensor_tensor(wg[1][:, :, 0:E], wg_raw[:, :, :], f32(wg[0][:, :, 0:E]),
                                        ALU.subtract).then_inc(wg_ready, 1)
                v.wait_ge(ln_ready, 1)

                def step(G, r, j):
                    if fills(G, 0):
                        v.wait_ge(x1_loaded[r], 16 * (j + 1))
                        wait(v, y_stored[r], 16 * j)
                        wait(v, yT_done, 2 * (G - 1))
                        for i in range(4):
                            nc.vector.tensor_scalar(y[r][:, i, :], x1_in[r][:, i, :],
                                                    rstd2[:, bass.ds(4 * G + i, 1)], shift2[:, bass.ds(4 * G + i, 1)],
                                                    ALU.mult, ALU.add).then_inc(y_done, 1)
                    if fills(G, 2):
                        v.wait_ge(l_done, G - 1)
                        nc.vector.tensor_copy(
                            c.logits[:, bass.ds((G - 2) * 4 * E, 4 * E)].rearrange("p (i e) -> p i e", e=E),
                            ps_l[r][:, :, 0:E]).then_inc(l_copied, 1)
                    if fills(G, 0):
                        for k in range(DC):
                            v.wait_ge(yT_hi, 2 * G + k + 1)
                            nc.vector.tensor_tensor(yT[r][1][:, k, :], ps_y[2 * r + k][:, :],
                                                    f32(yT[r][0][:, k, :]), ALU.subtract).then_inc(yT_lo, 1)

                pipeline(v, step)


def route(nc, c):
    W = TILES * E
    with ExitStack() as ctx:
        sb, ps, sem = allocator(nc, ctx)
        rank_row = sb("rank_row", [P, E])
        token_no = sb("token_no", [P, TILES])
        iota_lo, iota_hi = sb("iota_lo", [P, P]), sb("iota_hi", [P, SLOT_TILES])
        before, ones = sb("before", [P, P], BF16), sb("ones", [P, P], BF16)
        top = [sb(f"top{k}", [P, TILES]) for k in range(2)]
        first = sb("first", [P, TILES])
        mask = [sb(f"mask{k}", [P, W]) for k in range(2)]
        work, rest = sb("work", [P, W]), sb("rest", [P, W])
        both = sb("both", [P, W], BF16)
        total = sb("total", [P, TILES])
        zeros = sb("zeros_t", [P, TILES])
        counts, upto, place = sb("counts", [P, W]), sb("upto", [P, W]), sb("place", [P, W])
        padded_i, padded = sb("padded_i", [P, E], I32), sb("padded", [P, E])
        ends, offsets = sb("ends", [P, E]), sb("offsets", [P, E])
        slot = [sb(f"slot{k}", [P, TILES]) for k in range(2)]
        part_i = sb("part_i", [P, TILES], I32)
        slot_hi = [sb(f"slot_hi{k}", [P, TILES]) for k in range(2)]
        slot_lo = [sb(f"slot_lo{k}", [P, TILES]) for k in range(2)]
        pair_ends = sb("pair_ends", [1, E])
        passed, pair_sum = sb("passed", [1, PAIRS * E]), sb("pair_sum", [1, PAIRS])
        OH = 8
        hot_lo = [sb(f"hot_lo{i}", [P, P]) for i in range(OH)]
        hot_hi = [sb(f"hot_hi{i}", [P, SLOT_TILES]) for i in range(OH)]
        ps_before = [ps(f"ps_before{i}", [P, 512]) for i in range(2)]
        ps_count = [ps(f"ps_count{i}", [P, 512]) for i in range(2)]
        ps_inv = ps("ps_inv", [P, 512])

        consts, chain, gap_ready, exp_done = sem("consts"), sem("chain"), sem("gap_ready"), sem("exp_done_r")
        both_ready, counted = sem("both_ready"), sem("counted")
        hot_lo_ready, hot_hi_ready, hot_used = sem("hot_lo_ready"), sem("hot_hi_ready"), sem("hot_used")
        slots_ready, split_hi, split_lo = sem("slots_ready"), sem("w_split_hi"), sem("w_split_lo")

        def te(t):
            return t[:, :].rearrange("p (t e) -> p t e", e=E)

        def per_tile(t):
            return t[:, :].unsqueeze(2).broadcast_to((P, TILES, E))

        def per_expert(t):
            return t[:, :].unsqueeze(1).broadcast_to((P, TILES, E))

        halves = [slice(0, 512), slice(512, 1024)]

        with nc.Block() as block:

            @block.gpsimd
            def _(pool):
                steps = [0]

                def link(ins):
                    steps[0] += 1
                    ins.then_inc(consts, 1)
                    pool.wait_ge(consts, steps[0])

                g = nc.gpsimd
                exact = dict(allow_small_or_imprecise_dtypes=True)
                link(g.iota(rank_row[:, :], [[-1, E]], base=E, channel_multiplier=0, **exact))
                link(g.iota(token_no[:, :], [[P, TILES]], base=0, channel_multiplier=1, **exact))
                link(g.iota(iota_lo[:, :], [[1, P]], base=0, channel_multiplier=0, **exact))
                link(g.iota(iota_hi[:, :], [[1, SLOT_TILES]], base=0, channel_multiplier=0, **exact))
                link(g.memset(ones[:, :], 1.0))
                link(g.memset(zeros[:, :], 0.0))
                link(g.affine_select(out=before[:, :], in_=ones[:, :], compare_op=ALU.is_gt, fill=0.0, base=0,
                                     pattern=[[1, P]], channel_multiplier=-1))
                for n in range(4):
                    e = slice(4 * n, 4 * n + 4)
                    pool.wait_ge(split_hi, 2 * n + 2)
                    g.tensor_tensor(c.w1_lo[:, e, :, :], c.w1_raw[:, e, :, :], f32(c.w1_hi[:, e, :, :]),
                                    ALU.subtract).then_inc(split_lo, 1)
                    g.tensor_tensor(c.w2_lo[:, e, :], c.w2_raw[:, e, :], f32(c.w2_hi[:, e, :]),
                                    ALU.subtract).then_inc(split_lo, 1)

            @block.scalar
            def _(act):
                def high(n):
                    e = slice(4 * n, 4 * n + 4)
                    nc.scalar.activation(c.w1_hi[:, e, :, :], c.w1_raw[:, e, :, :], ACT.Copy).then_inc(split_hi, 1)
                    nc.scalar.activation(c.w2_hi[:, e, :], c.w2_raw[:, e, :], ACT.Copy).then_inc(split_hi, 1)

                high(0)
                act.wait_ge(gap_ready, 1)
                nc.scalar.activation(te(work), te(work), ACT.Exp).then_inc(exp_done, 1)
                act.wait_ge(gap_ready, 2)
                nc.scalar.activation(c.weight[1][:, :], c.weight[1][:, :], ACT.Exp).then_inc(exp_done, 1)
                for n in range(1, 4):
                    high(n)

            @block.tensor
            def _(pe):
                pe.wait_ge(consts, 7)
                pe.wait_ge(both_ready, 1)
                for i in range(2):
                    nc.tensor.matmul(ps_before[i][:, :], before[:, :], both[:, halves[i]],
                                     start=True, stop=True).then_inc(counted, 1)
                    nc.tensor.matmul(ps_count[i][:, :], ones[:, :], both[:, halves[i]],
                                     start=True, stop=True).then_inc(counted, 1)

                def add_tile(j, u, first, last):
                    pe.wait_ge(hot_lo_ready, OH * j + u + 1)
                    pe.wait_ge(hot_hi_ready, OH * j + u + 1)
                    nc.tensor.matmul(ps_inv[:, 0:SLOT_TILES], hot_lo[u][:, :], hot_hi[u][:, :],
                                     start=first, stop=last, skip_group_check=True).then_inc(hot_used, 1)

                rounds = 2 * TILES // OH
                for u in range(OH):
                    add_tile(0, u, u == 0, False)
                with pe.Fori(1, rounds - 1) as j:
                    for u in range(OH):
                        add_tile(j, u, False, False)
                for u in range(OH):
                    add_tile(rounds - 1, u, False, u == OH - 1)

            @block.vector
            def _(v):
                steps = [0]

                def link(ins):
                    steps[0] += 1
                    ins.then_inc(chain, 1)
                    v.wait_ge(chain, steps[0])

                V = nc.vector
                v.wait_ge(consts, 7)
                logits, source = te(c.logits), te(c.logits)
                for k in range(2):
                    link(V.tensor_reduce(top[k][:, :], source, AX.X, ALU.max))
                    link(V.tensor_tensor(te(mask[k]), source, per_tile(top[k]), ALU.is_equal))
                    link(V.tensor_tensor(te(mask[k]), te(mask[k]), per_expert(rank_row), ALU.mult))
                    link(V.tensor_reduce(first[:, :], te(mask[k]), AX.X, ALU.max))
                    link(V.tensor_tensor(te(mask[k]), te(mask[k]), per_tile(first), ALU.is_equal))
                    if k == 0:
                        link(V.scalar_tensor_tensor(rest[:, :], mask[0][:, :], -3e38, c.logits[:, :],
                                                    ALU.mult, ALU.add))
                        source = te(rest)
                link(V.tensor_tensor(both[:, :], mask[0][:, :], mask[1][:, :], ALU.add))
                V.tensor_tensor(te(work), logits, per_tile(top[0]), ALU.subtract).then_inc(gap_ready, 1)
                V.tensor_tensor(c.weight[1][:, :], top[1][:, :], top[0][:, :], ALU.subtract).then_inc(gap_ready, 1)
                V.memset(total[:, :], 0.0).then_inc(both_ready, 1)

                v.wait_ge(counted, 4)
                for i in range(2):
                    link(V.tensor_copy(counts[:, halves[i]], ps_count[i][:, :]))
                for e in range(E):
                    ins = V.tensor_tensor_scan(te(upto)[:, :, e], te(counts)[:, :, e], zeros[:, :], 0.0,
                                               ALU.add, ALU.add)
                link(ins)
                link(V.tensor_scalar(padded_i[:, :], te(upto)[:, TILES - 1, :], float(2 * P - 1), None, ALU.add))
                link(V.tensor_scalar(padded_i[:, :], padded_i[:, :], 8, 8, ALU.logical_shift_right,
                                     ALU.logical_shift_left))
                link(V.tensor_copy(padded[:, :], padded_i[:, :]))
                link(V.tensor_tensor_scan(ends[:, :], padded[:, :], zeros[:, 0:E], 0.0, ALU.add, ALU.add))
                link(V.tensor_tensor(offsets[:, :], ends[:, :], padded[:, :], ALU.subtract))
                link(V.tensor_tensor(te(place), te(upto), te(counts), ALU.subtract))
                link(V.tensor_tensor(te(place), te(place), per_expert(offsets), ALU.add))
                for i in range(2):
                    link(V.tensor_tensor(place[:, halves[i]], ps_before[i][:, :], place[:, halves[i]], ALU.add))
                for k in range(2):
                    link(V.tensor_tensor(mask[k][:, :], mask[k][:, :], place[:, :], ALU.mult))
                    link(V.tensor_reduce(slot[k][:, :], te(mask[k]), AX.X, ALU.add))
                    link(V.tensor_copy(c.slot_i[k][:, :], slot[k][:, :]))
                    link(V.tensor_scalar(part_i[:, :], c.slot_i[k][:, :], 7, None, ALU.logical_shift_right))
                    link(V.tensor_copy(slot_hi[k][:, :], part_i[:, :]))
                    link(V.scalar_tensor_tensor(slot_lo[k][:, :], slot_hi[k][:, :], -float(P), slot[k][:, :],
                                                ALU.mult, ALU.add))

                def one_hots(j, u):
                    t, k = bass.ds(j * (OH // 2) + u // 2, 1), u % 2
                    wait(v, hot_used, OH * (j - 1) + u + 1)
                    V.tensor_scalar(hot_lo[u][:, :], iota_lo[:, :], slot_lo[k][:, t], None,
                                    ALU.is_equal).then_inc(hot_lo_ready, 1)
                    V.tensor_scalar(hot_hi[u][:, :], iota_hi[:, :], slot_hi[k][:, t], token_no[:, t],
                                    ALU.is_equal, ALU.mult).then_inc(hot_hi_ready, 1)

                for u in range(OH):
                    one_hots(0, u)
                with v.Fori(1, 2 * TILES // OH) as j:
                    for u in range(OH):
                        one_hots(j, u)

                v.wait_ge(exp_done, 2)
                link(V.tensor_reduce(total[:, :], te(work), AX.X, ALU.add))
                link(V.reciprocal(total[:, :], total[:, :]))
                link(V.tensor_scalar(c.weight[0][:, :], total[:, :], c.tanh_g[:, 1:2], None, ALU.mult))
                link(V.tensor_tensor(c.weight[1][:, :], c.weight[1][:, :], c.weight[0][:, :], ALU.mult))

                link(V.tensor_scalar(pair_ends[:, :], ends[0:1, :], 1.0 / (2 * P), None, ALU.mult))
                by_pair = passed[:, :].rearrange("p (q e) -> p q e", e=E)
                link(V.tensor_tensor(by_pair, iota_hi[0:1, 0:PAIRS].unsqueeze(2).broadcast_to((1, PAIRS, E)),
                                     pair_ends[:, :].unsqueeze(1).broadcast_to((1, PAIRS, E)), ALU.is_ge))
                link(V.tensor_reduce(pair_sum[:, :], by_pair, AX.X, ALU.add))
                link(V.tensor_scalar(c.pair_expert[:, :], pair_sum[:, :], float(E - 1), None, ALU.min))

                v.wait_ge(hot_used, 2 * TILES)
                link(V.tensor_copy(c.slot_token[:, :], ps_inv[:, 0:SLOT_TILES]))
                v.wait_ge(split_lo, 8)


def experts(nc, c):
    U = 8
    ROUNDS = PAIRS // U
    NB = 4
    with ExitStack() as ctx:
        sb, ps, sem = allocator(nc, ctx)
        index = [sb(f"index{i}", [P, 2 * NB], I32) for i in range(2)]
        rows = [sb(f"rows{i}", [P, 2, D]) for i in range(NB)]
        yT = [[sb(f"eyT{i}_{s}", [P, DC, 2 * P], F32R) for s in ("hi", "lo")] for i in range(2)]
        silu = [sb(f"silu{i}", [P, 2, HID]) for i in range(2)]
        a = [sb(f"a{i}", [P, 2, HID]) for i in range(2)]
        aT = [[sb(f"aT{i}_{s}", [P, 2, P], F32R) for s in ("hi", "lo")] for i in range(2)]
        z = [sb(f"z{i}", [P, 2, D]) for i in range(NB)]
        ps_y = [ps(f"ps_ey{i}", [P, DC, 2 * P]) for i in range(2)]
        ps_h = [ps(f"ps_h{i}", [P, 2, 2 * HID]) for i in range(2)]
        ps_a = [ps(f"ps_a{i}", [P, 2 * DC, P]) for i in range(2)]
        ps_z = [ps(f"ps_z{i}", [P, 2, D]) for i in range(2)]

        index_ready, go = sem("index_ready"), sem("gather_go")
        gathered = [sem(f"gathered{i}") for i in range(NB)]
        z_stored = [sem(f"z_stored{i}") for i in range(NB)]
        yT_done, yT_hi, yT_lo = sem("eyT_done"), sem("eyT_hi"), sem("eyT_lo")
        h_done, silu_done, a_done = sem("h_done"), sem("silu_done"), sem("a_done")
        aT_done, aT_hi, aT_lo, z_done, z_copied = (
            sem("aT_done"), sem("aT_hi"), sem("aT_lo"), sem("z_done"), sem("z_copied"))

        def pairs_of(eng, step, lag=0):
            for u in range(U):
                step(u, u, 0)
            with eng.Fori(1, ROUNDS) as j:
                for u in range(U):
                    step(U * j + u, u, j)
            for u in range(lag):
                step(PAIRS + u, u, ROUNDS)

        def exists(q):
            return not isinstance(q, int) or 0 <= q < PAIRS

        with nc.Block() as block:

            @block.gpsimd
            def _(pool):
                def step(q, u, j):
                    if u % NB == 0:
                        pool.wait_ge(index_ready, 2 * j + u // NB + 1)
                    wait(pool, yT_done, q - NB + 1)
                    pool.sem_inc(go, 1)
                    for i in range(2):
                        column = 2 * (u % NB) + i
                        pool.indirect_dma_start(rows[u % NB][:, i, :], None, c.y, bass.IndirectOffsetOnAxis(
                            index[u // NB][:, column:column + 1], 0)).then_inc(gathered[u % NB], 16)

                pairs_of(pool, step)

            @block.sync
            def _(sp):
                def step(q, u, j):
                    sp.wait_ge(z_copied, q + 1)
                    sp.dma_start(c.z[bass.ds(q * 2 * P, 2 * P), :].rearrange("(i p) d -> p i d", p=P),
                                 z[u % NB][:, :, :]).then_inc(z_stored[u % NB], 16)

                pairs_of(sp, step)
                for i in range(NB):
                    sp.wait_ge(z_stored[i], 16 * (PAIRS // NB))

            @block.tensor
            def _(pe):
                def transpose_rows(q, u, j):
                    pe.wait_ge(gathered[u % NB], 32 * (2 * j + u // NB + 1))
                    for i in range(2):
                        for k in range(DC):
                            last = nc.tensor.transpose(ps_y[u % 2][:, k, i * P:(i + 1) * P],
                                                       rows[u % NB][:, i, k * P:(k + 1) * P], c.ident[:, :])
                    last.then_inc(yT_done, 1)

                def hidden(q, p, w1_at):
                    pe.wait_ge(yT_lo, q + 1)
                    weights = [(c.w1_hi_flat[:, bass.ds(w1_at + k * D, D)], c.w1_lo_flat[:, bass.ds(w1_at + k * D, D)])
                               for k in range(DC)]
                    for i in range(2):
                        token = slice(i * P, (i + 1) * P)
                        last = products(nc, ps_h[p][:, i, :], [
                            (yT[p][0][:, k, token], yT[p][1][:, k, token], *weights[k]) for k in range(DC)])
                    last.then_inc(h_done, 1)

                def transpose_a(q, p):
                    pe.wait_ge(a_done, q + 1)
                    for i in range(2):
                        last = nc.tensor.transpose(ps_a[p][:, i, :], a[p][:, i, :], c.ident[:, :])
                    last.then_inc(aT_done, 1)

                def down(q, p, w2_at):
                    pe.wait_ge(aT_lo, q + 1)
                    weights = c.w2_hi_flat[:, bass.ds(w2_at, D)], c.w2_lo_flat[:, bass.ds(w2_at, D)]
                    for i in range(2):
                        last = products(nc, ps_z[p][:, i, :], [(aT[p][0][:, i, :], aT[p][1][:, i, :], *weights)])
                    last.then_inc(z_done, 1)

                known = {}

                def expert_of(q, u):
                    if u not in known:
                        known[u] = pe.value_load(c.pair_expert[0:1, bass.ds(q, 1)], min_val=0, max_val=E - 1)
                    return known[u]

                def step(s, u, j):
                    if u == 0:
                        known.clear()
                    if exists(s):
                        transpose_rows(s, u, j)
                    if exists(s - 1):
                        hidden(s - 1, (u - 1) % 2, expert_of(s - 1, u - 1) * (DC * D))
                    if exists(s - 2):
                        transpose_a(s - 2, u % 2)
                    if exists(s - 3):
                        down(s - 3, (u - 3) % 2, expert_of(s - 3, u - 3) * D)

                pairs_of(pe, step, lag=3)

            @block.scalar
            def _(act):
                def step(s, u, j):
                    if exists(s):
                        p = u % 2
                        act.wait_ge(yT_done, s + 1)
                        wait(act, h_done, s - 1)
                        nc.scalar.activation(yT[p][0][:, :, :], ps_y[p][:, :, :], ACT.Copy).then_inc(yT_hi, 1)
                    if exists(s - 1):
                        q, p = s - 1, (u - 1) % 2
                        act.wait_ge(h_done, q + 1)
                        wait(act, a_done, q - 1)
                        nc.scalar.activation(silu[p][:, :, :], ps_h[p][:, :, HID:], ACT.Silu).then_inc(silu_done, 1)
                    if exists(s - 2):
                        q, p = s - 2, u % 2
                        act.wait_ge(aT_done, q + 1)
                        wait(act, z_done, q - 1)
                        nc.scalar.activation(aT[p][0][:, :, :], ps_a[p][:, 0:2, :], ACT.Copy).then_inc(aT_hi, 1)

                pairs_of(act, step, lag=2)

            @block.vector
            def _(v):
                def indices(first_tile, half):
                    nc.vector.tensor_copy(index[half][:, :],
                                          c.slot_token[:, bass.ds(first_tile, 2 * NB)]).then_inc(index_ready, 1)

                indices(0, 0)
                indices(2 * NB, 1)

                def step(s, u, j):
                    if exists(s):
                        p = u % 2
                        v.wait_ge(yT_hi, s + 1)
                        nc.vector.tensor_tensor(yT[p][1][:, :, :], ps_y[p][:, :, :], f32(yT[p][0][:, :, :]),
                                                ALU.subtract).then_inc(yT_lo, 1)
                    if exists(s - 1):
                        q, p = s - 1, (u - 1) % 2
                        v.wait_ge(silu_done, q + 1)
                        wait(v, aT_done, q - 1)
                        nc.vector.tensor_tensor(a[p][:, :, :], ps_h[p][:, :, 0:HID], silu[p][:, :, :],
                                                ALU.mult).then_inc(a_done, 1)
                    if exists(s - 2):
                        q, p = s - 2, u % 2
                        v.wait_ge(aT_hi, q + 1)
                        nc.vector.tensor_tensor(aT[p][1][:, :, :], ps_a[p][:, 0:2, :], f32(aT[p][0][:, :, :]),
                                                ALU.subtract).then_inc(aT_lo, 1)
                    if exists(s - 3):
                        p, b = (u - 3) % 2, (u - 3) % NB
                        v.wait_ge(z_done, s - 2)
                        wait(v, z_stored[b], 16 * (2 * j + (u - 3) // NB))
                        nc.vector.tensor_copy(z[b][:, :, :], ps_z[p][:, :, :]).then_inc(z_copied, 1)
                    if u % NB == NB - 1 and exists(s) and not (isinstance(j, int) and j == ROUNDS - 1):
                        v.wait_ge(gathered[NB - 1], 32 * (2 * j + u // NB + 1))
                        indices(2 * (U * (j + 1) + u - (NB - 1)), u // NB)

                for u in range(U):
                    step(u, u, 0)
                with v.Fori(1, ROUNDS - 1) as j:
                    for u in range(U):
                        step(U * j + u, u, j)
                for s in range(U * (ROUNDS - 1), PAIRS + 3):
                    step(s, s % U, s // U)


def combine(nc, c):
    STEPS = TILES // 4
    with ExitStack() as ctx:
        sb, ps, sem = allocator(nc, ctx)
        ws1_raw, ws2_raw = sb("ws1_raw", [P, DC, 2 * HS]), sb("ws2_raw", [P, 2, D])
        ws1 = [sb(f"ws1_{s}", [P, DC, 2 * HS], F32R) for s in ("hi", "lo")]
        ws2 = [sb(f"ws2_{s}", [P, 2, D], F32R) for s in ("hi", "lo")]
        index = [sb(f"zindex{i}", [P, 2, 4], I32) for i in range(2)]
        zg = [sb(f"zg{i}", [P, 8, D]) for i in range(2)]
        y = [sb(f"cy{i}", [P, 4, D]) for i in range(2)]
        x1 = [sb(f"cx{i}", [P, 4, D]) for i in range(2)]
        o = [sb(f"o{i}", [P, 4, D]) for i in range(2)]
        yT = [[sb(f"cyT{i}_{s}", [P, DC, 512], F32R) for s in ("hi", "lo")] for i in range(2)]
        silu = [sb(f"csilu{i}", [P, 512]) for i in range(2)]
        a = [sb(f"ca{i}", [P, 512]) for i in range(2)]
        aT = [[sb(f"caT{i}_{s}", [P, 2, 512], F32R) for s in ("hi", "lo")] for i in range(2)]
        ps_y = [ps(f"ps_cy{i}", [P, 512]) for i in range(2)]
        ps_g = [ps(f"ps_g{i}", [P, 512]) for i in range(2)]
        ps_u = [ps(f"ps_u{i}", [P, 512]) for i in range(2)]
        ps_o = [ps(f"ps_co{i}", [P, 2, D]) for i in range(2)]

        ws_in, ws_scaled, ws_hi, ws_ready = sem("ws_in"), sem("ws_scaled"), sem("ws_hi"), sem("ws_ready")
        y_in = [sem(f"cy_in{i}") for i in range(2)]
        x1_in = [sem(f"cx_in{i}") for i in range(2)]
        gathered = [sem(f"zgathered{i}") for i in range(2)]
        out_stored = [sem(f"out_stored{i}") for i in range(2)]
        index_ready, go = sem("zindex_ready"), sem("zgather_go")
        yT_done, yT_hi, yT_lo = sem("cyT_done"), sem("cyT_hi"), sem("cyT_lo")
        g_done, u_done, silu_done, a_done = sem("g_done"), sem("u_done"), sem("csilu_done"), sem("ca_done")
        aT_hi, aT_lo, o_done, added, fin1, fin2 = (
            sem("caT_hi"), sem("caT_lo"), sem("co_done"), sem("added"), sem("fin1"), sem("fin2"))

        def pipeline(eng, step):
            for G in range(4):
                step(G, G % 2, G // 2)
            with eng.Fori(2, STEPS // 2 - 1) as j:
                for r in range(2):
                    step(2 * j + r, r, j)
            for G in range(STEPS - 2, STEPS + 2):
                step(G, G % 2, G // 2)

        def exists(G):
            return not isinstance(G, int) or 0 <= G < STEPS

        with nc.Block() as block:

            @block.sync
            def _(sp):
                def rows(dram, G):
                    return dram[bass.ds(G * 512, 512), :].rearrange("(i p) d -> p i d", p=P)

                for G in range(2):
                    sp.dma_start(y[G][:, :, :], rows(c.y, G)).then_inc(y_in[G], 16)
                sp.dma_start(ws1_raw[:, :, :], c.Ws1.rearrange("(k p) h -> p k h", p=P)).then_inc(ws_in, 16)
                sp.dma_start(ws2_raw[:, :, :], c.Ws2.rearrange("(k p) h -> p k h", p=P)).then_inc(ws_in, 16)

                def step(G, r, j):
                    if exists(G + 2):
                        sp.wait_ge(yT_done, 2 * G + 2)
                        sp.dma_start(y[r][:, :, :], rows(c.y, G + 2)).then_inc(y_in[r], 16)
                    if exists(G):
                        wait(sp, added, 2 * (G - 1))
                        sp.dma_start(x1[r][:, :, :], rows(c.x1, G)).then_inc(x1_in[r], 16)
                    if exists(G - 2):
                        sp.wait_ge(fin2, 4 * (G - 1))
                        sp.dma_start(rows(c.out, G - 2), o[r][:, :, :]).then_inc(out_stored[r], 16)

                pipeline(sp, step)
                for r in range(2):
                    sp.wait_ge(out_stored[r], 16 * (STEPS // 2))

            @block.gpsimd
            def _(pool):
                def step(G, r, j):
                    if not exists(G):
                        return
                    pool.wait_ge(index_ready, 2 * G + 2)
                    wait(pool, fin2, 4 * (G - 1))
                    pool.sem_inc(go, 1)
                    for i in range(4):
                        for k in range(2):
                            pool.indirect_dma_start(
                                zg[r][:, 2 * i + k, :], None, c.z,
                                bass.IndirectOffsetOnAxis(index[r][:, k, i:i + 1], 0)).then_inc(gathered[r], 16)

                pipeline(pool, step)

            @block.tensor
            def _(pe):
                def transpose_y(G, p, j):
                    pe.wait_ge(y_in[p], 16 * (j + 1))
                    for k in range(DC):
                        for i in range(4):
                            last = nc.tensor.transpose(ps_y[k][:, i * P:(i + 1) * P], y[p][:, i, k * P:(k + 1) * P],
                                                       c.ident[:, :])
                        last.then_inc(yT_done, 1)

                def hidden(G, r):
                    for n in range(2):
                        wait(pe, a_done, 2 * G + n - 1)
                        for bank, first, done in ((ps_g[n], HS + n * P, g_done), (ps_u[n], n * P, u_done)):
                            products(nc, bank[:, :], [
                                (ws1[0][:, k, first:first + P], ws1[1][:, k, first:first + P],
                                 yT[r][0][:, k, :], yT[r][1][:, k, :]) for k in range(DC)]).then_inc(done, 1)

                def down(G, p):
                    pe.wait_ge(aT_lo, 2 * G + 2)
                    for b in range(2):
                        wait(pe, added, 2 * (G - 1) + b + 1)
                        for i in (2 * b, 2 * b + 1):
                            last = products(nc, ps_o[b][:, i % 2, :], [
                                (aT[p][0][:, n, i * P:(i + 1) * P], aT[p][1][:, n, i * P:(i + 1) * P],
                                 ws2[0][:, n, :], ws2[1][:, n, :]) for n in range(2)])
                        last.then_inc(o_done, 1)

                transpose_y(0, 0, 0)
                pe.wait_ge(ws_ready, 2)

                def step(G, r, j):
                    if exists(G):
                        pe.wait_ge(yT_lo, 2 * G + 2)
                    if exists(G + 1):
                        transpose_y(G + 1, 1 - r, j + r)
                    if exists(G):
                        hidden(G, r)
                    if exists(G - 1):
                        down(G - 1, 1 - r)

                pipeline(pe, step)

            @block.scalar
            def _(act):
                def high_yT(G, p):
                    wait(act, u_done, 2 * (G - 1))
                    for k in range(DC):
                        act.wait_ge(yT_done, 2 * G + k + 1)
                        nc.scalar.activation(yT[p][0][:, k, :], ps_y[k][:, :], ACT.Copy).then_inc(yT_hi, 1)

                def high_aT(G, r, n):
                    act.wait_ge(a_done, 2 * G + n + 1)
                    wait(act, o_done, 2 * (G - 1))
                    nc.scalar.activation(aT[r][0][:, n, :], a[n][:, :], ACT.Copy).then_inc(aT_hi, 1)

                high_yT(0, 0)
                act.wait_ge(ws_in, 32)
                nc.scalar.activation(ws1[0][:, :, :], ws1_raw[:, :, :], ACT.Copy).then_inc(ws_hi, 1)
                act.wait_ge(ws_scaled, 1)
                nc.scalar.activation(ws2[0][:, :, :], ws2_raw[:, :, :], ACT.Copy).then_inc(ws_hi, 1)

                def step(G, r, j):
                    if exists(G + 1):
                        high_yT(G + 1, 1 - r)
                    if exists(G):
                        for n in range(2):
                            act.wait_ge(g_done, 2 * G + n + 1)
                            wait(act, a_done, 2 * G + n - 1)
                            nc.scalar.activation(silu[n][:, :], ps_g[n][:, :], ACT.Silu).then_inc(silu_done, 1)
                            high_aT(G, r, n)

                pipeline(act, step)

            @block.vector
            def _(v):
                V = nc.vector

                def indices(G, r):
                    for k in range(2):
                        V.tensor_copy(index[r][:, k, :],
                                      c.slot_i[k][:, bass.ds(4 * G, 4)]).then_inc(index_ready, 1)

                def low_yT(G, p):
                    for k in range(DC):
                        v.wait_ge(yT_hi, 2 * G + k + 1)
                        V.tensor_tensor(yT[p][1][:, k, :], ps_y[k][:, :], f32(yT[p][0][:, k, :]),
                                        ALU.subtract).then_inc(yT_lo, 1)

                def multiply(G, n):
                    v.wait_ge(silu_done, 2 * G + n + 1)
                    v.wait_ge(u_done, 2 * G + n + 1)
                    wait(v, aT_lo, 2 * G + n - 1)
                    V.tensor_tensor(a[n][:, :], ps_u[n][:, :], silu[n][:, :], ALU.mult).then_inc(a_done, 1)

                def low_aT(G, r, n):
                    v.wait_ge(aT_hi, 2 * G + n + 1)
                    V.tensor_tensor(aT[r][1][:, n, :], a[n][:, :], f32(aT[r][0][:, n, :]),
                                    ALU.subtract).then_inc(aT_lo, 1)

                def add_x1(G, p, j):
                    v.wait_ge(x1_in[p], 16 * (j + 1))
                    wait(v, out_stored[p], 16 * j)
                    for b in range(2):
                        v.wait_ge(o_done, 2 * G + b + 1)
                        V.tensor_tensor(o[p][:, 2 * b:2 * b + 2, :], ps_o[b][:, :, :], x1[p][:, 2 * b:2 * b + 2, :],
                                        ALU.add).then_inc(added, 1)

                def add_routed(G, r, k):
                    done = (fin1, fin2)[k]
                    for i in range(4):
                        if k:
                            v.wait_ge(fin1, 4 * G + i + 1)
                        V.scalar_tensor_tensor(o[r][:, i, :], zg[r][:, 2 * i + k, :],
                                               c.weight[k][:, bass.ds(4 * G + i, 1)], o[r][:, i, :],
                                               ALU.mult, ALU.add).then_inc(done, 1)

                indices(0, 0)
                indices(1, 1)
                low_yT(0, 0)
                v.wait_ge(ws_in, 32)
                V.tensor_scalar(ws2_raw[:, :, :], ws2_raw[:, :, :], c.tanh_g[:, 1:2], None,
                                ALU.mult).then_inc(ws_scaled, 1)
                v.wait_ge(ws_hi, 2)
                V.tensor_tensor(ws1[1][:, :, :], ws1_raw[:, :, :], f32(ws1[0][:, :, :]),
                                ALU.subtract).then_inc(ws_ready, 1)
                V.tensor_tensor(ws2[1][:, :, :], ws2_raw[:, :, :], f32(ws2[0][:, :, :]),
                                ALU.subtract).then_inc(ws_ready, 1)

                def step(G, r, j):
                    if exists(G + 1):
                        low_yT(G + 1, 1 - r)
                    if exists(G - 2):
                        v.wait_ge(gathered[r], 128 * j)
                        v.wait_ge(added, 2 * (G - 1))
                        add_routed(G - 2, r, 0)
                        if exists(G):
                            indices(G, r)
                    if exists(G):
                        multiply(G, 0)
                    if exists(G - 2):
                        add_routed(G - 2, r, 1)
                    if exists(G):
                        low_aT(G, r, 0)
                        multiply(G, 1)
                    if exists(G - 1):
                        add_x1(G - 1, 1 - r, j + r - 1)
                    if exists(G):
                        low_aT(G, r, 1)

                pipeline(v, step)


def flamingo(nc, x, xT, ctxT, g_xattn, g_ffn, WqT, WkT, Wv, Wout, bout, WgT, W1, W2, Ws1, Ws2, out, upto=9):
    c = Common()
    c.x, c.xT, c.ctxT, c.g_xattn, c.g_ffn = x, xT, ctxT, g_xattn, g_ffn
    c.WqT, c.WkT, c.Wv, c.Wout, c.bout = WqT, WkT, Wv, Wout, bout
    c.WgT, c.W1, c.W2, c.Ws1, c.Ws2, c.out = WgT, W1, W2, Ws1, Ws2, out
    c.x1 = nc.dram_tensor("x1_scratch", (T, D), F32, kind="Internal").ap()
    with ExitStack() as ctx:
        sb, _, _ = allocator(nc, ctx)
        c.ident = sb("ident", [P, P])
        c.tanh_g = sb("tanh_g", [P, 2])
        c.stats2 = sb("stats2", [P, TILES * 6])
        with ExitStack() as attention:
            sb, _, _ = allocator(nc, attention)
            c.rstd1 = sb("rstd1", [P, TILES])
            c.bias = sb("bias", [P, D])
            c.wqk_hi, c.wqk_lo = (sb(f"wqk_{s}", [P, 2, H, D], F32R) for s in ("hi", "lo"))
            c.wv_hi, c.wv_lo = (sb(f"wv_{s}", [P, 2, INNER], F32R) for s in ("hi", "lo"))
            c.wo_hi, c.wo_lo = (sb(f"wo_{s}", [P, 4, D], F32R) for s in ("hi", "lo"))
            prepare(nc, c)
            if upto >= 1:
                attend(nc, c)
        if upto < 2:
            return
        sb, _, _ = allocator(nc, ctx)
        c.y = nc.dram_tensor("y_scratch", (T, D), F32, kind="Internal").ap()
        c.z = nc.dram_tensor("z_scratch", (SLOT_TILES * P, D), F32, kind="Internal").ap()
        c.logits = sb("logits", [P, TILES * E])
        c.weight = [sb(f"weight{k}", [P, TILES]) for k in range(2)]
        c.slot_i = [sb(f"slot_i{k}", [P, TILES], I32) for k in range(2)]
        c.slot_token = sb("slot_token", [P, SLOT_TILES], I32)
        c.pair_expert = sb("pair_expert", [1, PAIRS], I32)
        with ExitStack() as split_weights:
            sb, _, sem = allocator(nc, split_weights)
            c.weights_raw_in = sem("weights_raw_in")
            flat = [sb(f"w1_{s}", [P, E * DC * D], F32R) for s in ("hi", "lo")]
            c.w1_hi_flat, c.w1_lo_flat = flat
            c.w1_hi, c.w1_lo = (w[:, :].rearrange("p (e k h) -> p e k h", e=E, k=DC) for w in flat)
            flat = [sb(f"w2_{s}", [P, E * D], F32R) for s in ("hi", "lo")]
            c.w2_hi_flat, c.w2_lo_flat = flat
            c.w2_hi, c.w2_lo = (w[:, :].rearrange("p (e d) -> p e d", e=E) for w in flat)
            with ExitStack() as raw_weights:
                sb, _, _ = allocator(nc, raw_weights)
                c.w1_raw, c.w2_raw = sb("w1_raw", [P, E, DC, 2 * HID]), sb("w2_raw", [P, E, D])
                gate(nc, c)
                if upto >= 3:
                    route(nc, c)
            if upto >= 4:
                experts(nc, c)
        if upto >= 5:
            combine(nc, c)


_INS = ["x", "xT", "ctxT", "g_xattn", "g_ffn", "WqT", "WkT", "Wv", "Wout", "bout", "WgT", "W1", "W2", "Ws1", "Ws2"]


def kernel(**inputs):
    import numpy as np
    import concourse.bacc as bacc
    from concourse.bass_utils import run_bass_kernel_spmd

    def lay(name):
        return np.asarray(inputs[name])

    x = lay("x").reshape(T, D)
    laid = {
        "x": x,
        "xT": x.T,
        "ctxT": lay("ctx_768").reshape(B * CK, CD).T,
        "g_xattn": lay("g_xattn").reshape(1, 1),
        "g_ffn": lay("g_ffn").reshape(1, 1),
        "WqT": lay("L0_xattn_Wq").T,
        "WkT": lay("L0_xattn_Wk").T,
        "Wv": lay("L0_xattn_Wv"),
        "Wout": lay("L0_xattn_Wout"),
        "bout": lay("L0_xattn_bout").reshape(1, D),
        "WgT": lay("L0_ffn_Wg").T,
        "W1": lay("L0_ffn_W1"),
        "W2": lay("L0_ffn_W2"),
        "Ws1": lay("L0_ffn_Ws1"),
        "Ws2": lay("L0_ffn_Ws2"),
    }
    nc = bacc.Bacc("TRN2", target_bir_lowering=False, num_devices=1)
    arrays, args = {}, []
    for name in _INS:
        arrays[f"in_{name}"] = a = np.ascontiguousarray(laid[name])
        args.append(nc.dram_tensor(f"in_{name}", a.shape, mybir.dt.from_np(a.dtype), kind="ExternalInput").ap())
    out = nc.dram_tensor("out", (T, D), F32, kind="ExternalOutput").ap()
    flamingo(nc, *args, out)
    got = run_bass_kernel_spmd(nc, [arrays], core_ids=[0])
    return got.results[0]["out"].reshape(B, N, D)
```

```python
from contextlib import ExitStack
from itertools import islice

import concourse.bass as bass
from concourse import mybir

ALU = mybir.AluOpType
ACT = mybir.ActivationFunctionType
AX = mybir.AxisListType
F32 = mybir.dt.float32
F32R = mybir.dt.float32r
BF16 = mybir.dt.bfloat16
I32 = mybir.dt.int32

P = 128
B, N, D = 32, 256, 256
CK, CD = 77, 192
H, DH = 8, 64
INNER = H * DH
E, HID = 16, 128
HS = 2 * HID
T = B * N
TILES = T // P
DC = D // P
GB = 4
GROUPS = B // GB
GK = GB * CK
HK = H * CK
HALF = HK // 2
PAIRS = TILES + E
SLOT_TILES = 2 * PAIRS
LN_EPS = 1e-5
SCALE = DH ** -0.5
MPAR = DC * GB * HK
KP = 96


def wait(eng, sem, value):
    if not isinstance(value, int) or value > 0:
        eng.wait_ge(sem, value)


def f32(ap):
    return ap.bitcast(F32)


def products(nc, out, pairs, start=True, stop=True):
    last = None
    for n, (lh, ll, rh, rl) in enumerate(pairs):
        nc.tensor.matmul(out, lh, rh, start=start and n == 0, stop=False)
        nc.tensor.matmul(out, lh, rl, start=False, stop=False)
        last = nc.tensor.matmul(out, ll, rh, start=False, stop=stop and n == len(pairs) - 1)
    return last


class Common:
    pass


def allocator(nc, ctx):
    def sb(name, shape, dt=F32):
        return ctx.enter_context(nc.sbuf_tensor(name, shape, dt))

    def ps(name, shape):
        return ctx.enter_context(nc.psum_tensor(name, shape, F32))

    def sem(name):
        return ctx.enter_context(nc.semaphore(name))

    return sb, ps, sem


def rstd_steps(nc, v, stats, mean, rstd, var, chain, root_ready, root_done):
    step = [0]

    def link(ins):
        step[0] += 1
        ins.then_inc(chain, 1)
        v.wait_ge(chain, step[0])

    me, mo = stats[:, :, 1], stats[:, :, 4]
    link(nc.vector.tensor_tensor(mean, me, mo, ALU.add))
    link(nc.vector.tensor_scalar(mean, mean, 0.5, None, ALU.mult))
    link(nc.vector.tensor_tensor(rstd, mean, me, ALU.subtract))
    link(nc.vector.tensor_tensor(rstd, rstd, rstd, ALU.mult))
    link(nc.vector.scalar_tensor_tensor(rstd, stats[:, :, 2], 1.0 / D, rstd, ALU.mult, ALU.add))
    link(nc.vector.scalar_tensor_tensor(rstd, stats[:, :, 5], 1.0 / D, rstd, ALU.mult, ALU.add))
    link(nc.vector.tensor_scalar(rstd, rstd, LN_EPS, None, ALU.add))
    nc.vector.tensor_copy(var, rstd).then_inc(root_ready, 1)
    v.wait_ge(root_done, 1)
    link(nc.vector.reciprocal(rstd, rstd))
    link(nc.vector.tensor_tensor(var, var, rstd, ALU.mult))
    link(nc.vector.tensor_tensor(var, var, rstd, ALU.mult))
    link(nc.vector.tensor_scalar(var, var, -0.5, 1.5, ALU.mult, ALU.add))
    link(nc.vector.tensor_tensor(rstd, rstd, var, ALU.mult))


def attention_tensors(nc, c, ctx):
    a = Common()
    sb, ps, sem = allocator(nc, ctx)
    a.ctx_raw = sb("ctx_raw", [P, 2, GK])
    a.ctxM = [sb(f"ctxM_{s}", [P, 2, GK], F32R) for s in ("hi", "lo")]
    a.kT = [sb(f"kT_{s}", [P, GK], F32R) for s in ("hi", "lo")]
    a.ctxb_raw = [sb(f"ctxb_raw{i}", [P, 2, CK]) for i in range(2)]
    a.ctxb = [[sb(f"ctxb{i}_{s}", [P, 2, CK], F32R) for s in ("hi", "lo")] for i in range(2)]
    a.xT_raw = [sb(f"xT_raw{i}", [P, DC, N]) for i in range(2)]
    a.xT = [[sb(f"xT{i}_{s}", [P, DC, N], F32R) for s in ("hi", "lo")] for i in range(2)]
    a.x_tok = [sb(f"x_tok{i}", [P, 2, D]) for i in range(2)]
    a.M = [sb(f"M_{s}", [P, 2 * MPAR], F32R) for s in ("hi", "lo")]
    a.PT = [sb(f"PT_{s}", [KP, H, N], F32R) for s in ("hi", "lo")]
    a.V = [sb(f"V_{s}", [KP, 4, 4, DH], F32R) for s in ("hi", "lo")]
    a.ps_proj = [ps(f"ps_proj{i}", [P, 512]) for i in range(2)]
    a.ctx_in = sem("ctx_in")
    a.ctxb_in = [sem(f"ctxb_in{i}") for i in range(2)]
    a.xT_in = [sem(f"xT_in{i}") for i in range(2)]
    a.x_in = [sem(f"x_in{i}") for i in range(2)]
    a.ctx_hi, a.ctx_split = sem("ctx_hi"), sem("ctx_split")
    a.x_hi, a.x_split, a.cb_split = sem("x_hi"), sem("x_split"), sem("cb_split")
    a.K_done, a.K_hi, a.K_lo = sem("K_done"), sem("K_hi"), sem("K_lo")
    a.M_done, a.M_hi, a.M_lo = sem("M_done"), sem("M_hi"), sem("M_lo")
    return a


def load_group(sp, c, a, g):
    sp.dma_start(a.ctx_raw[:, 0, :], c.ctxT[0:P, bass.ds(g * GK, GK)]).then_inc(a.ctx_in, 16)
    sp.dma_start(a.ctx_raw[0:CD - P, 1, :], c.ctxT[P:CD, bass.ds(g * GK, GK)]).then_inc(a.ctx_in, 16)


def load_x_side(sp, c, a, b, par):
    sp.dma_start(a.xT_raw[par][:, :, :],
                 c.xT[:, bass.ds(b * N, N)].rearrange("(c p) n -> p c n", p=P)).then_inc(a.xT_in[par], 16)
    sp.dma_start(a.ctxb_raw[par][:, 0, :], c.ctxT[0:P, bass.ds(b * CK, CK)]).then_inc(a.ctxb_in[par], 16)
    sp.dma_start(a.ctxb_raw[par][0:CD - P, 1, :], c.ctxT[P:CD, bass.ds(b * CK, CK)]).then_inc(a.ctxb_in[par], 16)


def load_x(sp, c, a, b, par):
    sp.dma_start(a.x_tok[par][:, :, :], c.x[bass.ds(b * N, N), :].rearrange("(i p) d -> p i d", p=P)
                 ).then_inc(a.x_in[par], 16)


def high(nc, out, source, done):
    nc.scalar.activation(out, source, ACT.Copy).then_inc(done, 1)


def low(nc, lo, hi, source, done):
    nc.vector.tensor_tensor(lo, source, f32(hi), ALU.subtract).then_inc(done, 1)


def high_group(nc, act, a, g):
    act.wait_ge(a.ctx_in, 32 * (g + 1))
    wait(act, a.K_done, 4 * g)
    high(nc, a.ctxM[0][:, 0, :], a.ctx_raw[:, 0, :], a.ctx_hi)
    high(nc, a.ctxM[0][0:CD - P, 1, :], a.ctx_raw[0:CD - P, 1, :], a.ctx_hi)


def split_group(nc, pool, a, g):
    pool.wait_ge(a.ctx_hi, 2 * g + 2)
    nc.gpsimd.tensor_tensor(a.ctxM[1][:, 0, :], a.ctx_raw[:, 0, :], f32(a.ctxM[0][:, 0, :]), ALU.subtract)
    nc.gpsimd.tensor_tensor(a.ctxM[1][0:CD - P, 1, :], a.ctx_raw[0:CD - P, 1, :],
                            f32(a.ctxM[0][0:CD - P, 1, :]), ALU.subtract).then_inc(a.ctx_split, 1)


def high_batch(nc, act, a, b_half, par):
    act.wait_ge(a.xT_in[par], 16 * (b_half + 1))
    high(nc, a.xT[par][0][:, :, :], a.xT_raw[par][:, :, :], a.x_hi)
    act.wait_ge(a.ctxb_in[par], 32 * (b_half + 1))
    high(nc, a.ctxb[par][0][:, 0, :], a.ctxb_raw[par][:, 0, :], a.x_hi)
    high(nc, a.ctxb[par][0][0:CD - P, 1, :], a.ctxb_raw[par][0:CD - P, 1, :], a.x_hi)


def split_batch(nc, pool, a, b, par):
    pool.wait_ge(a.x_hi, 3 * b + 3)
    nc.gpsimd.tensor_tensor(a.xT[par][1][:, :, :], a.xT_raw[par][:, :, :], f32(a.xT[par][0][:, :, :]),
                            ALU.subtract).then_inc(a.x_split, 1)
    nc.gpsimd.tensor_tensor(a.ctxb[par][1][:, 0, :], a.ctxb_raw[par][:, 0, :],
                            f32(a.ctxb[par][0][:, 0, :]), ALU.subtract)
    nc.gpsimd.tensor_tensor(a.ctxb[par][1][0:CD - P, 1, :], a.ctxb_raw[par][0:CD - P, 1, :],
                            f32(a.ctxb[par][0][0:CD - P, 1, :]), ALU.subtract).then_inc(a.cb_split, 1)



def make_K(nc, pe, c, a, n, pair):
    wait(pe, a.M_lo, 4 * n)
    products(nc, a.ps_proj[1][:, 0:GK], [
        (c.wk_hi[:, k, pair * P:(pair + 1) * P], c.wk_lo[:, k, pair * P:(pair + 1) * P],
         a.ctxM[0][:, k, :], a.ctxM[1][:, k, :]) for k in range(2)]).then_inc(a.K_done, 1)


def make_M(nc, pe, c, a, n, pair, k):
    pe.wait_ge(a.K_lo, n + 1)
    wait(pe, a.M_lo, 4 * n + k - 1)
    h, cc = 2 * pair + k // 2, k % 2
    products(nc, a.ps_proj[cc][:, 0:GK], [
        (c.wq_hi[:, h, cc * P:(cc + 1) * P], c.wq_lo[:, h, cc * P:(cc + 1) * P],
         a.kT[0][:, :], a.kT[1][:, :])]).then_inc(a.M_done, 1)


def high_K(nc, act, a, n):
    act.wait_ge(a.K_done, n + 1)
    wait(act, a.M_done, 4 * n)
    high(nc, a.kT[0][:, :], a.ps_proj[1][:, 0:GK], a.K_hi)


def low_K(nc, v, a, n):
    v.wait_ge(a.K_hi, n + 1)
    low(nc, a.kT[1][:, :], a.kT[0][:, :], a.ps_proj[1][:, 0:GK], a.K_lo)


def M_out(a, s, parity, cc, h):
    region = a.M[s][:, bass.ds(parity * MPAR + cc * GB * HK, GB * HK)]
    return region.rearrange("p (b x) -> p b x", b=GB)[:, :, h * CK:(h + 1) * CK]


def M_bank(a, cc):
    return a.ps_proj[cc][:, 0:GK].rearrange("p (b k) -> p b k", b=GB)


def high_M(nc, act, a, n, parity, pair, k):
    act.wait_ge(a.M_done, 4 * n + k + 1)
    high(nc, M_out(a, 0, parity, k % 2, 2 * pair + k // 2), M_bank(a, k % 2), a.M_hi)


def low_M(nc, v, a, n, parity, pair, k):
    v.wait_ge(a.M_hi, 4 * n + k + 1)
    h, cc = 2 * pair + k // 2, k % 2
    low(nc, M_out(a, 1, parity, cc, h), M_out(a, 0, parity, cc, h), M_bank(a, cc), a.M_lo)


def prepare(nc, c, a):
    XB = 3
    with ExitStack() as ctx:
        sb, _, sem = allocator(nc, ctx)
        wq_raw = sb("wq_raw", [P, 4, D])
        wk_raw, wv_raw = (sb(name, [P, 2, INNER]) for name in ("wk_raw", "wv_raw"))
        wo_raw = sb("wo_raw", [P, 4, D])
        xs = [sb(f"xs{i}", [P, 4, D]) for i in range(XB)]
        qmean = sb("qmean", [P, 4])
        stats = sb("stats1", [P, TILES, 6])
        mean1 = sb("mean1", [P, TILES])
        var1 = sb("var1", [P, TILES])
        gates = sb("gates", [P, 2])

        wq_in, wk_in, wvo_in, gates_in = sem("wq_in"), sem("wk_in"), sem("wvo_in"), sem("gates_in")
        x_in = [sem(f"pre_x_in{i}") for i in range(XB)]
        stats_done, chain1 = sem("stats_done"), sem("chain1")
        root_ready, root_done = sem("root_ready1"), sem("root_done1")
        qmean_done, qmean_scaled, centred = sem("qmean_done"), sem("qmean_scaled"), sem("centred")
        wk_hi_done, wk_lo_done, wq_hi_done, wq_lo_done = (
            sem("wk_hi_done"), sem("wk_lo_done"), sem("wq_hi_done"), sem("wq_lo_done"))
        tanh_done, wo_scaled = sem("tanh_done"), sem("wo_scaled")
        zeroed, w_hi, ident_done = sem("zeroed"), sem("w_hi"), sem("ident_done")

        def head_rows(w, j):
            return w[j * DH:(j + 1) * DH, :].rearrange("p (q j) d -> p q j d", j=2)[:, :, j, :]

        with nc.Block() as block:

            @block.sync
            def _(sp):
                for k, (lo, rows) in enumerate(((0, P), (P, CD - P))):
                    sp.dma_start(wk_raw[0:rows, k, :], c.Wk[lo:lo + rows, :]).then_inc(wk_in, 16)
                load_group(sp, c, a, 0)
                sp.dma_start(wq_raw[:, :, :], c.WqT.rearrange("(q p) d -> p q d", p=P)).then_inc(wq_in, 16)
                sp.dma_start(gates[:, 0:1], c.g_xattn.broadcast_to((P, 1))).then_inc(gates_in, 16)
                sp.dma_start(gates[:, 1:2], c.g_ffn.broadcast_to((P, 1))).then_inc(gates_in, 16)
                sp.dma_start(c.bias[:, :], c.bout.broadcast_to((P, D))).then_inc(gates_in, 16)
                for n in range(TILES // 4):
                    if n >= XB:
                        sp.wait_ge(stats_done, 4 * (n - XB + 1))
                    sp.dma_start(xs[n % XB][:, :, :], c.x[n * 512:(n + 1) * 512, :].rearrange("(i p) d -> p i d", p=P)
                                 ).then_inc(x_in[n % XB], 16)
                    if n == 1:
                        sp.dma_start(wv_raw[:, 0, :], c.Wv[0:P, :]).then_inc(wvo_in, 16)
                        sp.dma_start(wv_raw[0:CD - P, 1, :], c.Wv[P:CD, :]).then_inc(wvo_in, 16)
                        sp.dma_start(wo_raw[:, :, :], c.Wout.rearrange("(q p) n -> p q n", p=P)).then_inc(wvo_in, 16)
                    if n == XB:
                        sp.wait_ge(a.ctx_split, 1)
                        load_group(sp, c, a, 1)
                        load_x_side(sp, c, a, 0, 0)
                        load_x_side(sp, c, a, 1, 1)
                        load_x(sp, c, a, 0, 0)

            @block.gpsimd
            def _(pool):
                for w in (c.wk_hi, c.wk_lo, *a.ctxM):
                    nc.gpsimd.memset(f32(w[:, 1, :]), 0.0).then_inc(zeroed, 1)
                for w in (c.wq_hi, c.wq_lo):
                    nc.gpsimd.memset(f32(w[:, :, :]), 0.0).then_inc(zeroed, 1)
                pool.wait_ge(wk_hi_done, 2)
                nc.gpsimd.tensor_tensor(c.wk_lo[:, 0, :], wk_raw[:, 0, :], f32(c.wk_hi[:, 0, :]),
                                        ALU.subtract).then_inc(wk_lo_done, 1)
                nc.gpsimd.tensor_tensor(c.wk_lo[0:CD - P, 1, :], wk_raw[0:CD - P, 1, :],
                                        f32(c.wk_hi[0:CD - P, 1, :]), ALU.subtract).then_inc(wk_lo_done, 1)
                split_group(nc, pool, a, 0)
                for w in (*a.ctxb[0], *a.ctxb[1], c.wv_hi, c.wv_lo):
                    nc.gpsimd.memset(f32(w[:, 1, :]), 0.0).then_inc(zeroed, 1)
                nc.gpsimd.memset(c.ident[:, :], 0.0).then_inc(ident_done, 1)
                pool.wait_ge(ident_done, 1)
                nc.gpsimd.affine_select(out=c.ident[:, :], in_=c.ident[:, :], compare_op=ALU.not_equal, fill=1.0,
                                        base=0, pattern=[[-1, P]], channel_multiplier=1).then_inc(ident_done, 1)
                for w in (*a.PT, *a.V):
                    nc.gpsimd.memset(f32(w[:]), 0.0).then_inc(zeroed, 1)
                pool.wait_ge(w_hi, 2)
                nc.gpsimd.tensor_tensor(c.wv_lo[:, 0, :], wv_raw[:, 0, :], f32(c.wv_hi[:, 0, :]),
                                        ALU.subtract)
                nc.gpsimd.tensor_tensor(c.wv_lo[0:CD - P, 1, :], wv_raw[0:CD - P, 1, :],
                                        f32(c.wv_hi[0:CD - P, 1, :]), ALU.subtract)
                pool.wait_ge(w_hi, 3)
                nc.gpsimd.tensor_tensor(c.wo_lo[:, :, :], wo_raw[:, :, :], f32(c.wo_hi[:, :, :]),
                                        ALU.subtract)
                split_group(nc, pool, a, 1)
                split_batch(nc, pool, a, 0, 0)

            @block.tensor
            def _(pe):
                pe.wait_ge(wk_lo_done, 2)
                pe.wait_ge(a.ctx_split, 1)
                for n in range(4):
                    make_K(nc, pe, c, a, n, n)
                    pe.wait_ge(wq_lo_done, 2)
                    for k in range(4):
                        make_M(nc, pe, c, a, n, n, k)
                pe.wait_ge(a.ctx_split, 2)
                make_K(nc, pe, c, a, 4, 0)

            @block.scalar
            def _(act):
                act.wait_ge(zeroed, 4)
                act.wait_ge(wk_in, 32)
                high(nc, c.wk_hi[:, 0, :], wk_raw[:, 0, :], wk_hi_done)
                high(nc, c.wk_hi[0:CD - P, 1, :], wk_raw[0:CD - P, 1, :], wk_hi_done)
                high_group(nc, act, a, 0)
                act.wait_ge(zeroed, 6)
                act.wait_ge(centred, 4)
                for j in range(2):
                    high(nc, head_rows(c.wq_hi, j), wq_raw[j * DH:(j + 1) * DH, :, :], wq_hi_done)
                act.wait_ge(gates_in, 48)
                nc.scalar.activation(c.tanh_g[:, :], gates[:, :], ACT.Tanh).then_inc(tanh_done, 1)
                act.wait_ge(zeroed, 12)
                for n in range(4):
                    high_K(nc, act, a, n)
                    for k in range(4):
                        high_M(nc, act, a, n, 0, n, k)
                    if n == 0:
                        act.wait_ge(wvo_in, 48)
                        high(nc, c.wv_hi[:, 0, :], wv_raw[:, 0, :], w_hi)
                        high(nc, c.wv_hi[0:CD - P, 1, :], wv_raw[0:CD - P, 1, :], w_hi)
                    if n == 1:
                        act.wait_ge(wo_scaled, 1)
                        high(nc, c.wo_hi[:, :, :], wo_raw[:, :, :], w_hi)
                high_group(nc, act, a, 1)
                high_batch(nc, act, a, 0, 0)
                high_K(nc, act, a, 4)
                act.wait_ge(root_ready, 1)
                nc.scalar.activation(c.rstd1[:, :], c.rstd1[:, :], ACT.Sqrt).then_inc(root_done, 1)

            @block.vector
            def _(v):
                v.wait_ge(wq_in, 16)
                nc.vector.tensor_reduce(qmean[:, :], wq_raw[:, :, :], AX.X, ALU.add).then_inc(qmean_done, 1)
                v.wait_ge(qmean_done, 1)
                nc.vector.tensor_scalar(qmean[:, :], qmean[:, :], 1.0 / D, None, ALU.mult).then_inc(qmean_scaled, 1)
                v.wait_ge(qmean_scaled, 1)
                for q in range(4):
                    nc.vector.tensor_scalar(wq_raw[:, q, :], wq_raw[:, q, :], qmean[:, q:q + 1], SCALE,
                                            ALU.subtract, ALU.mult).then_inc(centred, 1)
                for j in range(2):
                    v.wait_ge(wq_hi_done, j + 1)
                    low(nc, head_rows(c.wq_lo, j), head_rows(c.wq_hi, j), wq_raw[j * DH:(j + 1) * DH, :, :], wq_lo_done)

                def tile_stats(tiles):
                    for t in tiles:
                        n = t // 4
                        v.wait_ge(x_in[n % XB], 16 * (n // XB + 1))
                        nc.vector.bn_stats(stats[:, t, :], xs[n % XB][:, t % 4, :]).then_inc(stats_done, 1)

                t = iter(range(TILES))
                for n in range(4):
                    tile_stats(islice(t, 3))
                    low_K(nc, v, a, n)
                    tile_stats(islice(t, 3))
                    for k in range(4):
                        low_M(nc, v, a, n, 0, n, k)
                        tile_stats(islice(t, 2 if k < 3 else 0))
                    if n == 0:
                        v.wait_ge(tanh_done, 1)
                        nc.vector.tensor_scalar(c.bias[:, :], c.bias[:, :], c.tanh_g[:, 0:1], None, ALU.mult)
                        v.wait_ge(wvo_in, 48)
                        nc.vector.tensor_scalar(wo_raw[:, :, :], wo_raw[:, :, :], c.tanh_g[:, 0:1], None,
                                                ALU.mult).then_inc(wo_scaled, 1)
                tile_stats(t)
                low_K(nc, v, a, 4)
                v.wait_ge(stats_done, TILES)
                rstd_steps(nc, v, stats, mean1[:, :], c.rstd1[:, :], var1[:, :], chain1, root_ready, root_done)


def attend(nc, c, a):
    with ExitStack() as ctx:
        sb, ps, sem = allocator(nc, ctx)
        ctxb, xT, x_tok, M, PT, V = a.ctxb, a.xT, a.x_tok, a.M, a.PT, a.V
        x1_tok = [sb(f"x1_tok{i}", [P, 2, D]) for i in range(2)]
        prob = [sb(f"prob{i}", [P, HK]) for i in range(2)]
        row_max = [sb(f"row_max{i}", [P, H]) for i in range(2)]
        row_sum = [sb(f"row_sum{i}", [P, H]) for i in range(2)]
        OT = [sb(f"OT_{s}", [P, 4, N], F32R) for s in ("hi", "lo")]
        ps_proj = a.ps_proj
        ps_s = ps("ps_s", [P, 2, 512])
        ps_pt = [ps(f"ps_pt{i}", [P, 512]) for i in range(2)]
        ps_o = [ps(f"ps_o{i}", [P, 512]) for i in range(2)]

        x1_out = [sem(f"x1_out{i}") for i in range(2)]
        normed, biased = sem("normed"), sem("biased")
        score_done, V_done, PT_done, OT_done, out_done = (
            sem("score_done"), sem("V_done"), sem("PT_done"), sem("OT_done"), sem("out_done"))
        V_hi, PT_hi, OT_hi, exp_done = sem("V_hi"), sem("PT_hi"), sem("OT_hi"), sem("exp_done")
        V_lo, PT_lo, OT_lo = sem("V_lo"), sem("PT_lo"), sem("OT_lo")
        max_done, sub_done, sum_done, inv_done = sem("max_done"), sem("sub_done"), sem("sum_done"), sem("inv_done")
        x1_done, x1_stats = sem("x1_done"), sem("x1_stats")

        def M_at(s, parity, cc, q, lo, size):
            return M[s][:, bass.ds(parity * MPAR + (cc * GB + q) * HK + lo, size)]

        def groups(eng, body):
            body(0, True, False)
            with eng.Fori(1, GROUPS - 2) as g:
                body(g, False, False)
            body(GROUPS - 2, False, False)
            body(GROUPS - 1, False, True)

        def exists(g):
            return not isinstance(g, int) or g < GROUPS

        def makes_K(g, q):
            return exists(g + 1) and (q < GB - 1 or exists(g + 2))

        with nc.Block() as block:

            @block.sync
            def _(sp):
                def store(b, par):
                    sp.wait_ge(x1_done, 2 * b + 2)
                    sp.dma_start(c.x1[bass.ds(b * N, N), :].rearrange("(i p) d -> p i d", p=P),
                                 x1_tok[par][:, :, :]).then_inc(x1_out[par], 16)

                def body(g, first, last):
                    for q in range(GB):
                        b, par, nxt = GB * g + q, q % 2, (q + 1) % 2
                        if q == 0 and exists(g + 2):
                            sp.wait_ge(a.ctx_split, g + 2)
                            load_group(sp, c, a, g + 2)
                        if not (last and q >= GB - 2):
                            sp.wait_ge(a.x_split, b + 1)
                            sp.wait_ge(a.cb_split, b + 1)
                            load_x_side(sp, c, a, b + 2, par)
                        if not (last and q == GB - 1):
                            wait(sp, x1_done, 2 * b)
                            load_x(sp, c, a, b + 1, nxt)
                        if not (first and q == 0):
                            store(b - 1, nxt)

                groups(sp, body)
                store(B - 1, (B - 1) % 2)
                for par in range(2):
                    sp.wait_ge(x1_out[par], 16 * (B // 2))

            @block.gpsimd
            def _(pool):
                def norm(b, i):
                    pool.wait_ge(inv_done, 2 * b + i + 1)
                    pr = prob[i][:, :].rearrange("p (h k) -> p h k", h=H)
                    nc.gpsimd.tensor_tensor(pr, pr, row_sum[i][:, :].unsqueeze(2).broadcast_to((P, H, CK)),
                                            ALU.mult).then_inc(normed, 1)

                def body(g, first, last):
                    for q in range(GB):
                        b, par, nxt = GB * g + q, q % 2, (q + 1) % 2
                        if not (last and q == GB - 1):
                            split_batch(nc, pool, a, b + 1, nxt)
                        norm(b, 0)
                        if q == GB - 1 and exists(g + 2):
                            split_group(nc, pool, a, g + 2)
                        pool.wait_ge(a.x_in[par], 16 * (2 * g + q // 2 + 1))
                        xr = x_tok[par][:, :, :]
                        nc.gpsimd.tensor_tensor(xr, xr, c.bias[:, :].unsqueeze(1).broadcast_to((P, 2, D)),
                                                ALU.add).then_inc(biased, 1)
                        norm(b, 1)

                groups(pool, body)

            @block.tensor
            def _(pe):
                def scores(b, g, q, i):
                    wait(pe, sub_done, 2 * b + i)
                    xs = xT[q % 2]
                    for half in range(2):
                        last = products(nc, ps_s[:, half, 0:HALF], [
                            (xs[0][:, k, i * P:(i + 1) * P], xs[1][:, k, i * P:(i + 1) * P],
                             M_at(0, g % 2, k, q, half * HALF, HALF), M_at(1, g % 2, k, q, half * HALF, HALF))
                            for k in range(DC)])
                    last.then_inc(score_done, 1)

                def attend_values(b):
                    pe.wait_ge(PT_lo, 4 * b + 4)
                    pe.wait_ge(V_lo, b + 1)
                    wait(pe, x1_done, 2 * b)
                    for k in range(2):
                        for pr in range(2):
                            pair = 2 * k + pr
                            last = products(nc, ps_o[k][:, pr * N:(pr + 1) * N], [
                                (V[0][:, pair, 2 * j:2 * j + 2, :].rearrange("p a e -> p (a e)"),
                                 V[1][:, pair, 2 * j:2 * j + 2, :].rearrange("p a e -> p (a e)"),
                                 PT[0][:, 2 * pair + j, :], PT[1][:, 2 * pair + j, :]) for j in range(2)])
                        last.then_inc(OT_done, 1)

                def project_out(b):
                    pe.wait_ge(OT_lo, 2 * b + 2)
                    for i in range(2):
                        products(nc, ps_o[i][:, 0:D], [
                            (OT[0][:, k, i * P:(i + 1) * P], OT[1][:, k, i * P:(i + 1) * P],
                             c.wo_hi[:, k, :], c.wo_lo[:, k, :]) for k in range(4)]).then_inc(out_done, 1)

                def make_V(b, par, m_units):
                    pe.wait_ge(a.cb_split, b + 1)
                    pe.wait_ge(a.M_lo, m_units)
                    products(nc, ps_proj[0][0:CK, :], [
                        (ctxb[par][0][:, k, :], ctxb[par][1][:, k, :], c.wv_hi[:, k, :], c.wv_lo[:, k, :])
                        for k in range(2)]).then_inc(V_done, 1)

                def transpose_probs(b, i):
                    pe.wait_ge(normed, 2 * b + i + 1)
                    for j in range(2):
                        wait(pe, PT_lo, 4 * b + 2 * i + j - 1)
                        for h in range(4):
                            lo = (4 * j + h) * CK
                            last = nc.tensor.transpose(ps_pt[j][0:CK, h * P:(h + 1) * P], prob[i][:, lo:lo + CK],
                                                       c.ident[:, :])
                        last.then_inc(PT_done, 1)

                def make_M_units(b, q, head):
                    for k in (2 * head, 2 * head + 1):
                        make_M(nc, pe, c, a, b + GB, q, k)

                def body(g, first, last):
                    for q in range(GB):
                        b = GB * g + q
                        pe.wait_ge(a.x_split, b + 1)
                        if q == 0:
                            pe.wait_ge(a.M_lo, 2 * H * (g + 1))
                        scores(b, g, q, 0)
                        if not last:
                            wait(pe, V_lo, 0 if first and q == 0 else b)
                            make_M_units(b, q, 0)
                        if not (first and q == 0):
                            attend_values(b - 1)
                        scores(b, g, q, 1)
                        if not last:
                            make_M_units(b, q, 1)
                        transpose_probs(b, 0)
                        if not (first and q == 0):
                            project_out(b - 1)
                        if makes_K(g, q):
                            if q == GB - 1:
                                pe.wait_ge(a.ctx_split, g + 3)
                            make_K(nc, pe, c, a, b + GB + 1, (q + 1) % GB)
                        make_V(b, q % 2, 2 * H * GROUPS if last else 2 * H + 4 * b + 3)
                        transpose_probs(b, 1)

                groups(pe, body)
                attend_values(B - 1)
                project_out(B - 1)

            def V_out(s):
                return V[s][0:CK, :, 0:4:3, :]

            V_bank = ps_proj[0][0:CK, :].rearrange("p (a b e) -> p a b e", a=4, b=2)

            def PT_out(s, i, j):
                return PT[s][0:CK, 4 * j:4 * j + 4, i * P:(i + 1) * P]

            def PT_bank(j):
                return ps_pt[j][0:CK, :].rearrange("p (h n) -> p h n", h=4)

            def OT_out(s, k):
                return OT[s][:, 2 * k:2 * k + 2, :]

            def OT_bank(k):
                return ps_o[k][:, :].rearrange("p (c n) -> p c n", c=2)

            @block.scalar
            def _(act):
                def exponentials(b, i):
                    act.wait_ge(sub_done, 2 * b + i + 1)
                    nc.scalar.activation(prob[i][:, :], prob[i][:, :], ACT.Exp,
                                         scale=c.rstd1[:, bass.ds(2 * b + i, 1)]).then_inc(exp_done, 1)

                def high_OT(b):
                    for k in range(2):
                        act.wait_ge(OT_done, 2 * b + k + 1)
                        high(nc, OT_out(0, k), OT_bank(k), OT_hi)

                def high_M_units(b, g, q, head):
                    for k in (2 * head, 2 * head + 1):
                        high_M(nc, act, a, b + GB, (g + 1) % 2, q, k)

                def high_PT(b, i):
                    for j in range(2):
                        act.wait_ge(PT_done, 4 * b + 2 * i + j + 1)
                        high(nc, PT_out(0, i, j), PT_bank(j), PT_hi)

                def body(g, first, last):
                    for q in range(GB):
                        b = GB * g + q
                        if not (last and q == GB - 1):
                            wait(act, score_done, 2 * b)
                            wait(act, V_done, b)
                            high_batch(nc, act, a, 2 * g + (q + 1) // 2, (q + 1) % 2)
                        if q == GB - 1 and exists(g + 2):
                            high_group(nc, act, a, g + 2)
                        if not last:
                            high_M_units(b, g, q, 0)
                        exponentials(b, 0)
                        if not (first and q == 0):
                            high_OT(b - 1)
                        if not last:
                            high_M_units(b, g, q, 1)
                        exponentials(b, 1)
                        high_PT(b, 0)
                        if makes_K(g, q):
                            high_K(nc, act, a, b + GB + 1)
                        act.wait_ge(V_done, b + 1)
                        high(nc, V_out(0), V_bank, V_hi)
                        high_PT(b, 1)

                groups(act, body)
                high_OT(B - 1)

            @block.vector
            def _(v):
                S = ps_s[:, :, 0:HALF].rearrange("p a (h k) -> p a h k", h=4)

                def subtract_max(b, i):
                    v.wait_ge(score_done, 2 * b + i + 1)
                    mx = row_max[i][:, :].rearrange("p (a h) -> p a h", a=2)
                    nc.vector.tensor_reduce(mx, S, AX.X, ALU.max).then_inc(max_done, 1)
                    v.wait_ge(max_done, 2 * b + i + 1)
                    wait(v, PT_done, 4 * b + 2 * i - 2)
                    nc.vector.tensor_tensor(prob[i][:, :].rearrange("p (a h k) -> p a h k", a=2, h=4), S,
                                            mx.unsqueeze(3).broadcast_to((P, 2, 4, CK)),
                                            ALU.subtract).then_inc(sub_done, 1)

                def sums(b, i):
                    v.wait_ge(exp_done, 2 * b + i + 1)
                    wait(v, normed, 2 * b + i - 1)
                    nc.vector.tensor_reduce(row_sum[i][:, :], prob[i][:, :].rearrange("p (h k) -> p h k", h=H),
                                            AX.X, ALU.add).then_inc(sum_done, 1)
                    v.wait_ge(sum_done, 2 * b + i + 1)
                    nc.vector.reciprocal(row_sum[i][:, :], row_sum[i][:, :]).then_inc(inv_done, 1)

                def low_OT(b, k):
                    v.wait_ge(OT_hi, 2 * b + k + 1)
                    low(nc, OT_out(1, k), OT_out(0, k), OT_bank(k), OT_lo)

                def residual(b, b_half, par):
                    v.wait_ge(biased, b + 1)
                    wait(v, x1_out[par], 16 * b_half)
                    for i in range(2):
                        v.wait_ge(out_done, 2 * b + i + 1)
                        nc.vector.tensor_tensor(x1_tok[par][:, i, :], ps_o[i][:, 0:D], x_tok[par][:, i, :],
                                                ALU.add).then_inc(x1_done, 1)
                        v.wait_ge(x1_done, 2 * b + i + 1)
                        nc.vector.bn_stats(c.stats2[:, bass.ds((2 * b + i) * 6, 6)],
                                           x1_tok[par][:, i, :]).then_inc(x1_stats, 1)

                def low_M_units(b, g, q, head):
                    for k in (2 * head, 2 * head + 1):
                        low_M(nc, v, a, b + GB, (g + 1) % 2, q, k)

                def low_PT(b, i):
                    for j in range(2):
                        v.wait_ge(PT_hi, 4 * b + 2 * i + j + 1)
                        low(nc, PT_out(1, i, j), PT_out(0, i, j), PT_bank(j), PT_lo)

                def body(g, first, last):
                    for q in range(GB):
                        b = GB * g + q
                        subtract_max(b, 0)
                        if not last:
                            low_M_units(b, g, q, 0)
                        sums(b, 0)
                        if not (first and q == 0):
                            low_OT(b - 1, 0)
                            low_OT(b - 1, 1)
                        subtract_max(b, 1)
                        if not last:
                            low_M_units(b, g, q, 1)
                        sums(b, 1)
                        low_PT(b, 0)
                        if not (first and q == 0):
                            residual(b - 1, 2 * g + (q - 1) // 2, (q + 1) % 2)
                        if makes_K(g, q):
                            low_K(nc, v, a, b + GB + 1)
                        v.wait_ge(V_hi, b + 1)
                        low(nc, V_out(1), V_out(0), V_bank, V_lo)
                        low_PT(b, 1)

                groups(v, body)
                low_OT(B - 1, 0)
                low_OT(B - 1, 1)
                residual(B - 1, B // 2 - 1, (B - 1) % 2)
                v.wait_ge(x1_stats, 2 * B)



def gate(nc, c):
    STEPS = TILES // 4
    NB = 4
    with ExitStack() as ctx:
        sb, ps, sem = allocator(nc, ctx)
        mean2, rstd2, shift2 = sb("mean2", [P, TILES]), c.rstd2, c.shift2
        var2 = sb("var2", [P, TILES])
        wg_raw = sb("wg_raw", [P, DC, E])
        wg = [sb(f"wg_{s}", [P, DC, P], F32R) for s in ("hi", "lo")]
        lgT = [sb(f"lgT{i}", [P, 512]) for i in range(2)]
        x1_in = [sb(f"x1_in{i}", [P, 4, D]) for i in range(NB)]
        y = [sb(f"y{i}", [P, 4, D]) for i in range(NB)]
        yT = [[sb(f"yT{i}_{s}", [P, DC, 512], F32R) for s in ("hi", "lo")] for i in range(2)]
        ps_y = [ps(f"ps_y{i}", [P, 512]) for i in range(4)]
        ps_lt = [ps(f"ps_lt{i}", [P, 512]) for i in range(2)]
        ps_l = [ps(f"ps_l{i}", [P, 4, P]) for i in range(2)]

        x1_loaded = [sem(f"x1_loaded{i}") for i in range(NB)]
        y_stored = [sem(f"y_stored{i}") for i in range(NB)]
        wg_in = sem("wg_in")
        chain2, root_ready, root_done, ln_ready = sem("chain2"), sem("root_ready2"), sem("root_done2"), sem("ln_ready")
        wg_zero, wg_hi_done, wg_ready, y_done = sem("wg_zero"), sem("wg_hi_done"), sem("wg_ready"), sem("y_done")
        yT_done, yT_hi, yT_lo = sem("yT_done"), sem("yT_hi"), sem("yT_lo")
        lt_done, lt_copied, l_done, l_copied = sem("lt_done"), sem("lt_copied"), sem("l_done"), sem("l_copied")
        stats = c.stats2[:, :].rearrange("p (t s) -> p t s", s=6)

        def pipeline(eng, step):
            for G in range(NB):
                step(G, G, 0)
            with eng.Fori(1, STEPS // NB - 1) as j:
                for u in range(NB):
                    step(NB * j + u, u, j)
            for G in range(STEPS - NB, STEPS + 2):
                step(G, G % NB, G // NB)

        def exists(G):
            return not isinstance(G, int) or 0 <= G < STEPS

        with nc.Block() as block:

            @block.sync
            def _(sp):
                def rows(dram, G):
                    return dram[bass.ds(G * 512, 512), :].rearrange("(i p) d -> p i d", p=P)

                sp.dma_start(wg_raw[:, :, :], c.WgT.rearrange("(k p) e -> p k e", p=P)).then_inc(wg_in, 16)
                for G in range(NB):
                    sp.dma_start(x1_in[G][:, :, :], rows(c.x1, G)).then_inc(x1_loaded[G], 16)

                def step(G, u, j):
                    if not exists(G):
                        return
                    sp.wait_ge(y_done, 4 * (G + 1))
                    sp.dma_start(rows(c.y, G), y[u][:, :, :]).then_inc(y_stored[u], 16)
                    if exists(G + NB):
                        sp.dma_start(x1_in[u][:, :, :], rows(c.x1, G + NB)).then_inc(x1_loaded[u], 16)

                pipeline(sp, step)
                for b in range(NB):
                    sp.wait_ge(y_stored[b], 16 * (STEPS // NB))

            @block.gpsimd
            def _(pool):
                for w in wg:
                    nc.gpsimd.memset(f32(w[:, :, :]), 0.0).then_inc(wg_zero, 1)

            @block.tensor
            def _(pe):
                pe.wait_ge(wg_ready, 1)

                def step(G, u, j):
                    if exists(G):
                        r = u % 2
                        wait(pe, yT_lo, 2 * (G - 1))
                        pe.wait_ge(y_done, 4 * (G + 1))
                        for k in range(DC):
                            for i in range(4):
                                last = nc.tensor.transpose(ps_y[2 * r + k][:, i * P:(i + 1) * P],
                                                           y[u][:, i, k * P:(k + 1) * P], c.ident[:, :])
                            last.then_inc(yT_done, 1)
                    if exists(G - 2):
                        p = u % 2
                        pe.wait_ge(lt_copied, G - 1)
                        wait(pe, l_copied, G - 3)
                        for i in range(4):
                            last = nc.tensor.transpose(ps_l[p][:, i, :], lgT[p][:, i * P:(i + 1) * P], c.ident[:, :])
                        last.then_inc(l_done, 1)
                    if exists(G - 1):
                        r = (u - 1) % 2
                        pe.wait_ge(yT_lo, 2 * G)
                        wait(pe, lt_copied, G - 2)
                        products(nc, ps_lt[r][:, :], [
                            (wg[0][:, k, :], wg[1][:, k, :], yT[r][0][:, k, :], yT[r][1][:, k, :])
                            for k in range(DC)]).then_inc(lt_done, 1)

                pipeline(pe, step)

            @block.scalar
            def _(act):
                act.wait_ge(root_ready, 1)
                nc.scalar.activation(rstd2[:, :], rstd2[:, :], ACT.Sqrt).then_inc(root_done, 1)
                act.wait_ge(wg_zero, 2)
                act.wait_ge(wg_in, 16)
                nc.scalar.activation(wg[0][:, :, 0:E], wg_raw[:, :, :], ACT.Copy).then_inc(wg_hi_done, 1)

                def step(G, u, j):
                    if exists(G):
                        r = u % 2
                        wait(act, lt_done, G - 1)
                        for k in range(DC):
                            act.wait_ge(yT_done, 2 * G + k + 1)
                            nc.scalar.activation(yT[r][0][:, k, :], ps_y[2 * r + k][:, :], ACT.Copy).then_inc(yT_hi, 1)
                    if exists(G - 1):
                        r = (u - 1) % 2
                        act.wait_ge(lt_done, G)
                        wait(act, l_done, G - 2)
                        nc.scalar.activation(lgT[r][:, :], ps_lt[r][:, :], ACT.Copy).then_inc(lt_copied, 1)

                pipeline(act, step)

            @block.vector
            def _(v):
                rstd_steps(nc, v, stats, mean2[:, :], rstd2[:, :], var2[:, :], chain2, root_ready, root_done)
                nc.vector.scalar_tensor_tensor(shift2[:, :], mean2[:, :], -1.0, rstd2[:, :], ALU.mult,
                                               ALU.mult).then_inc(ln_ready, 1)
                v.wait_ge(wg_hi_done, 1)
                nc.vector.tensor_tensor(wg[1][:, :, 0:E], wg_raw[:, :, :], f32(wg[0][:, :, 0:E]),
                                        ALU.subtract).then_inc(wg_ready, 1)
                v.wait_ge(ln_ready, 1)

                def normalise(G, u, j):
                    b, round_ = u % NB, j + u // NB
                    v.wait_ge(x1_loaded[b], 16 * (round_ + 1))
                    wait(v, y_stored[b], 16 * round_)
                    wait(v, yT_done, 2 * (G - NB + 1))
                    for i in range(4):
                        nc.vector.tensor_scalar(y[b][:, i, :], x1_in[b][:, i, :],
                                                rstd2[:, bass.ds(4 * G + i, 1)], shift2[:, bass.ds(4 * G + i, 1)],
                                                ALU.mult, ALU.add).then_inc(y_done, 1)

                normalise(0, 0, 0)

                def step(G, u, j):
                    if exists(G + 1):
                        normalise(G + 1, u + 1, j)
                    if exists(G):
                        r = u % 2
                        for k in range(DC):
                            v.wait_ge(yT_hi, 2 * G + k + 1)
                            nc.vector.tensor_tensor(yT[r][1][:, k, :], ps_y[2 * r + k][:, :],
                                                    f32(yT[r][0][:, k, :]), ALU.subtract).then_inc(yT_lo, 1)
                    if exists(G - 2):
                        v.wait_ge(l_done, G - 1)
                        nc.vector.tensor_copy(
                            c.logits[:, bass.ds((G - 2) * 4 * E, 4 * E)].rearrange("p (i e) -> p i e", e=E),
                            ps_l[u % 2][:, :, 0:E]).then_inc(l_copied, 1)

                pipeline(v, step)


def route(nc, c):
    W = TILES * E
    with ExitStack() as ctx:
        sb, ps, sem = allocator(nc, ctx)
        WB = 3
        w1_raw = [sb(f"w1_raw{i}", [P, DC, D]) for i in range(WB)]
        w2_raw = [sb(f"w2_raw{i}", [P, D]) for i in range(WB)]
        raw_in = [sem(f"w_raw_in{i}") for i in range(WB)]
        w_hi, w_lo = sem("expert_w_hi"), sem("expert_w_lo")
        ws1_raw, ws2_raw = sb("ws1_raw", [P, DC, 2 * HS]), sb("ws2_raw", [P, 2, D])
        ws_in, ws_scaled, ws_hi = sem("ws_in"), sem("ws_scaled"), sem("ws_hi")
        rank_row = sb("rank_row", [P, E])
        token_no = sb("token_no", [P, TILES])
        iota_lo, iota_hi = sb("iota_lo", [P, P]), sb("iota_hi", [P, SLOT_TILES])
        after, ones = sb("after", [P, P], BF16), sb("ones", [P, P], BF16)
        top = [sb(f"top{k}", [P, TILES]) for k in range(2)]
        first = sb("first", [P, TILES])
        mask = [sb(f"mask{k}", [P, W]) for k in range(2)]
        work, rest = sb("work", [P, W]), sb("rest", [P, W])
        both = sb("both", [P, W], BF16)
        total = sb("total", [P, TILES])
        zeros, one = sb("zeros_t", [P, TILES]), sb("one", [P, 1])
        upto, place = sb("upto", [P, W]), sb("place", [P, W])
        padded_i, padded = sb("padded_i", [P, E], I32), sb("padded", [P, E])
        ends, offsets = sb("ends", [P, E]), sb("offsets", [P, E])
        slot = [sb(f"slot{k}", [P, TILES]) for k in range(2)]
        part_i = sb("part_i", [P, TILES], I32)
        slot_hi = [sb(f"slot_hi{k}", [P, TILES]) for k in range(2)]
        slot_lo = [sb(f"slot_lo{k}", [P, TILES]) for k in range(2)]
        pair_ends = sb("pair_ends", [1, E])
        passed, pair_sum = sb("passed", [1, PAIRS * E]), sb("pair_sum", [1, PAIRS])
        OH = 16
        PIECE = 4
        gap = [mask[m // 2][:, m % 2 * PIECE * P:(m % 2 + 1) * PIECE * P].rearrange("p (t l) -> p t l", t=PIECE)
               for m in range(4)]
        hot_lo = [sb(f"hot_lo{m}", [P, PIECE, P]) for m in range(4)]
        hot_hi = [sb(f"hot_hi{i}", [P, SLOT_TILES]) for i in range(OH)]
        ps_after, ps_count = ps("ps_after", [P, W]), ps("ps_count", [P, W])
        ps_inv = ps("ps_inv", [P, 512])

        consts, chain, gap_ready, exp_done = sem("consts"), sem("chain"), sem("gap_ready"), sem("exp_done_r")
        both_ready, counted = sem("both_ready"), sem("counted")
        hot_hi_ready, hot_used = sem("hot_hi_ready"), sem("hot_used")
        slots_ready, gap_done, abs_done, hot_lo_ready = (
            sem("slots_ready"), sem("gap_done"), sem("abs_done"), sem("hot_lo_ready"))
        one_ready = sem("one_ready")

        def te(t):
            return t[:, :].rearrange("p (t e) -> p t e", e=E)

        def per_tile(t):
            return t[:, :].unsqueeze(2).broadcast_to((P, TILES, E))

        def per_expert(t):
            return t[:, :].unsqueeze(1).broadcast_to((P, TILES, E))

        halves = [slice(0, 512), slice(512, 1024)]
        ROUNDS = 2 * TILES // OH

        def rounds_of(eng, step, n):
            for m in range(n):
                step(0, m)
            with eng.Fori(1, ROUNDS) as j:
                for m in range(n):
                    step(j, m)

        with nc.Block() as block:

            @block.sync
            def _(sp):
                for e in range(E):
                    if e >= WB:
                        sp.wait_ge(w_lo, 2 * (e - WB + 1))
                    sp.dma_start(w1_raw[e % WB][:, :, :],
                                 c.W1[e].rearrange("(k p) h -> p k h", p=P)).then_inc(raw_in[e % WB], 16)
                    sp.dma_start(w2_raw[e % WB][:, :], c.W2[e]).then_inc(raw_in[e % WB], 16)
                sp.dma_start(ws1_raw[:, :, :], c.Ws1.rearrange("(k p) h -> p k h", p=P)).then_inc(ws_in, 16)
                sp.dma_start(ws2_raw[:, :, :], c.Ws2.rearrange("(k p) h -> p k h", p=P)).then_inc(ws_in, 16)

            @block.gpsimd
            def _(pool):
                steps = [0]

                def link(ins):
                    steps[0] += 1
                    ins.then_inc(consts, 1)
                    pool.wait_ge(consts, steps[0])

                g = nc.gpsimd
                exact = dict(allow_small_or_imprecise_dtypes=True)
                link(g.iota(rank_row[:, :], [[-1, E]], base=E, channel_multiplier=0, **exact))
                link(g.iota(token_no[:, :], [[P, TILES]], base=0, channel_multiplier=1, **exact))
                link(g.iota(iota_lo[:, :], [[1, P]], base=0, channel_multiplier=0, **exact))
                link(g.iota(iota_hi[:, :], [[1, SLOT_TILES]], base=0, channel_multiplier=0, **exact))
                link(g.memset(ones[:, :], 1.0))
                g.memset(one[:, :], 1.0).then_inc(one_ready, 1)
                link(g.memset(zeros[:, :], 0.0))
                link(g.memset(after[:, :], 0.0))
                link(g.affine_select(out=after[:, :], in_=after[:, :], compare_op=ALU.is_gt, fill=-1.0, base=0,
                                     pattern=[[1, P]], channel_multiplier=-1))
                for e in range(E):
                    pool.wait_ge(w_hi, 2 * e + 1)
                    g.tensor_tensor(c.w1_lo[:, e, :, :], w1_raw[e % WB][:, :, :], f32(c.w1_hi[:, e, :, :]),
                                    ALU.subtract).then_inc(w_lo, 1)
                    pool.wait_ge(w_hi, 2 * e + 2)
                    g.tensor_tensor(c.w2_lo[:, e, :], w2_raw[e % WB][:, :], f32(c.w2_hi[:, e, :]),
                                    ALU.subtract).then_inc(w_lo, 1)
                pool.wait_ge(slots_ready, 2)

                def gaps(j, m):
                    wait(pool, hot_lo_ready, 4 * (j - 1) + m + 1)
                    digit = slot_lo[m % 2][:, bass.ds(j * (OH // 2) + m // 2 * PIECE, PIECE)]
                    g.tensor_tensor(gap[m], iota_lo[:, :].unsqueeze(1).broadcast_to((P, PIECE, P)),
                                    digit.unsqueeze(2).broadcast_to((P, PIECE, P)),
                                    ALU.subtract).then_inc(gap_done, 1)

                rounds_of(pool, gaps, 4)
                pool.wait_ge(ws_hi, 1)
                g.tensor_tensor(c.ws1[1][:, :, :], ws1_raw[:, :, :], f32(c.ws1[0][:, :, :]), ALU.subtract)
                pool.wait_ge(ws_hi, 2)
                g.tensor_tensor(c.ws2[1][:, :, :], ws2_raw[:, :, :], f32(c.ws2[0][:, :, :]), ALU.subtract)

            @block.scalar
            def _(act):
                for e in range(E):
                    act.wait_ge(raw_in[e % WB], 32 * (e // WB + 1))
                    nc.scalar.activation(c.w1_hi[:, e, :, :], w1_raw[e % WB][:, :, :], ACT.Copy).then_inc(w_hi, 1)
                    nc.scalar.activation(c.w2_hi[:, e, :], w2_raw[e % WB][:, :], ACT.Copy).then_inc(w_hi, 1)
                    if e == E // 2:
                        act.wait_ge(gap_ready, 1)
                        nc.scalar.activation(te(work), te(work), ACT.Exp).then_inc(exp_done, 1)
                        act.wait_ge(gap_ready, 2)
                        nc.scalar.activation(c.weight[1][:, :], c.weight[1][:, :], ACT.Exp).then_inc(exp_done, 1)
                act.wait_ge(ws_in, 32)
                nc.scalar.activation(c.ws1[0][:, :, :], ws1_raw[:, :, :], ACT.Copy).then_inc(ws_hi, 1)
                nc.scalar.activation(ws2_raw[:, :, :], ws2_raw[:, :, :], ACT.Identity,
                                     scale=c.tanh_g[:, 1:2]).then_inc(ws_scaled, 1)
                act.wait_ge(ws_scaled, 1)
                nc.scalar.activation(c.ws2[0][:, :, :], ws2_raw[:, :, :], ACT.Copy).then_inc(ws_hi, 1)
                act.wait_ge(one_ready, 1)

                def absolute(j, m):
                    act.wait_ge(gap_done, 4 * j + m + 1)
                    nc.scalar.activation(gap[m], gap[m], ACT.Abs).then_inc(abs_done, 1)

                def one_hots(j, m):
                    act.wait_ge(abs_done, 4 * j + m)
                    p = m - 1
                    wait(act, hot_used, OH * (j - 1) + 8 * (p // 2) + 8)
                    nc.scalar.activation(hot_lo[p % 4][:, :, :], gap[p % 4], ACT.Relu, bias=one[:, 0:1],
                                         scale=-1.0).then_inc(hot_lo_ready, 1)

                def round_(j):
                    for m in range(4):
                        absolute(j, m)
                        if not isinstance(j, int) or 4 * j + m > 0:
                            one_hots(j, m)

                for j in range(2):
                    round_(j)
                with act.Fori(2, ROUNDS) as j:
                    round_(j)
                one_hots(ROUNDS, 0)

            @block.tensor
            def _(pe):
                pe.wait_ge(consts, 8)
                pe.wait_ge(both_ready, 1)
                for i in range(2):
                    nc.tensor.matmul(ps_count[:, halves[i]], ones[:, :], both[:, halves[i]],
                                     start=True, stop=True).then_inc(counted, 1)
                for i in range(2):
                    nc.tensor.matmul(ps_after[:, halves[i]], after[:, :], both[:, halves[i]],
                                     start=True, stop=True).then_inc(counted, 1)

                def add_tile(j, u, first, last):
                    m = u // 8 * 2 + u % 2
                    pe.wait_ge(hot_lo_ready, 4 * j + m + 1)
                    pe.wait_ge(hot_hi_ready, OH * j + u + 1)
                    nc.tensor.matmul(ps_inv[:, 0:SLOT_TILES], hot_lo[m][:, u % 8 // 2, :], hot_hi[u][:, :],
                                     start=first, stop=last, skip_group_check=True).then_inc(hot_used, 1)

                for u in range(OH):
                    add_tile(0, u, u == 0, False)
                with pe.Fori(1, ROUNDS - 1) as j:
                    for u in range(OH):
                        add_tile(j, u, False, False)
                for u in range(OH):
                    add_tile(ROUNDS - 1, u, False, u == OH - 1)

            @block.vector
            def _(v):
                steps = [0]

                def link(ins):
                    steps[0] += 1
                    ins.then_inc(chain, 1)
                    v.wait_ge(chain, steps[0])

                V = nc.vector
                v.wait_ge(consts, 8)
                logits, source = te(c.logits), te(c.logits)
                for k in range(2):
                    link(V.tensor_reduce(top[k][:, :], source, AX.X, ALU.max))
                    link(V.tensor_tensor(te(mask[k]), source, per_tile(top[k]), ALU.is_equal))
                    link(V.tensor_tensor(te(mask[k]), te(mask[k]), per_expert(rank_row), ALU.mult))
                    link(V.tensor_reduce(first[:, :], te(mask[k]), AX.X, ALU.max))
                    link(V.tensor_tensor(te(mask[k]), te(mask[k]), per_tile(first), ALU.is_equal))
                    if k == 0:
                        link(V.scalar_tensor_tensor(rest[:, :], mask[0][:, :], -3e38, c.logits[:, :],
                                                    ALU.mult, ALU.add))
                        source = te(rest)
                V.tensor_tensor(both[:, :], mask[0][:, :], mask[1][:, :], ALU.add).then_inc(both_ready, 1)
                V.tensor_tensor(te(work), logits, per_tile(top[0]), ALU.subtract).then_inc(gap_ready, 1)
                V.tensor_tensor(c.weight[1][:, :], top[1][:, :], top[0][:, :], ALU.subtract).then_inc(gap_ready, 1)

                v.wait_ge(counted, 2)
                for e in range(E):
                    ins = V.tensor_tensor_scan(te(upto)[:, :, e], te(ps_count)[:, :, e], zeros[:, :], 0.0,
                                               ALU.add, ALU.add)
                link(ins)
                v.wait_ge(exp_done, 2)
                link(V.tensor_reduce(total[:, :], te(work), AX.X, ALU.add))
                link(V.reciprocal(total[:, :], total[:, :]))
                link(V.tensor_scalar(c.weight[0][:, :], total[:, :], c.tanh_g[:, 1:2], None, ALU.mult))
                link(V.tensor_tensor(c.weight[1][:, :], c.weight[1][:, :], c.weight[0][:, :], ALU.mult))

                link(V.tensor_scalar(padded_i[:, :], te(upto)[:, TILES - 1, :], float(2 * P - 1), None, ALU.add))
                link(V.tensor_scalar(padded_i[:, :], padded_i[:, :], 8, 8, ALU.logical_shift_right,
                                     ALU.logical_shift_left))
                link(V.tensor_copy(padded[:, :], padded_i[:, :]))
                link(V.tensor_tensor_scan(ends[:, :], padded[:, :], zeros[:, 0:E], 0.0, ALU.add, ALU.add))
                link(V.tensor_tensor(offsets[:, :], ends[:, :], padded[:, :], ALU.subtract))
                link(V.tensor_tensor(te(place), te(upto), per_expert(offsets), ALU.add))
                v.wait_ge(counted, 4)
                link(V.tensor_tensor(place[:, :], ps_after[:, :], place[:, :], ALU.add))
                for k in range(2):
                    link(V.tensor_tensor(mask[k][:, :], mask[k][:, :], place[:, :], ALU.mult))
                    link(V.tensor_reduce(slot[k][:, :], te(mask[k]), AX.X, ALU.add))
                    link(V.tensor_copy(c.slot_i[k][:, :], slot[k][:, :]))
                    link(V.tensor_scalar(part_i[:, :], c.slot_i[k][:, :], 7, None, ALU.logical_shift_right))
                    link(V.tensor_copy(slot_hi[k][:, :], part_i[:, :]))
                    V.scalar_tensor_tensor(slot_lo[k][:, :], slot_hi[k][:, :], -float(P), slot[k][:, :],
                                           ALU.mult, ALU.add).then_inc(slots_ready, 1)

                link(V.tensor_scalar(pair_ends[:, :], ends[0:1, :], 1.0 / (2 * P), None, ALU.mult))
                by_pair = passed[:, :].rearrange("p (q e) -> p q e", e=E)
                link(V.tensor_tensor(by_pair, iota_hi[0:1, 0:PAIRS].unsqueeze(2).broadcast_to((1, PAIRS, E)),
                                     pair_ends[:, :].unsqueeze(1).broadcast_to((1, PAIRS, E)), ALU.is_ge))
                link(V.tensor_reduce(pair_sum[:, :], by_pair, AX.X, ALU.add))
                link(V.tensor_scalar(c.pair_expert[:, :], pair_sum[:, :], float(E - 1), None, ALU.min))

                def one_hots(j, u):
                    t, k = bass.ds(j * (OH // 2) + u // 2, 1), u % 2
                    wait(v, hot_used, OH * (j - 1) + u + 1)
                    V.tensor_scalar(hot_hi[u][:, :], iota_hi[:, :], slot_hi[k][:, t], token_no[:, t],
                                    ALU.is_equal, ALU.mult).then_inc(hot_hi_ready, 1)

                rounds_of(v, one_hots, OH)

                v.wait_ge(hot_used, 2 * TILES)
                link(V.tensor_copy(c.slot_token[:, :], ps_inv[:, 0:SLOT_TILES]))


def experts(nc, c):
    U = 8
    ROUNDS = PAIRS // U
    NB = 4
    with ExitStack() as ctx:
        sb, ps, sem = allocator(nc, ctx)
        index = [sb(f"index{i}", [P, 2 * NB], I32) for i in range(2)]
        rows = [sb(f"rows{i}", [P, 2, D]) for i in range(NB)]
        yT = [[sb(f"eyT{i}_{s}", [P, DC, 2 * P], F32R) for s in ("hi", "lo")] for i in range(2)]
        silu = [sb(f"silu{i}", [P, 2, HID]) for i in range(2)]
        a = [sb(f"a{i}", [P, 2, HID]) for i in range(2)]
        aT = [[sb(f"aT{i}_{s}", [P, 2, P], F32R) for s in ("hi", "lo")] for i in range(2)]
        z = [sb(f"z{i}", [P, 2, D]) for i in range(NB)]
        ps_y = [ps(f"ps_ey{i}", [P, DC, 2 * P]) for i in range(2)]
        ps_h = [ps(f"ps_h{i}", [P, 2, 2 * HID]) for i in range(2)]
        ps_a = [ps(f"ps_a{i}", [P, 2 * DC, P]) for i in range(2)]
        ps_z = [ps(f"ps_z{i}", [P, 2, D]) for i in range(2)]

        index_ready, go = sem("index_ready"), sem("gather_go")
        gathered = [sem(f"gathered{i}") for i in range(NB)]
        z_stored = [sem(f"z_stored{i}") for i in range(NB)]
        yT_done, yT_hi, yT_lo = sem("eyT_done"), sem("eyT_hi"), sem("eyT_lo")
        h_done, silu_done, a_done = sem("h_done"), sem("silu_done"), sem("a_done")
        aT_done, aT_hi, aT_lo, z_done, z_copied = (
            sem("aT_done"), sem("aT_hi"), sem("aT_lo"), sem("z_done"), sem("z_copied"))

        def pairs_of(eng, step, lag=0):
            for u in range(U):
                step(u, u, 0)
            with eng.Fori(1, ROUNDS) as j:
                for u in range(U):
                    step(U * j + u, u, j)
            for u in range(lag):
                step(PAIRS + u, u, ROUNDS)

        def exists(q):
            return not isinstance(q, int) or 0 <= q < PAIRS

        with nc.Block() as block:

            @block.gpsimd
            def _(pool):
                def step(q, u, j):
                    if u % NB == 0:
                        pool.wait_ge(index_ready, 2 * j + u // NB + 1)
                    wait(pool, yT_done, q - NB + 1)
                    pool.sem_inc(go, 1)
                    for i in range(2):
                        column = 2 * (u % NB) + i
                        pool.indirect_dma_start(rows[u % NB][:, i, :], None, c.y, bass.IndirectOffsetOnAxis(
                            index[u // NB][:, column:column + 1], 0)).then_inc(gathered[u % NB], 16)

                pairs_of(pool, step)

            @block.sync
            def _(sp):
                def step(q, u, j):
                    sp.wait_ge(z_copied, q + 1)
                    sp.dma_start(c.z[bass.ds(q * 2 * P, 2 * P), :].rearrange("(i p) d -> p i d", p=P),
                                 z[u % NB][:, :, :]).then_inc(z_stored[u % NB], 16)

                pairs_of(sp, step)
                for n in range(3):
                    sp.dma_start(c.x1_rows[n][:, :, :], c.x1[n * 512:(n + 1) * 512, :].rearrange("(i p) d -> p i d", p=P)
                                 ).then_inc(c.x1_rows_in[n], 16)
                for i in range(NB):
                    sp.wait_ge(z_stored[i], 16 * (PAIRS // NB))

            @block.tensor
            def _(pe):
                def transpose_rows(q, u, j):
                    pe.wait_ge(gathered[u % NB], 32 * (2 * j + u // NB + 1))
                    for i in range(2):
                        for k in range(DC):
                            last = nc.tensor.transpose(ps_y[u % 2][:, k, i * P:(i + 1) * P],
                                                       rows[u % NB][:, i, k * P:(k + 1) * P], c.ident[:, :])
                    last.then_inc(yT_done, 1)

                def hidden(q, p, w1_at):
                    pe.wait_ge(yT_lo, q + 1)
                    weights = [(c.w1_hi_flat[:, bass.ds(w1_at + k * D, D)], c.w1_lo_flat[:, bass.ds(w1_at + k * D, D)])
                               for k in range(DC)]
                    for i in range(2):
                        token = slice(i * P, (i + 1) * P)
                        last = products(nc, ps_h[p][:, i, :], [
                            (yT[p][0][:, k, token], yT[p][1][:, k, token], *weights[k]) for k in range(DC)])
                    last.then_inc(h_done, 1)

                def transpose_a(q, p):
                    pe.wait_ge(a_done, q + 1)
                    for i in range(2):
                        last = nc.tensor.transpose(ps_a[p][:, i, :], a[p][:, i, :], c.ident[:, :])
                    last.then_inc(aT_done, 1)

                def down(q, p, w2_at):
                    pe.wait_ge(aT_lo, q + 1)
                    weights = c.w2_hi_flat[:, bass.ds(w2_at, D)], c.w2_lo_flat[:, bass.ds(w2_at, D)]
                    for i in range(2):
                        last = products(nc, ps_z[p][:, i, :], [(aT[p][0][:, i, :], aT[p][1][:, i, :], *weights)])
                    last.then_inc(z_done, 1)

                known = {}

                def expert_of(q, u):
                    if u not in known:
                        known[u] = pe.value_load(c.pair_expert[0:1, bass.ds(q, 1)], min_val=0, max_val=E - 1)
                    return known[u]

                def step(s, u, j):
                    if u == 0:
                        known.clear()
                    if exists(s):
                        transpose_rows(s, u, j)
                    if exists(s - 1):
                        hidden(s - 1, (u - 1) % 2, expert_of(s - 1, u - 1) * (DC * D))
                    if exists(s - 2):
                        transpose_a(s - 2, u % 2)
                    if exists(s - 3):
                        down(s - 3, (u - 3) % 2, expert_of(s - 3, u - 3) * D)

                pairs_of(pe, step, lag=3)

            @block.scalar
            def _(act):
                def step(s, u, j):
                    if exists(s):
                        p = u % 2
                        act.wait_ge(yT_done, s + 1)
                        wait(act, h_done, s - 1)
                        nc.scalar.activation(yT[p][0][:, :, :], ps_y[p][:, :, :], ACT.Copy).then_inc(yT_hi, 1)
                    if exists(s - 1):
                        q, p = s - 1, (u - 1) % 2
                        act.wait_ge(h_done, q + 1)
                        wait(act, a_done, q - 1)
                        nc.scalar.activation(silu[p][:, :, :], ps_h[p][:, :, HID:], ACT.Silu).then_inc(silu_done, 1)
                    if exists(s - 2):
                        q, p = s - 2, u % 2
                        act.wait_ge(aT_done, q + 1)
                        wait(act, z_done, q - 1)
                        nc.scalar.activation(aT[p][0][:, :, :], ps_a[p][:, 0:2, :], ACT.Copy).then_inc(aT_hi, 1)

                pairs_of(act, step, lag=2)

            @block.vector
            def _(v):
                def indices(first_tile, half):
                    nc.vector.tensor_copy(index[half][:, :],
                                          c.slot_token[:, bass.ds(first_tile, 2 * NB)]).then_inc(index_ready, 1)

                indices(0, 0)
                indices(2 * NB, 1)

                def step(s, u, j):
                    if exists(s):
                        p = u % 2
                        v.wait_ge(yT_hi, s + 1)
                        nc.vector.tensor_tensor(yT[p][1][:, :, :], ps_y[p][:, :, :], f32(yT[p][0][:, :, :]),
                                                ALU.subtract).then_inc(yT_lo, 1)
                    if exists(s - 1):
                        q, p = s - 1, (u - 1) % 2
                        v.wait_ge(silu_done, q + 1)
                        wait(v, aT_done, q - 1)
                        nc.vector.tensor_tensor(a[p][:, :, :], ps_h[p][:, :, 0:HID], silu[p][:, :, :],
                                                ALU.mult).then_inc(a_done, 1)
                    if exists(s - 2):
                        q, p = s - 2, u % 2
                        v.wait_ge(aT_hi, q + 1)
                        nc.vector.tensor_tensor(aT[p][1][:, :, :], ps_a[p][:, 0:2, :], f32(aT[p][0][:, :, :]),
                                                ALU.subtract).then_inc(aT_lo, 1)
                    if exists(s - 3):
                        p, b = (u - 3) % 2, (u - 3) % NB
                        v.wait_ge(z_done, s - 2)
                        wait(v, z_stored[b], 16 * (2 * j + (u - 3) // NB))
                        nc.vector.tensor_copy(z[b][:, :, :], ps_z[p][:, :, :]).then_inc(z_copied, 1)
                    if u % NB == NB - 1 and exists(s) and not (isinstance(j, int) and j == ROUNDS - 1):
                        v.wait_ge(gathered[NB - 1], 32 * (2 * j + u // NB + 1))
                        indices(2 * (U * (j + 1) + u - (NB - 1)), u // NB)

                for u in range(U):
                    step(u, u, 0)
                with v.Fori(1, ROUNDS - 1) as j:
                    for u in range(U):
                        step(U * j + u, u, j)
                for s in range(U * (ROUNDS - 1), PAIRS + 3):
                    step(s, s % U, s // U)


def combine(nc, c):
    STEPS = TILES // 4
    NX = 4
    with ExitStack() as ctx:
        sb, ps, sem = allocator(nc, ctx)
        ws1, ws2, x1, x1_in = c.ws1, c.ws2, c.x1_rows, c.x1_rows_in
        index = [sb(f"zindex{i}", [P, 2, 4], I32) for i in range(NX)]
        zg = [sb(f"zg{i}", [P, 8, D]) for i in range(NX)]
        y = [sb(f"cy{i}", [P, 4, D]) for i in range(2)]
        o = [sb(f"o{i}", [P, 4, D]) for i in range(2)]
        yT = [[sb(f"cyT{i}_{s}", [P, DC, 512], F32R) for s in ("hi", "lo")] for i in range(2)]
        silu = [sb(f"csilu{i}", [P, 512]) for i in range(2)]
        a = [sb(f"ca{i}", [P, 512]) for i in range(2)]
        aT = [[sb(f"caT{i}_{s}", [P, 2, 512], F32R) for s in ("hi", "lo")] for i in range(2)]
        ps_y = [ps(f"ps_cy{i}", [P, 512]) for i in range(2)]
        ps_g = [ps(f"ps_g{i}", [P, 512]) for i in range(2)]
        ps_u = [ps(f"ps_u{i}", [P, 512]) for i in range(2)]
        ps_o = [ps(f"ps_co{i}", [P, 2, D]) for i in range(2)]

        y_ready = sem("cy_ready")
        gathered = [sem(f"zgathered{i}") for i in range(NX)]
        out_stored = [sem(f"out_stored{i}") for i in range(2)]
        index_ready, go = sem("zindex_ready"), sem("zgather_go")
        yT_done, yT_hi, yT_lo = sem("cyT_done"), sem("cyT_hi"), sem("cyT_lo")
        g_done, u_done, silu_done, a_done = sem("g_done"), sem("u_done"), sem("csilu_done"), sem("ca_done")
        aT_hi, aT_lo, o_done, added, fin1, fin2 = (
            sem("caT_hi"), sem("caT_lo"), sem("co_done"), sem("added"), sem("fin1"), sem("fin2"))

        def pipeline(eng, step):
            for G in range(NX):
                step(G, G, 0)
            with eng.Fori(1, STEPS // NX - 1) as j:
                for u in range(NX):
                    step(NX * j + u, u, j)
            for G in range(STEPS - NX, STEPS + 2):
                step(G, G % NX, G // NX)

        def exists(G):
            return not isinstance(G, int) or 0 <= G < STEPS

        with nc.Block() as block:

            @block.sync
            def _(sp):
                def rows(dram, G):
                    return dram[bass.ds(G * 512, 512), :].rearrange("(i p) d -> p i d", p=P)

                def step(G, u, j):
                    r = u % 2
                    if exists(G - 2):
                        sp.wait_ge(fin2, 4 * (G - 1))
                        sp.dma_start(rows(c.out, G - 2), o[r][:, :, :]).then_inc(out_stored[r], 16)
                    if exists(G + NX - 1):
                        b = (u - 1) % NX
                        wait(sp, added, 2 * G)
                        sp.dma_start(x1[b][:, :, :], rows(c.x1, G + NX - 1)).then_inc(x1_in[b], 16)

                pipeline(sp, step)
                for r in range(2):
                    sp.wait_ge(out_stored[r], 16 * (STEPS // 2))

            @block.gpsimd
            def _(pool):
                def step(G, u, j):
                    if not exists(G):
                        return
                    pool.wait_ge(index_ready, 2 * G + 2)
                    wait(pool, fin2, 4 * (G - NX + 1))
                    pool.sem_inc(go, 1)
                    for i in range(4):
                        for k in range(2):
                            pool.indirect_dma_start(
                                zg[u][:, 2 * i + k, :], None, c.z,
                                bass.IndirectOffsetOnAxis(index[u][:, k, i:i + 1], 0)).then_inc(gathered[u], 16)

                pipeline(pool, step)

            @block.tensor
            def _(pe):
                def transpose_y(G, p):
                    pe.wait_ge(y_ready, G + 1)
                    for k in range(DC):
                        for i in range(4):
                            last = nc.tensor.transpose(ps_y[k][:, i * P:(i + 1) * P], y[p][:, i, k * P:(k + 1) * P],
                                                       c.ident[:, :])
                        last.then_inc(yT_done, 1)

                def hidden(G, r):
                    for n in range(2):
                        wait(pe, a_done, 2 * G + n - 1)
                        for bank, first, done in ((ps_g[n], HS + n * P, g_done), (ps_u[n], n * P, u_done)):
                            products(nc, bank[:, :], [
                                (ws1[0][:, k, first:first + P], ws1[1][:, k, first:first + P],
                                 yT[r][0][:, k, :], yT[r][1][:, k, :]) for k in range(DC)]).then_inc(done, 1)

                def down(G, p):
                    pe.wait_ge(aT_lo, 2 * G + 2)
                    for b in range(2):
                        wait(pe, added, 2 * (G - 1) + b + 1)
                        for i in (2 * b, 2 * b + 1):
                            last = products(nc, ps_o[b][:, i % 2, :], [
                                (aT[p][0][:, n, i * P:(i + 1) * P], aT[p][1][:, n, i * P:(i + 1) * P],
                                 ws2[0][:, n, :], ws2[1][:, n, :]) for n in range(2)])
                        last.then_inc(o_done, 1)

                transpose_y(0, 0)

                def step(G, u, j):
                    r = u % 2
                    if exists(G):
                        pe.wait_ge(yT_lo, 2 * G + 2)
                    if exists(G + 1):
                        transpose_y(G + 1, 1 - r)
                    if exists(G):
                        hidden(G, r)
                    if exists(G - 1):
                        down(G - 1, 1 - r)

                pipeline(pe, step)

            @block.scalar
            def _(act):
                def high_yT(G, p):
                    wait(act, u_done, 2 * (G - 1))
                    for k in range(DC):
                        act.wait_ge(yT_done, 2 * G + k + 1)
                        nc.scalar.activation(yT[p][0][:, k, :], ps_y[k][:, :], ACT.Copy).then_inc(yT_hi, 1)

                def high_aT(G, r, n):
                    act.wait_ge(a_done, 2 * G + n + 1)
                    wait(act, o_done, 2 * (G - 1))
                    nc.scalar.activation(aT[r][0][:, n, :], a[n][:, :], ACT.Copy).then_inc(aT_hi, 1)

                def normalise(G, u, j):
                    act.wait_ge(x1_in[u % NX], 16 * (j + u // NX + 1))
                    wait(act, yT_done, 2 * (G - 1))
                    for i in range(4):
                        last = nc.scalar.activation(y[u % 2][:, i, :], x1[u % NX][:, i, :], ACT.Identity,
                                                    bias=c.shift2[:, bass.ds(4 * G + i, 1)],
                                                    scale=c.rstd2[:, bass.ds(4 * G + i, 1)])
                    last.then_inc(y_ready, 1)

                normalise(0, 0, 0)
                normalise(1, 1, 0)
                high_yT(0, 0)

                def step(G, u, j):
                    r = u % 2
                    if exists(G + 1):
                        high_yT(G + 1, 1 - r)
                    if exists(G):
                        for n in range(2):
                            act.wait_ge(g_done, 2 * G + n + 1)
                            wait(act, a_done, 2 * G + n - 1)
                            nc.scalar.activation(silu[n][:, :], ps_g[n][:, :], ACT.Silu).then_inc(silu_done, 1)
                            if n == 1 and exists(G + 2):
                                normalise(G + 2, u + 2, j)
                            high_aT(G, r, n)

                pipeline(act, step)

            @block.vector
            def _(v):
                V = nc.vector

                def indices(G, u):
                    for k in range(2):
                        V.tensor_copy(index[u][:, k, :],
                                      c.slot_i[k][:, bass.ds(4 * G, 4)]).then_inc(index_ready, 1)

                def low_yT(G, p):
                    for k in range(DC):
                        v.wait_ge(yT_hi, 2 * G + k + 1)
                        V.tensor_tensor(yT[p][1][:, k, :], ps_y[k][:, :], f32(yT[p][0][:, k, :]),
                                        ALU.subtract).then_inc(yT_lo, 1)

                def multiply(G, n):
                    v.wait_ge(silu_done, 2 * G + n + 1)
                    v.wait_ge(u_done, 2 * G + n + 1)
                    wait(v, aT_lo, 2 * G + n - 1)
                    V.tensor_tensor(a[n][:, :], ps_u[n][:, :], silu[n][:, :], ALU.mult).then_inc(a_done, 1)

                def low_aT(G, r, n):
                    v.wait_ge(aT_hi, 2 * G + n + 1)
                    V.tensor_tensor(aT[r][1][:, n, :], a[n][:, :], f32(aT[r][0][:, n, :]),
                                    ALU.subtract).then_inc(aT_lo, 1)

                def add_x1(G, u, j):
                    p, b_x = u % 2, u % NX
                    v.wait_ge(x1_in[b_x], 16 * (j + u // NX + 1))
                    wait(v, out_stored[p], 16 * (2 * j + u // 2))
                    for b in range(2):
                        v.wait_ge(o_done, 2 * G + b + 1)
                        V.tensor_tensor(o[p][:, 2 * b:2 * b + 2, :], ps_o[b][:, :, :], x1[b_x][:, 2 * b:2 * b + 2, :],
                                        ALU.add).then_inc(added, 1)

                def add_routed(G, u, k):
                    r, done = u % 2, (fin1, fin2)[k]
                    for i in range(4):
                        if k:
                            v.wait_ge(fin1, 4 * G + i + 1)
                        V.scalar_tensor_tensor(o[r][:, i, :], zg[u][:, 2 * i + k, :],
                                               c.weight[k][:, bass.ds(4 * G + i, 1)], o[r][:, i, :],
                                               ALU.mult, ALU.add).then_inc(done, 1)

                for G in range(NX):
                    indices(G, G)
                low_yT(0, 0)

                def step(G, u, j):
                    r = u % 2
                    if exists(G + 1):
                        low_yT(G + 1, 1 - r)
                    if exists(G - 2):
                        b = (u - 2) % NX
                        v.wait_ge(gathered[b], 128 * (j + (u - 2) // NX + 1))
                        v.wait_ge(added, 2 * (G - 1))
                        add_routed(G - 2, b, 0)
                        if exists(G + 2):
                            indices(G + 2, b)
                    if exists(G):
                        multiply(G, 0)
                    if exists(G - 2):
                        add_routed(G - 2, (u - 2) % NX, 1)
                    if exists(G):
                        low_aT(G, r, 0)
                        multiply(G, 1)
                    if exists(G - 1):
                        add_x1(G - 1, u - 1, j)
                    if exists(G):
                        low_aT(G, r, 1)

                pipeline(v, step)


def flamingo(nc, x, xT, ctxT, g_xattn, g_ffn, WqT, Wk, Wv, Wout, bout, WgT, W1, W2, Ws1, Ws2, out, upto=9):
    c = Common()
    c.x, c.xT, c.ctxT, c.g_xattn, c.g_ffn = x, xT, ctxT, g_xattn, g_ffn
    c.WqT, c.Wk, c.Wv, c.Wout, c.bout = WqT, Wk, Wv, Wout, bout
    c.WgT, c.W1, c.W2, c.Ws1, c.Ws2, c.out = WgT, W1, W2, Ws1, Ws2, out
    c.x1 = nc.dram_tensor("x1_scratch", (T, D), F32, kind="Internal").ap()
    with ExitStack() as ctx:
        sb, _, _ = allocator(nc, ctx)
        c.ident = sb("ident", [P, P])
        c.tanh_g = sb("tanh_g", [P, 2])
        c.stats2 = sb("stats2", [P, TILES * 6])
        with ExitStack() as attention:
            sb, _, _ = allocator(nc, attention)
            c.rstd1 = sb("rstd1", [P, TILES])
            c.bias = sb("bias", [P, D])
            c.wq_hi, c.wq_lo = (sb(f"wq_{s}", [P, H, D], F32R) for s in ("hi", "lo"))
            c.wk_hi, c.wk_lo = (sb(f"wk_{s}", [P, 2, INNER], F32R) for s in ("hi", "lo"))
            c.wv_hi, c.wv_lo = (sb(f"wv_{s}", [P, 2, INNER], F32R) for s in ("hi", "lo"))
            c.wo_hi, c.wo_lo = (sb(f"wo_{s}", [P, 4, D], F32R) for s in ("hi", "lo"))
            a = attention_tensors(nc, c, attention)
            prepare(nc, c, a)
            if upto >= 1:
                attend(nc, c, a)
        if upto < 2:
            return
        sb, _, sem = allocator(nc, ctx)
        c.y = nc.dram_tensor("y_scratch", (T, D), F32, kind="Internal").ap()
        c.z = nc.dram_tensor("z_scratch", (SLOT_TILES * P, D), F32, kind="Internal").ap()
        c.rstd2, c.shift2 = sb("rstd2", [P, TILES]), sb("shift2", [P, TILES])
        c.logits = sb("logits", [P, TILES * E])
        c.weight = [sb(f"weight{k}", [P, TILES]) for k in range(2)]
        c.slot_i = [sb(f"slot_i{k}", [P, TILES], I32) for k in range(2)]
        c.slot_token = sb("slot_token", [P, SLOT_TILES], I32)
        c.pair_expert = sb("pair_expert", [1, PAIRS], I32)
        c.ws1 = [sb(f"ws1_{s}", [P, DC, 2 * HS], F32R) for s in ("hi", "lo")]
        c.ws2 = [sb(f"ws2_{s}", [P, 2, D], F32R) for s in ("hi", "lo")]
        c.x1_rows = [sb(f"cx{i}", [P, 4, D]) for i in range(4)]
        c.x1_rows_in = [sem(f"cx_in{i}") for i in range(4)]
        with ExitStack() as split_weights:
            sb, _, _ = allocator(nc, split_weights)
            c.w1_hi_flat, c.w1_lo_flat = (sb(f"w1_{s}", [P, E * DC * D], F32R) for s in ("hi", "lo"))
            c.w2_hi_flat, c.w2_lo_flat = (sb(f"w2_{s}", [P, E * D], F32R) for s in ("hi", "lo"))
            c.w1_hi, c.w1_lo = (w[:, :].rearrange("p (e k h) -> p e k h", e=E, k=DC)
                                for w in (c.w1_hi_flat, c.w1_lo_flat))
            c.w2_hi, c.w2_lo = (w[:, :].rearrange("p (e d) -> p e d", e=E) for w in (c.w2_hi_flat, c.w2_lo_flat))
            gate(nc, c)
            if upto >= 3:
                route(nc, c)
            if upto >= 4:
                experts(nc, c)
        if upto >= 5:
            combine(nc, c)


_INS = ["x", "xT", "ctxT", "g_xattn", "g_ffn", "WqT", "Wk", "Wv", "Wout", "bout", "WgT", "W1", "W2", "Ws1", "Ws2"]


def kernel(**inputs):
    import numpy as np
    import concourse.bacc as bacc
    from concourse.bass_utils import run_bass_kernel_spmd

    def lay(name):
        return np.asarray(inputs[name])

    x = lay("x").reshape(T, D)
    laid = {
        "x": x,
        "xT": x.T,
        "ctxT": lay("ctx_768").reshape(B * CK, CD).T,
        "g_xattn": lay("g_xattn").reshape(1, 1),
        "g_ffn": lay("g_ffn").reshape(1, 1),
        "WqT": lay("L0_xattn_Wq").T,
        "Wk": lay("L0_xattn_Wk"),
        "Wv": lay("L0_xattn_Wv"),
        "Wout": lay("L0_xattn_Wout"),
        "bout": lay("L0_xattn_bout").reshape(1, D),
        "WgT": lay("L0_ffn_Wg").T,
        "W1": lay("L0_ffn_W1"),
        "W2": lay("L0_ffn_W2"),
        "Ws1": lay("L0_ffn_Ws1"),
        "Ws2": lay("L0_ffn_Ws2"),
    }
    nc = bacc.Bacc("TRN2", target_bir_lowering=False, num_devices=1)
    arrays, args = {}, []
    for name in _INS:
        arrays[f"in_{name}"] = a = np.ascontiguousarray(laid[name])
        args.append(nc.dram_tensor(f"in_{name}", a.shape, mybir.dt.from_np(a.dtype), kind="ExternalInput").ap())
    out = nc.dram_tensor("out", (T, D), F32, kind="ExternalOutput").ap()
    flamingo(nc, *args, out)
    got = run_bass_kernel_spmd(nc, [arrays], core_ids=[0])
    return got.results[0]["out"].reshape(B, N, D)
```
